# Optimizing a Trainium2 kernel written in Bass

```python
import numpy as np
import jax
import jax.numpy as jnp

def _softmax(x, axis=-1):
    return jax.nn.softmax(x, axis=axis)

def _gelu(x):
    return jax.nn.gelu(x, approximate=True)

def _silu(x):
    return jax.nn.silu(x)

def _sigmoid(x):
    return jax.nn.sigmoid(x)

def _layernorm(x, axis=-1, eps=1e-05):
    m = jnp.mean(x, axis=axis, keepdims=True)
    v = jnp.var(x, axis=axis, keepdims=True)
    return (x - m) / jnp.sqrt(v + eps)

def _scatter_add(tgt, idx, src, axis=0):
    return tgt.at[idx].add(src)

def _segment_sum(src, seg, n):
    return jax.ops.segment_sum(src, seg, n)
kernel_name = 'mk_macaron_d2_jaxref_r4_15f673'

def setup_inputs(seed: int=0):
    np.random.seed(seed)
    _w = jnp.asarray

    def _L0_attn_setup():
        import jax, jax.numpy as jnp
        import numpy as np
        INV_SQRT_M = 1.0 / np.sqrt(256.0).astype(np.float32)

        def _kernel_features(x, random_matrix):
            x_proj = jnp.einsum('bhsd,dm->bhsm', x, random_matrix)
            return (jax.nn.elu(x_proj) + 1.0) * INV_SQRT_M
        key = jax.random.key(seed)
        ks = jax.random.split(key, 7)
        B, S, D, H, M = (4, 1024, 256, 16, 64)
        hd = D // H
        std = 1.0 / np.sqrt(D)
        return {'x': jax.random.normal(ks[0], (B, S, D), jnp.float32), 'Wq': jax.random.normal(ks[1], (D, D), jnp.float32) * std, 'bq': jnp.zeros((D,), jnp.float32), 'Wk': jax.random.normal(ks[2], (D, D), jnp.float32) * std, 'bk': jnp.zeros((D,), jnp.float32), 'Wv': jax.random.normal(ks[3], (D, D), jnp.float32) * std, 'bv': jnp.zeros((D,), jnp.float32), 'Wo': jax.random.normal(ks[4], (D, D), jnp.float32) * std, 'bo': jnp.zeros((D,), jnp.float32), 'random_matrix': jax.random.normal(ks[5], (hd, M), jnp.float32)}
    _L0_attn_in = _L0_attn_setup()

    def _L0_ffn_setup():
        import jax, jax.numpy as jnp
        import numpy as np
        EPS = 1e-05

        def _quantize(W):
            gamma = jnp.mean(jnp.abs(W))
            return jnp.clip(jnp.round(W / (gamma + EPS)), -1.0, 1.0)
        key = jax.random.key(seed)
        k_x, k_w1, k_b1, k_w2, k_b2 = jax.random.split(key, 5)
        n_embd = 256
        d_ff = 4 * n_embd
        B, S = (4, 1024)
        bound1 = 1.0 / np.sqrt(n_embd)
        bound2 = 1.0 / np.sqrt(d_ff)
        x = jax.random.normal(k_x, (B, S, n_embd), dtype=jnp.float32)
        W1 = jax.random.uniform(k_w1, (d_ff, n_embd), jnp.float32, -bound1, bound1)
        b1 = jax.random.uniform(k_b1, (d_ff,), jnp.float32, -bound1, bound1)
        W2 = jax.random.uniform(k_w2, (n_embd, d_ff), jnp.float32, -bound2, bound2)
        b2 = jax.random.uniform(k_b2, (n_embd,), jnp.float32, -bound2, bound2)
        return {'x': x, 'W1': W1, 'b1': b1, 'W2': W2, 'b2': b2}
    _L0_ffn_in = _L0_ffn_setup()

    def _L1_attn_setup():
        import jax, jax.numpy as jnp
        import numpy as np
        import math
        D_MODEL, D_C, D_R, NH = (256, 128, 32, 16)
        HD = D_MODEL // NH
        B, T = (2, 512)

        def _rope_tables(T, d_R):
            inv_freq = 1.0 / 10000.0 ** (jnp.arange(0, d_R, 2, dtype=jnp.float32) / d_R)
            t = jnp.arange(T, dtype=jnp.float32)
            freqs = jnp.outer(t, inv_freq)
            return (jnp.cos(freqs), jnp.sin(freqs))

        def _rotary_apply(x, cos, sin):
            d = x.shape[-1]
            x1, x2 = (x[..., :d // 2], x[..., d // 2:])
            return jnp.concatenate([x1 * cos - x2 * sin, x2 * cos + x1 * sin], axis=-1)
        key = jax.random.key(seed)
        ks = jax.random.split(key, 8)
        s = lambda fan_in: 1.0 / math.sqrt(fan_in)
        return {'x': jax.random.normal(ks[0], (B, T, D_MODEL), jnp.float32), 'W_kv_down': jax.random.normal(ks[1], (D_MODEL, D_C), jnp.float32) * s(D_MODEL), 'W_k_up': jax.random.normal(ks[2], (D_C, D_MODEL), jnp.float32) * s(D_C), 'W_v_up': jax.random.normal(ks[3], (D_C, D_MODEL), jnp.float32) * s(D_C), 'W_q': jax.random.normal(ks[4], (D_MODEL, D_MODEL), jnp.float32) * s(D_MODEL), 'W_q_rope': jax.random.normal(ks[5], (D_MODEL, D_R), jnp.float32) * s(D_MODEL), 'W_k_rope': jax.random.normal(ks[6], (D_C, D_R), jnp.float32) * s(D_C), 'W_o': jax.random.normal(ks[7], (D_MODEL, D_MODEL), jnp.float32) * s(D_MODEL)}
    _L1_attn_in = _L1_attn_setup()

    def _L1_ffn_setup():
        import jax, jax.numpy as jnp
        import numpy as np
        B, S, D = (2, 512, 256)
        H = 16
        HD = D // H
        N_EXP = 16384
        SQRT_N = 64
        SUB = HD // 2
        K = 16
        K_PRE = min(K * 4, SQRT_N)
        LN_EPS = 1e-05
        key = jax.random.key(seed)
        ks = jax.random.split(key, 9)
        inv_d = 1.0 / np.sqrt(D)
        return {'x': jax.random.normal(ks[0], (B, S, D), dtype=jnp.float32), 'Wq': jax.random.normal(ks[1], (D, D), dtype=jnp.float32) * inv_d, 'ln_g': jnp.ones((HD,), dtype=jnp.float32), 'ln_b': jnp.zeros((HD,), dtype=jnp.float32), 'c_keys': jax.random.normal(ks[2], (SQRT_N, SUB), dtype=jnp.float32) * 0.1, 'c_prime_keys': jax.random.normal(ks[3], (SQRT_N, SUB), dtype=jnp.float32) * 0.1, 'w_down': jax.random.normal(ks[4], (N_EXP, HD), dtype=jnp.float32), 'w_up': jax.random.normal(ks[5], (N_EXP, HD), dtype=jnp.float32), 'Wout': jax.random.normal(ks[6], (D, D), dtype=jnp.float32) * inv_d}
    _L1_ffn_in = _L1_ffn_setup()
    _d = {'L0_attn_x': _L0_attn_in['x'], 'L0_attn_Wq': _L0_attn_in['Wq'], 'L0_attn_bq': _L0_attn_in['bq'], 'L0_attn_Wk': _L0_attn_in['Wk'], 'L0_attn_bk': _L0_attn_in['bk'], 'L0_attn_Wv': _L0_attn_in['Wv'], 'L0_attn_bv': _L0_attn_in['bv'], 'L0_attn_Wo': _L0_attn_in['Wo'], 'L0_attn_bo': _L0_attn_in['bo'], 'L0_attn_random_matrix': _L0_attn_in['random_matrix'], 'L0_ffn_W1': _L0_ffn_in['W1'], 'L0_ffn_b1': _L0_ffn_in['b1'], 'L0_ffn_W2': _L0_ffn_in['W2'], 'L0_ffn_b2': _L0_ffn_in['b2'], 'L1_attn_W_kv_down': _L1_attn_in['W_kv_down'], 'L1_attn_W_k_up': _L1_attn_in['W_k_up'], 'L1_attn_W_v_up': _L1_attn_in['W_v_up'], 'L1_attn_W_q': _L1_attn_in['W_q'], 'L1_attn_W_q_rope': _L1_attn_in['W_q_rope'], 'L1_attn_W_k_rope': _L1_attn_in['W_k_rope'], 'L1_attn_W_o': _L1_attn_in['W_o'], 'L1_ffn_Wq': _L1_ffn_in['Wq'], 'L1_ffn_ln_g': _L1_ffn_in['ln_g'], 'L1_ffn_ln_b': _L1_ffn_in['ln_b'], 'L1_ffn_c_keys': _L1_ffn_in['c_keys'], 'L1_ffn_c_prime_keys': _L1_ffn_in['c_prime_keys'], 'L1_ffn_w_down': _L1_ffn_in['w_down'], 'L1_ffn_w_up': _L1_ffn_in['w_up'], 'L1_ffn_Wout': _L1_ffn_in['Wout']}
    _x0 = _d['L0_attn_x']
    _d['L0_attn_x'] = jax.random.normal(jax.random.fold_in(jax.random.key(seed), 1), (2, 2048, 256), dtype=_x0.dtype)
    del _x0
    return _d

def reference(L0_attn_x, L0_attn_Wq, L0_attn_bq, L0_attn_Wk, L0_attn_bk, L0_attn_Wv, L0_attn_bv, L0_attn_Wo, L0_attn_bo, L0_attn_random_matrix, L0_ffn_W1, L0_ffn_b1, L0_ffn_W2, L0_ffn_b2, L1_attn_W_kv_down, L1_attn_W_k_up, L1_attn_W_v_up, L1_attn_W_q, L1_attn_W_q_rope, L1_attn_W_k_rope, L1_attn_W_o, L1_ffn_Wq, L1_ffn_ln_g, L1_ffn_ln_b, L1_ffn_c_keys, L1_ffn_c_prime_keys, L1_ffn_w_down, L1_ffn_w_up, L1_ffn_Wout):

    def _L0_attn_ref(x, Wq, bq, Wk, bk, Wv, bv, Wo, bo, random_matrix):
        import jax, jax.numpy as jnp
        import numpy as np
        INV_SQRT_M = 1.0 / np.sqrt(256.0).astype(np.float32)

        def _kernel_features(x, random_matrix):
            x_proj = jnp.einsum('bhsd,dm->bhsm', x, random_matrix)
            return (jax.nn.elu(x_proj) + 1.0) * INV_SQRT_M
        B, S, D = x.shape
        hd, M = random_matrix.shape
        H = D // hd
        q = (x @ Wq + bq).reshape(B, S, H, hd).transpose(0, 2, 1, 3)
        k = (x @ Wk + bk).reshape(B, S, H, hd).transpose(0, 2, 1, 3)
        v = (x @ Wv + bv).reshape(B, S, H, hd).transpose(0, 2, 1, 3)
        q_prime = _kernel_features(q, random_matrix)
        k_prime = _kernel_features(k, random_matrix)
        kv = jnp.einsum('bhsm,bhsd->bhmd', k_prime, v)
        k_sum = k_prime.sum(axis=2)
        out = jnp.einsum('bhsm,bhmd->bhsd', q_prime, kv)
        normalizer = jnp.einsum('bhsm,bhm->bhs', q_prime, k_sum)[..., None]
        normalizer = jnp.maximum(normalizer, 1e-06)
        out = out / normalizer
        out = out.transpose(0, 2, 1, 3).reshape(B, S, D)
        return out @ Wo + bo

    def _L0_ffn_ref(x, W1, b1, W2, b2):
        import jax, jax.numpy as jnp
        import numpy as np
        EPS = 1e-05

        def _quantize(W):
            gamma = jnp.mean(jnp.abs(W))
            return jnp.clip(jnp.round(W / (gamma + EPS)), -1.0, 1.0)
        Wq1 = _quantize(W1)
        Wq2 = _quantize(W2)
        h = jax.nn.relu(jnp.einsum('bsd,fd->bsf', x, Wq1) + b1)
        out = jnp.einsum('bsf,df->bsd', h, Wq2) + b2
        return out

    def _L1_attn_ref(x, W_kv_down, W_k_up, W_v_up, W_q, W_q_rope, W_k_rope, W_o):
        import jax, jax.numpy as jnp
        import numpy as np
        import math
        D_MODEL, D_C, D_R, NH = (256, 128, 32, 16)
        HD = D_MODEL // NH
        B, T = (2, 512)

        def _rope_tables(T, d_R):
            inv_freq = 1.0 / 10000.0 ** (jnp.arange(0, d_R, 2, dtype=jnp.float32) / d_R)
            t = jnp.arange(T, dtype=jnp.float32)
            freqs = jnp.outer(t, inv_freq)
            return (jnp.cos(freqs), jnp.sin(freqs))

        def _rotary_apply(x, cos, sin):
            d = x.shape[-1]
            x1, x2 = (x[..., :d // 2], x[..., d // 2:])
            return jnp.concatenate([x1 * cos - x2 * sin, x2 * cos + x1 * sin], axis=-1)
        Bb, Tt, _ = x.shape
        cos, sin = _rope_tables(Tt, D_R)
        cos = cos[None]
        sin = sin[None]
        c_kv = x @ W_kv_down
        k_rope = _rotary_apply(c_kv @ W_k_rope, cos, sin)
        k = (c_kv @ W_k_up).reshape(Bb, Tt, NH, HD)
        v = (c_kv @ W_v_up).reshape(Bb, Tt, NH, HD)
        q = (x @ W_q).reshape(Bb, Tt, NH, HD)
        q_rope = _rotary_apply(x @ W_q_rope, cos, sin)
        scale = math.sqrt(HD + D_R)
        scores = jnp.einsum('bqhd,bkhd->bhqk', q, k)
        scores = scores + jnp.einsum('bqr,bkr->bqk', q_rope, k_rope)[:, None]
        scores = scores / scale
        causal = jnp.triu(jnp.ones((Tt, Tt), dtype=bool), k=1)
        scores = jnp.where(causal[None, None], -jnp.inf, scores)
        w = jax.nn.softmax(scores, axis=-1)
        attn = jnp.einsum('bhqk,bkhd->bqhd', w, v).reshape(Bb, Tt, D_MODEL)
        return attn @ W_o

    def _L1_ffn_ref(x, Wq, ln_g, ln_b, c_keys, c_prime_keys, w_down, w_up, Wout):
        import jax, jax.numpy as jnp
        import numpy as np
        B, S, D = (2, 512, 256)
        H = 16
        HD = D // H
        N_EXP = 16384
        SQRT_N = 64
        SUB = HD // 2
        K = 16
        K_PRE = min(K * 4, SQRT_N)
        LN_EPS = 1e-05
        b, s, d = x.shape
        q = (x @ Wq).reshape(b, s, H, HD)
        mu = q.mean(axis=-1, keepdims=True)
        var = jnp.mean((q - mu) ** 2, axis=-1, keepdims=True)
        qn = (q - mu) / jnp.sqrt(var + LN_EPS) * ln_g + ln_b
        q1, q2 = (qn[..., :SUB], qn[..., SUB:])
        s1 = q1 @ c_keys.T
        s2 = q2 @ c_prime_keys.T
        top_s1, idx1 = jax.lax.top_k(s1, K_PRE)
        top_s2, idx2 = jax.lax.top_k(s2, K_PRE)
        joint = top_s1[..., :, None] + top_s2[..., None, :]
        joint_flat = joint.reshape(b, s, H, K_PRE * K_PRE)
        final_scores, best = jax.lax.top_k(joint_flat, K)
        row = best // K_PRE
        col = best % K_PRE
        real_row = jnp.take_along_axis(idx1, row, axis=-1)
        real_col = jnp.take_along_axis(idx2, col, axis=-1)
        gidx = real_row * SQRT_N + real_col
        wd = w_down[gidx]
        wu = w_up[gidx]
        x_heads = x.reshape(b, s, H, HD)
        hidden = jax.nn.gelu(jnp.einsum('bshd,bshkd->bshk', x_heads, wd), approximate=False)
        rw = jax.nn.softmax(final_scores, axis=-1)
        hidden = hidden * rw
        out_heads = jnp.einsum('bshk,bshkd->bshd', hidden, wu)
        out = out_heads.reshape(b, s, d) @ Wout
        return out
    x = L0_attn_x
    x = x + 0.5 * _L0_ffn_ref(_layernorm(x, axis=-1), L0_ffn_W1, L0_ffn_b1, L0_ffn_W2, L0_ffn_b2)
    x = x + _L0_attn_ref(_layernorm(x, axis=-1), L0_attn_Wq, L0_attn_bq, L0_attn_Wk, L0_attn_bk, L0_attn_Wv, L0_attn_bv, L0_attn_Wo, L0_attn_bo, L0_attn_random_matrix)
    x = x + 0.5 * _L0_ffn_ref(_layernorm(x, axis=-1), L0_ffn_W1, L0_ffn_b1, L0_ffn_W2, L0_ffn_b2)
    x = x + 0.5 * _L1_ffn_ref(_layernorm(x, axis=-1), L1_ffn_Wq, L1_ffn_ln_g, L1_ffn_ln_b, L1_ffn_c_keys, L1_ffn_c_prime_keys, L1_ffn_w_down, L1_ffn_w_up, L1_ffn_Wout)
    x = x + _L1_attn_ref(_layernorm(x, axis=-1), L1_attn_W_kv_down, L1_attn_W_k_up, L1_attn_W_v_up, L1_attn_W_q, L1_attn_W_q_rope, L1_attn_W_k_rope, L1_attn_W_o)
    x = x + 0.5 * _L1_ffn_ref(_layernorm(x, axis=-1), L1_ffn_Wq, L1_ffn_ln_g, L1_ffn_ln_b, L1_ffn_c_keys, L1_ffn_c_prime_keys, L1_ffn_w_down, L1_ffn_w_up, L1_ffn_Wout)
    return x

_drawn_inputs = setup_inputs


def setup_inputs(seed=0):
    import zlib

    import numpy as np

    out = dict(_drawn_inputs(seed))
    spreads = {'L0_attn_bq': (0.0, 0.8),
     'L0_attn_bk': (0.0, 0.8),
     'L0_attn_bv': (0.0, 0.8),
     'L0_attn_bo': (0.0, 0.8),
     'L1_ffn_ln_g': (1.0, 0.6),
     'L1_ffn_ln_b': (0.0, 0.8)}
    factors = {'L0_attn_Wq': 8.0,
     'L0_attn_Wk': 8.0,
     'L0_attn_Wv': 8.0,
     'L0_attn_Wo': 8.0,
     'L0_attn_random_matrix': 8.0,
     'L0_ffn_b1': 8.0,
     'L0_ffn_b2': 8.0,
     'L1_attn_W_kv_down': 8.0,
     'L1_attn_W_k_up': 8.0,
     'L1_attn_W_v_up': 8.0,
     'L1_attn_W_q': 8.0,
     'L1_attn_W_q_rope': 8.0,
     'L1_attn_W_k_rope': 8.0,
     'L1_attn_W_o': 8.0,
     'L1_ffn_Wq': 8.0,
     'L1_ffn_c_keys': 8.0,
     'L1_ffn_c_prime_keys': 8.0,
     'L1_ffn_w_down': 8.0,
     'L1_ffn_w_up': 8.0,
     'L1_ffn_Wout': 8.0}
    for name, (base, spread) in spreads.items():
        noise = np.random.default_rng([zlib.crc32(name.encode()), seed]).standard_normal(out[name].shape)
        drawn = base * np.exp(spread * noise) if base else spread * noise
        out[name] = jnp.asarray(drawn.astype(out[name].dtype))
    for name, factor in factors.items():
        out[name] = (out[name] * factor).astype(out[name].dtype)
    return out
```

```python
import numpy as np
import concourse.bass as bass
from concourse import mybir
from concourse.alu_op_type import AluOpType as ALU
from contextlib import ExitStack

F32 = mybir.dt.float32
I32 = mybir.dt.int32
U32 = mybir.dt.uint32
ACT = mybir.ActivationFunctionType
AX = mybir.AxisListType

P = 128
SEQS = 2
T = 4096
NT = T // P
ST = NT // SEQS
SL = T // SEQS
BLK = 4
BW = BLK * P
NB = NT // BLK
SB = ST // BLK
D = 256
KC = D // P
FF = 1024
FC = FF // P
EPS = 1e-5
H = 16
HD = D // H
PAIRS = H // 2
HK = P // HD
M0 = 64
VC = HD + 1
DR = 32
DC = 128
SCALE = float(1.0 / np.sqrt(HD + DR))
NK = 64
TOP = 16
GH = 4
NG = H // GH
SEGS = [(0, 1, 16, 0), (1, 1, 8, 16), (2, 1, 5, 24), (3, 1, 4, 29), (4, 1, 3, 33), (5, 3, 2, 36), (8, 8, 1, 42)]
NJ = 50
LOWEST = -3.0e38
GROUPS = [(u % ST + BLK) // BLK for u in range(2 * ST)]
PT_AT = [sum(GROUPS[:u]) for u in range(2 * ST)]
PTN = sum(GROUPS) // 2
STAGES = 6


class Chain:

    def __init__(self, eng, sem):
        self.eng, self.sem, self.n = eng, sem, 0

    def mark(self, ins):
        ins.then_inc(self.sem, 1)
        self.n += 1

    def sync(self):
        self.eng.wait_ge(self.sem, self.n)

    def link(self, ins):
        self.mark(ins)
        self.sync()

    def restart(self):
        self.sync()
        self.eng.sem_clear(self.sem)
        self.n = 0


class Arena:

    def __init__(self, tensor, words):
        self.tensor, self.words, self.at = tensor, words, 0

    def reset(self):
        self.at = 0

    def take(self, *shape, parts=P, dt=F32):
        n = int(np.prod(shape))
        assert self.at + n <= self.words, (self.at, n, self.words)
        v = self.tensor[0:parts, self.at:self.at + n]
        self.at += n
        if dt is not F32:
            v = v.bitcast(dt)
        if len(shape) == 2:
            v = v.rearrange("p (a b) -> p a b", a=shape[0])
        elif len(shape) == 3:
            v = v.rearrange("p (a b c) -> p a b c", a=shape[0], b=shape[1])
        return v


def macaron(nc, ins, out):
    ctx = ExitStack()
    with ctx:
        def sb(name, shape, dt=F32):
            return ctx.enter_context(nc.sbuf_tensor(name, shape, dt))

        def sem(name):
            return ctx.enter_context(nc.semaphore(name))

        def sems(prefix, names):
            return {n: sem(f"{prefix}_{n}") for n in names.split()}

        psum = ctx.enter_context(nc.psum_tensor("psum", [P, 8, 512], F32))
        bank = [psum[:, i, :] for i in range(8)]

        X = sb("X", [P, NT, D])
        ident = sb("ident", [P, P])
        ones = sb("ones", [P, P])
        stats = sb("stats", [P, BLK, 6])
        mv = sb("mv", [P, BLK, 2])
        var = sb("var", [P, BLK])
        rstd = sb("rstd", [P, BLK])
        newton = sb("newton", [P, BLK])
        xn = sb("xn", [P, BLK, D])
        xT = sb("xT", [P, KC, BW])
        WORDS = 35500
        arena = Arena(sb("arena", [P, WORDS]), WORDS)

        w1t = arena.take(KC, FF)
        w2t = arena.take(FC, D)
        b1c = arena.take(FC)
        b2r = arena.take(D, parts=1)
        gsum = arena.take(2)
        thr = arena.take(4)
        wq0, wk0, wv0, wo0 = [arena.take(KC, D) for _ in range(4)]
        bq0, bk0 = arena.take(KC), arena.take(KC)
        bv0, bo0 = arena.take(D, parts=1), arena.take(D, parts=1)
        rm = arena.take(HK * M0)
        kv = arena.take(PAIRS, 2 * VC)
        vext = arena.take(2, H, VC)
        h = arena.take(FC, BW)
        wtmp = h.rearrange("p a b -> p (a b)")
        sT = arena.take(KC, SL)
        kT = arena.take(KC, BW)
        emin = arena.take(2, BW)
        efeat = arena.take(2, BW)
        kf = arena.take(2, PAIRS * P)
        o0 = arena.take(D)
        oT0 = arena.take(KC, P)
        nrm = arena.take(H)
        rnrm = arena.take(H)
        qf = h

        arena.reset()
        wqe = arena.take(KC, D)
        woute = arena.take(KC, D)
        keys = arena.take(HK * 2 * NK)
        lng = arena.take(HD)
        lnb = arena.take(HD)
        iota = arena.take(NJ)
        xne = [arena.take(1, D) for _ in range(2)]
        xTe = arena.take(KC, P)
        qc = arena.take(H, HD)
        qsq = arena.take(H, HD)
        hmean = arena.take(H)
        hvar = arena.take(H)
        hrstd = arena.take(H)
        hnewton = arena.take(H)
        qnT = arena.take(KC, P)
        scores = arena.take(2 * H, NK)
        V = arena.take(2 * H, TOP)
        I = arena.take(2 * H, TOP, dt=U32)
        IF = arena.take(2 * H, TOP)
        J = arena.take(H, NJ)
        GI = arena.take(H, NJ)
        best = arena.take(H, TOP)
        pos = arena.take(H, TOP, dt=U32)
        posf = arena.take(H, TOP)
        gidf = arena.take(H, TOP)
        hot = arena.take(GH, TOP, NJ)
        gidx = [arena.take(H * TOP, dt=U32) for _ in range(2)]
        wexp = arena.take(H, TOP)
        wsum = arena.take(H)
        rw = [arena.take(H, TOP) for _ in range(2)]
        G = arena.take(NG, GH * TOP, 2 * HD)
        prod = arena.take(GH * TOP, HD)
        hid = arena.take(2, GH * TOP)
        gel = arena.take(2, GH * TOP)
        oe = arena.take(H, HD)
        oTe = arena.take(KC, P)

        arena.reset()
        wkvd = arena.take(KC, DC)
        wkup = arena.take(PAIRS, P)
        wqp = arena.take(KC, PAIRS, P)
        wvup = arena.take(D)
        wqr, wqrs = arena.take(KC, DR), arena.take(KC, DR)
        wkr, wkrs = arena.take(DR), arena.take(DR)
        wo1 = arena.take(KC, D)
        cosT = arena.take(SL, parts=DR)
        sinT = arena.take(SL, parts=DR)
        causal = arena.take(P)
        rt = arena.take(4, BW, parts=DR)
        QA = arena.take(SL)
        KA = arena.take(SL)
        cb = arena.take(BW)
        cT = arena.take(SL)
        wpair = arena.take(1 + KC, P)
        otile = arena.take(D)
        vall = arena.take(ST, H, VC)
        probs = arena.take(SL)
        PT = arena.take(SL)
        oall = arena.take(ST, D)
        sT1 = arena.take(KC, SL)
        rmax = arena.take(2, 1)
        nmax = arena.take(2, 1)
        rden = arena.take(2, 1)
        oT1 = arena.take(KC, P)

        loaded = [sem(f"loaded{i}") for i in range(5)]
        const_ready = sem("const_ready")
        dve_chain = sem("dve_chain")
        gsum_ready = sem("gsum_ready")
        gamma_ready = sem("gamma_ready")
        phase_done = sem("phase_done")
        stored = sem("stored")
        passed_dve = sem("passed_dve")
        passed_pool = sem("passed_pool")
        sf = sems("ffn", "xn_ready xT_ps xT_ready h_ps h_ready out_ps")
        sk = sems("lin", "xn_ready xT_ps xT_ready kT_ps kT_ready kf_ps emin_ready e_ready kf_ready kv_ps "
                              "q_ps qT_ready qf_ps qmin_ready qe_ready qf_ready o_ps o_ready oT_ps oT_ready y_ps "
                              "y_added kv_done")
        se = sems("exp", "xn_ready xT_ps xT_ready q_ps qn_ready qnT_ps qnT_ready s_ps s_ready shift_ready "
                              "w_ready idx_ready hid_ready gel_ready slot_free oe_ready oT_ps oT_ready y_ps")
        gathered = [[sem(f"exp{r}_gathered{g}") for g in range(NG)] for r in range(2)]
        sa = sems("att", "xn_ready xT_ps xT_ready c_ps c_ready r_ps r_ready rope_copied v_ps v_ready "
                              "wpair_ready otile_ready kq_ps kq_ready pair_done s_ps m_ready p_ready pt_ps pt_ready o_ps o_read ot_ps "
                              "ot_ready y_ps y_added")

        block = ctx.enter_context(nc.Block())

        L0_LOADS = [
            (X[:], ins["x"].rearrange("(t p) d -> p t d", p=P)), (ident[:], ins["ident"]),
            (w1t, ins["w1t"].rearrange("(k p) f -> p k f", p=P)),
            (w2t, ins["w2t"].rearrange("(k p) f -> p k f", p=P)),
            (b1c, ins["b1"]), (b2r, ins["b2"]),
            (wq0, ins["wq0"].rearrange("(k p) n -> p k n", p=P)), (wk0, ins["wk0"].rearrange("(k p) n -> p k n", p=P)),
            (wv0, ins["wv0"].rearrange("(k p) n -> p k n", p=P)), (wo0, ins["wo0"].rearrange("(k p) n -> p k n", p=P)),
            (bq0, ins["bq0"]), (bk0, ins["bk0"]), (bv0, ins["bv0"]), (bo0, ins["bo0"]), (rm, ins["rm"])]
        EXP_LOADS = [
            (wqe, ins["wqe"].rearrange("(k p) n -> p k n", p=P)),
            (woute, ins["woute"].rearrange("(k p) n -> p k n", p=P)),
            (keys, ins["keys"]), (lng, ins["lng"].partition_broadcast(P)), (lnb, ins["lnb"].partition_broadcast(P)),
            (iota, ins["iota"].partition_broadcast(P))]
        ATT_LOADS = [
            (wkvd, ins["wkvd"].rearrange("(k p) n -> p k n", p=P)), (wkup, ins["wkup"]),
            (wqp, ins["wqp"].rearrange("(k p) a n -> p k a n", p=P)), (wvup, ins["wvup"]),
            (wqr, ins["wqr"].rearrange("(k p) n -> p k n", p=P)), (wqrs, ins["wqrs"].rearrange("(k p) n -> p k n", p=P)),
            (wkr, ins["wkr"]), (wkrs, ins["wkrs"]), (wo1, ins["wo1"].rearrange("(k p) n -> p k n", p=P)),
            (cosT, ins["cos"]), (sinT, ins["sin"]), (causal, ins["causal"])]
        PHASE_LOADS = [L0_LOADS, [], [], EXP_LOADS, ATT_LOADS, EXP_LOADS]

        @block.sync
        def _(sp):
            for ph, loads in enumerate(PHASE_LOADS[:STAGES]):
                if ph and loads:
                    sp.wait_ge(phase_done, ph)
                for dst, src in loads:
                    sp.dma_start(dst, src).then_inc(loaded[[0, 0, 0, 1, 2, 3][ph]], 16)
            sp.wait_ge(phase_done, STAGES)
            sp.dma_start(out.rearrange("(t p) d -> p t d", p=P), X[:]).then_inc(stored, 16)
            sp.wait_ge(stored, 16)

        def begin(eng, ph):
            if ph:
                eng.wait_ge(phase_done, ph)
            if PHASE_LOADS[ph]:
                eng.wait_ge(loaded[[0, 0, 0, 1, 2, 3][ph]], 16 * len(PHASE_LOADS[ph]))

        @block.vector
        def _(dve):
            ch = Chain(dve, dve_chain)
            v = nc.vector

            def end_phase():
                ch.sync()
                dve.sem_inc(phase_done, 1)

            def rsqrt(y, x, c):
                ch.link(v.tensor_scalar(c.bitcast(I32), x.bitcast(I32), 1, None, ALU.logical_shift_right))
                ch.link(v.tensor_scalar(y.bitcast(I32), c.bitcast(I32), -1.0, float(0x5f3759df), ALU.mult, ALU.add))
                for _ in range(4):
                    ch.link(v.scalar_tensor_tensor(out=c, in0=y, scalar=-0.5, in1=x, op0=ALU.mult, op1=ALU.mult))
                    ch.link(v.tensor_tensor(c, c, y, ALU.mult))
                    ch.link(v.scalar_tensor_tensor(out=y, in0=c, scalar=1.5, in1=y, op0=ALU.add, op1=ALU.mult))

            def layernorm(srcs, dst, ready):
                n = len(srcs)
                for t, src in enumerate(srcs):
                    ch.mark(v.bn_stats(stats[:, t, :], src))
                ch.sync()
                for t in range(n):
                    ch.mark(v.bn_aggr(mv[:, t, :], stats[:, t, :]))
                ch.sync()
                ch.link(v.tensor_scalar(var[:, 0:n], mv[:, 0:n, 1], EPS, None, ALU.add))
                rsqrt(rstd[:, 0:n], var[:, 0:n], newton[:, 0:n])
                for t, src in enumerate(srcs):
                    v.tensor_scalar(dst[:, t, :], src, mv[:, t, 0:1], rstd[:, t:t + 1],
                                    ALU.subtract, ALU.mult).then_inc(ready, 1)

            def ternary(w, col, count):
                ch.link(v.scalar_tensor_tensor(out=wtmp[:, 0:count // P], in0=w, scalar=-1.0, in1=w,
                                               op0=ALU.mult, op1=ALU.max))
                v.reduce_sum(gsum[:, col:col + 1], wtmp[:, 0:count // P], AX.X).then_inc(gsum_ready, 1)
                dve.wait_ge(gamma_ready, col + 1)
                tot = bank[0][:, col:col + 1]
                ch.mark(v.tensor_scalar(thr[:, 0:1], tot, 0.5 / count, 0.5 * EPS, ALU.mult, ALU.add))
                ch.mark(v.tensor_scalar(thr[:, 1:2], tot, -0.5 / count, -0.5 * EPS, ALU.mult, ALU.add))
                ch.sync()
                ch.link(v.tensor_scalar(wtmp[:, 0:count // P], w, thr[:, 1:2], None, ALU.is_lt))
                ch.link(v.scalar_tensor_tensor(out=w, in0=w, scalar=thr[:, 0:1], in1=wtmp[:, 0:count // P],
                                               op0=ALU.is_gt, op1=ALU.subtract))

            def ffn(s, r):
                ch.restart()
                with dve.Fori(0, NB) as b:
                    g = b + r * NB
                    layernorm([X[:, b * BLK + t, :] for t in range(BLK)], xn, s["xn_ready"])
                    for t in range(BLK):
                        dve.wait_ge(s["out_ps"], g * BLK + (t // 2 * 2 + 2))
                        xt = X[:, b * BLK + t, :]
                        ps = bank[6 + t // 2][:, (t % 2) * D:(t % 2 + 1) * D]
                        ch.mark(v.scalar_tensor_tensor(out=xt, in0=ps, scalar=0.5, in1=xt, op0=ALU.mult, op1=ALU.add))
                    ch.restart()

            def linear_attention(s):
                ch.restart()
                with dve.Fori(0, SEQS) as q:
                    ch.mark(v.memset(kv, 0.0))
                    ch.mark(v.memset(vext[:, :, :, HD:VC], 1.0))
                    ch.restart()
                    with dve.Fori(0, SB) as b:
                        g = b + q * SB
                        layernorm([X[:, g * BLK + t, :] for t in range(BLK)], xn, s["xn_ready"])
                        for t in range(BLK):
                            dve.wait_ge(s["kf_ps"], g * BLK + (t + 1))
                            for m in range(KC):
                                v.tensor_scalar(emin[:, m, :], bank[4 + m], 0.0, None,
                                                ALU.min).then_inc(s["emin_ready"], 1)
                            dve.wait_ge(s["e_ready"], g * BLK + (t + 1))
                            if t >= 2:
                                dve.wait_ge(s["kv_ps"], g * BLK + (t - 1))
                            for m in range(KC):
                                v.scalar_tensor_tensor(out=kf[:, t % 2, m * BW:(m + 1) * BW], in0=bank[4 + m],
                                                       scalar=0.0, in1=efeat[:, m, :], op0=ALU.max,
                                                       op1=ALU.add).then_inc(s["kf_ready"], 1)
                            v.tensor_copy(vext[:, t % 2, :, 0:HD],
                                          bank[6][:, 0:D].rearrange("p (h d) -> p h d", h=H)).then_inc(s["kf_ready"], 1)
                        dve.wait_ge(s["kv_ps"], g * BLK + BLK)
                        ps = bank[7][:, 0:PAIRS * 2 * VC].rearrange("p (a c) -> p a c", a=PAIRS)
                        for e in range(2):
                            rows, cols = slice(64 * e, 64 * e + 64), slice(VC * e, VC * e + VC)
                            ch.mark(v.scalar_tensor_tensor(out=kv[rows, :, cols], in0=ps[rows, :, cols],
                                                           scalar=1.0 / 256, in1=kv[rows, :, cols],
                                                           op0=ALU.mult, op1=ALU.add))
                        ch.restart()
                    dve.sem_inc(s["kv_done"], 1)
                    with dve.Fori(0, SB) as b:
                        g = b + q * SB
                        for p in range(PAIRS + 1):
                            if p < PAIRS:
                                dve.wait_ge(s["qf_ps"], g * PAIRS + (p + 1))
                                v.tensor_scalar(emin[:, p % 2, :], bank[2 + p % 4], 0.0, None,
                                                ALU.min).then_inc(s["qmin_ready"], 1)
                            if p:
                                dve.wait_ge(s["qe_ready"], g * PAIRS + p)
                                v.scalar_tensor_tensor(out=qf[:, p - 1, :], in0=bank[2 + (p - 1) % 4], scalar=0.0,
                                                       in1=efeat[:, (p - 1) % 2, :], op0=ALU.max,
                                                       op1=ALU.add).then_inc(s["qf_ready"], 1)
                        for t in range(BLK):
                            dve.wait_ge(s["o_ps"], g * BLK + (t + 1))
                            ps = bank[6][:, 0:H * VC].rearrange("p (h c) -> p h c", h=H)
                            ch.link(v.tensor_scalar(nrm, ps[:, :, HD], 1e-6, None, ALU.max))
                            ch.link(v.reciprocal(rnrm, nrm))
                            v.tensor_tensor(o0.rearrange("p (h d) -> p h d", h=H), ps[:, :, 0:HD],
                                            rnrm[:, :, None].to_broadcast([P, H, HD]), ALU.mult).then_inc(s["o_ready"], 1)
                            dve.wait_ge(s["y_ps"], g * BLK + (t + 1))
                            xt = X[:, g * BLK + t, :]
                            ch.link(v.tensor_tensor(xt, bank[7][:, D:2 * D], xt, ALU.add))
                            dve.sem_inc(s["y_added"], 1)
                        ch.restart()
            def expert_choice(s, n, c, buf):
                xt = X[:, n, :]
                layernorm([xt], xne[buf], s["xn_ready"])
                dve.wait_ge(s["q_ps"], (n + c) + 1)
                q = bank[1][:, 0:D].rearrange("p (h d) -> p h d", h=H)
                ch.link(v.reduce_sum(hmean, q, AX.X))
                ch.link(v.tensor_scalar(hmean, hmean, 1.0 / HD, None, ALU.mult))
                ch.link(v.tensor_tensor(qc, q, hmean[:, :, None].to_broadcast([P, H, HD]), ALU.subtract))
                ch.link(v.tensor_tensor(qsq, qc, qc, ALU.mult))
                ch.link(v.reduce_sum(hvar, qsq, AX.X))
                ch.link(v.tensor_scalar(hvar, hvar, 1.0 / HD, EPS, ALU.mult, ALU.add))
                rsqrt(hrstd, hvar, hnewton)
                ch.link(v.tensor_tensor(qc, qc, hrstd[:, :, None].to_broadcast([P, H, HD]), ALU.mult))
                ch.link(v.tensor_tensor(qc, qc, lng[:, None, :].to_broadcast([P, H, HD]), ALU.mult))
                v.tensor_tensor(qc, qc, lnb[:, None, :].to_broadcast([P, H, HD]), ALU.add).then_inc(s["qn_ready"], 1)
                dve.wait_ge(s["s_ready"], (n + c) * 4 + 4)
                dve.sem_inc(passed_dve, 1)
                for r in range(2 * H):
                    ch.mark(v.max(V[:, r, 0:8], scores[:, r, :]))
                ch.sync()
                for r in range(2 * H):
                    ch.mark(v.max_index(I[:, r, 0:8], V[:, r, 0:8], scores[:, r, :]))
                ch.sync()
                for r in range(2 * H):
                    ch.mark(v.match_replace(scores[:, r, :], V[:, r, 0:8], scores[:, r, :], LOWEST))
                ch.sync()
                for r in range(2 * H):
                    ch.mark(v.max(V[:, r, 8:16], scores[:, r, :]))
                ch.sync()
                for r in range(2 * H):
                    ch.mark(v.max_index(I[:, r, 8:16], V[:, r, 8:16], scores[:, r, :]))
                ch.sync()
                ch.link(v.tensor_copy(IF, I))
                v2 = V.rearrange("p (h two) k -> p h two k", two=2)
                i2 = IF.rearrange("p (h two) k -> p h two k", two=2)
                ch.link(v.tensor_scalar(i2[:, :, 0, :], i2[:, :, 0, :], float(NK), None, ALU.mult))
                for val, to in ((v2, J), (i2, GI)):
                    for i0, ni, nj, off in SEGS:
                        a = val[:, :, 0, i0:i0 + ni][:, :, :, None].to_broadcast([P, H, ni, nj])
                        bb = val[:, :, 1, 0:nj][:, :, None, :].to_broadcast([P, H, ni, nj])
                        o = to[:, :, off:off + ni * nj].rearrange("p h (i j) -> p h i j", i=ni)
                        if ni == 1:
                            a, bb, o = a[:, :, 0, :], bb[:, :, 0, :], o[:, :, 0, :]
                        elif nj == 1:
                            a, bb, o = a[:, :, :, 0], bb[:, :, :, 0], o[:, :, :, 0]
                        ch.mark(v.tensor_tensor(o, a, bb, ALU.add))
                ch.sync()
                for hh in range(H):
                    ch.mark(v.max(best[:, hh, 0:8], J[:, hh, :]))
                ch.sync()
                for hh in range(H):
                    ch.mark(v.max_index(pos[:, hh, 0:8], best[:, hh, 0:8], J[:, hh, :]))
                ch.sync()
                for hh in range(H):
                    ch.mark(v.match_replace(J[:, hh, :], best[:, hh, 0:8], J[:, hh, :], LOWEST))
                ch.sync()
                for hh in range(H):
                    ch.mark(v.max(best[:, hh, 8:16], J[:, hh, :]))
                ch.sync()
                for hh in range(H):
                    ch.mark(v.max_index(pos[:, hh, 8:16], best[:, hh, 8:16], J[:, hh, :]))
                v.tensor_tensor(wexp, best, best[:, :, 0:1].to_broadcast([P, H, TOP]),
                                ALU.subtract).then_inc(s["shift_ready"], 1)
                ch.sync()
                ch.link(v.tensor_copy(posf, pos))
                for g in range(NG):
                    hs = slice(g * GH, (g + 1) * GH)
                    ch.link(v.tensor_tensor(hot, posf[:, hs, :][:, :, :, None].to_broadcast([P, GH, TOP, NJ]),
                                            iota[:, None, None, :].to_broadcast([P, GH, TOP, NJ]), ALU.is_equal))
                    ch.link(v.tensor_tensor(hot, hot, GI[:, hs, :][:, :, None, :].to_broadcast([P, GH, TOP, NJ]),
                                            ALU.mult))
                    ch.link(v.reduce_sum(gidf[:, hs, :], hot, AX.X))
                ch.link(v.tensor_copy(gidx[buf], gidf.rearrange("p h k -> p (h k)")))
                dve.sem_inc(s["idx_ready"], 1)
                dve.wait_ge(s["w_ready"], (n + c) + 1)
                ch.link(v.reduce_sum(wsum, wexp, AX.X))
                ch.link(v.reciprocal(wsum, wsum))
                ch.mark(v.tensor_tensor(rw[buf], wexp, wsum[:, :, None].to_broadcast([P, H, TOP]), ALU.mult))
                ch.sync()

            def expert_mix(s, n, c, buf):
                for g in range(NG + 1):
                    if g < NG:
                        dve.wait_ge(gathered[c // NT][g], n * (16 * GH * TOP) + 16 * GH * TOP)
                        if g == 1:
                            dve.wait_ge(s["hid_ready"], (n + c) * NG + 1)
                        for hh in range(GH):
                            col = (g * GH + hh) * HD
                            xh = xne[buf][:, 0, col:col + HD][:, None, :].to_broadcast([P, TOP, HD])
                            ch.mark(v.tensor_tensor(prod[:, hh * TOP:(hh + 1) * TOP, :],
                                                    G[:, g, hh * TOP:(hh + 1) * TOP, 0:HD], xh, ALU.mult))
                        ch.sync()
                        v.reduce_sum(hid[:, g % 2, :], prod, AX.X).then_inc(s["hid_ready"], 1)
                    if g:
                        k = g - 1
                        dve.wait_ge(s["gel_ready"], (n + c) * NG + g)
                        hs = slice(k * GH, (k + 1) * GH)
                        ch.link(v.tensor_tensor(gel[:, k % 2, :], gel[:, k % 2, :],
                                                rw[buf][:, hs, :].rearrange("p h k -> p (h k)"), ALU.mult))
                        if g < NG:
                            dve.wait_ge(s["hid_ready"], (n + c) * NG + (g + 1))
                        ch.link(v.tensor_tensor(prod, G[:, k, :, HD:2 * HD],
                                                gel[:, k % 2, :][:, :, None].to_broadcast([P, GH * TOP, HD]), ALU.mult))
                        dve.sem_inc(s["slot_free"], 1)
                        ch.link(v.reduce_sum(oe[:, hs, :], prod.rearrange("p (h k) d -> p h d k", h=GH), AX.X))
                dve.sem_inc(s["oe_ready"], 1)
                dve.wait_ge(s["y_ps"], (n + c) + 1)
                xt = X[:, n, :]
                ch.link(v.scalar_tensor_tensor(out=xt, in0=bank[7][:, 0:D], scalar=0.5, in1=xt,
                                               op0=ALU.mult, op1=ALU.add))

            def experts(s, c):
                expert_choice(s, 0, c, 0)
                ch.restart()
                with dve.Fori(0, NT - 2, 2) as n:
                    for e in range(2):
                        expert_choice(s, n + (e + 1), c, 1 - e)
                        expert_mix(s, n + e, c, e)
                    ch.restart()
                expert_choice(s, NT - 1, c, 1)
                expert_mix(s, NT - 2, c, 0)
                expert_mix(s, NT - 1, c, 1)

            def attention(s):
                ch.restart()
                with dve.Fori(0, SEQS) as q:
                    ch.mark(v.memset(vall[:, :, :, HD:VC], 1.0))
                    ch.restart()
                    with dve.Fori(0, SB) as b:
                        g = b + q * SB
                        layernorm([X[:, g * BLK + t, :] for t in range(BLK)], xn, s["xn_ready"])
                        cols = bass.ds(b * BW, BW)
                        for i, to in enumerate((KA, QA)):
                            dve.wait_ge(s["r_ps"], g * 2 + (i + 1))
                            ch.mark(v.tensor_tensor(rt[:, 2 * i, :], bank[3 + 2 * i][0:DR, :], cosT[:, cols], ALU.mult))
                            ch.mark(v.tensor_tensor(rt[:, 2 * i + 1, :], bank[4 + 2 * i][0:DR, :], sinT[:, cols], ALU.mult))
                            ch.sync()
                            v.tensor_tensor(to[0:DR, cols], rt[:, 2 * i, :], rt[:, 2 * i + 1, :],
                                            ALU.add).then_inc(s["r_ready"], 1)
                        for t in range(BLK):
                            dve.wait_ge(s["v_ps"], g * 2 + (t // 2 + 1))
                            ps = bank[t // 2][:, (t % 2) * D:(t % 2 + 1) * D].rearrange("p (h d) -> p h d", h=H)
                            v.tensor_copy(vall[:, b * BLK + t, :, 0:HD], ps).then_inc(s["v_ready"], 1)
                        ch.restart()
                    with dve.Fori(0, PAIRS) as p:
                        pq = p + q * PAIRS
                        v.tensor_copy(wpair[:, 0, :], wkup[:, p, :]).then_inc(s["wpair_ready"], 1)
                        for k in range(KC):
                            v.tensor_copy(wpair[:, 1 + k, :], wqp[:, k, p, :]).then_inc(s["wpair_ready"], 1)
                        for i in range(8):
                            dve.wait_ge(s["kq_ps"], pq * 8 + (i + 1))
                            to, j = (KA, i) if i < 4 else (QA, i - 4)
                            for e in range(2):
                                r0 = 64 * e + DR
                                v.tensor_copy(to[r0:r0 + HD, j * BW:(j + 1) * BW],
                                              bank[i][r0:r0 + HD, :]).then_inc(s["kq_ready"], 1)
                        for e in range(2):
                            for qt in range(ST):
                                u, w = e * ST + qt, (qt + 1) * P
                                dve.wait_ge(s["s_ps"], pq * (2 * ST) + (u + 1))
                                S = psum[:, 0:4, :].rearrange("p a b -> p (a b)")
                                ch.link(v.tensor_tensor(S[:, qt * P:w], S[:, qt * P:w], causal, ALU.add))
                                ch.link(v.reduce_max(rmax[:, u % 2, :], S[:, 0:w], AX.X))
                                v.tensor_scalar(nmax[:, u % 2, :], rmax[:, u % 2, :], -SCALE, None,
                                                ALU.mult).then_inc(s["m_ready"], 1)
                                if u:
                                    finish(s, p, pq, u - 1)
                        finish(s, p, pq, 2 * ST - 1)
                        ch.restart()
                    dve.sem_inc(s["pair_done"], 1)
                    with dve.Fori(0, ST) as t:
                        v.tensor_copy(otile, oall[:, t, :]).then_inc(s["otile_ready"], 1)
                        dve.wait_ge(s["y_ps"], q * ST + (t + 1))
                        xt = X[:, q * ST + t, :]
                        ch.link(v.tensor_tensor(xt, bank[7][:, 0:D], xt, ALU.add))
                        dve.sem_inc(s["y_added"], 1)
                        ch.restart()

            def finish(s, p, pq, u):
                e, qt = u // ST, u % ST
                dve.wait_ge(s["o_ps"], pq * (2 * ST) + (u + 1))
                ps = bank[6 + u % 2]
                ch.link(v.reciprocal(rden[:, u % 2, :], ps[:, HD:VC]))
                v.tensor_scalar(oall[:, qt, bass.ds(p * (2 * HD) + e * HD, HD)], ps[:, 0:HD], rden[:, u % 2, :], None,
                                ALU.mult).then_inc(s["o_read"], 1)

            v.memset(ones[:], 1.0).then_inc(const_ready, 1)
            begin(dve, 0)
            ternary(w1t.rearrange("p k f -> p (k f)"), 0, D * FF)
            ternary(w2t.rearrange("p k f -> p (k f)"), 1, D * FF)
            dve.sem_inc(const_ready, 1)
            ffn(sf, 0)
            end_phase()
            if STAGES > 1:
                linear_attention(sk)
                end_phase()
            if STAGES > 2:
                ffn(sf, 1)
                end_phase()
            if STAGES > 3:
                begin(dve, 3)
                experts(se, 0 * NT)
                end_phase()
            if STAGES > 4:
                begin(dve, 4)
                attention(sa)
                end_phase()
            if STAGES > 5:
                begin(dve, 5)
                experts(se, 1 * NT)
                end_phase()

        @block.scalar
        def _(act):
            a = nc.scalar

            def ffn(s, r):
                with act.Fori(0, NB) as b:
                    g = b + r * NB
                    act.wait_ge(s["xT_ps"], g + 1)
                    for k in range(KC):
                        a.copy(xT[:, k, :], bank[k]).then_inc(s["xT_ready"], 1)
                    for m in range(FC):
                        act.wait_ge(s["h_ps"], g * FC + (m + 1))
                        a.activation(h[:, m, :], bank[2 + m % 4], ACT.Relu,
                                     bias=b1c[:, m:m + 1]).then_inc(s["h_ready"], 1)

            def linear_attention(s):
                with act.Fori(0, SEQS) as q:
                    with act.Fori(0, SB) as b:
                        g = b + q * SB
                        act.wait_ge(s["xT_ps"], g + 1)
                        for k in range(KC):
                            a.copy(xT[:, k, :], bank[k]).then_inc(s["xT_ready"], 1)
                            a.copy(sT[:, k, bass.ds(b * BW, BW)], bank[k]).then_inc(s["xT_ready"], 1)
                        for m in range(KC):
                            act.wait_ge(s["kT_ps"], g * KC + (m + 1))
                            a.activation(kT[:, m, :], bank[2 + m], ACT.Identity,
                                         bias=bk0[:, m:m + 1]).then_inc(s["kT_ready"], 1)
                        for t in range(BLK):
                            act.wait_ge(s["emin_ready"], g * (2 * BLK) + 2 * (t + 1))
                            a.activation(efeat, emin, ACT.Exp).then_inc(s["e_ready"], 1)
                    with act.Fori(0, SB) as b:
                        g = b + q * SB
                        for m in range(KC):
                            act.wait_ge(s["q_ps"], g * KC + (m + 1))
                            a.activation(kT[:, m, :], bank[m], ACT.Identity,
                                         bias=bq0[:, m:m + 1]).then_inc(s["qT_ready"], 1)
                        for p in range(PAIRS):
                            act.wait_ge(s["qmin_ready"], g * PAIRS + (p + 1))
                            a.activation(efeat[:, p % 2, :], emin[:, p % 2, :], ACT.Exp).then_inc(s["qe_ready"], 1)
                        for t in range(BLK):
                            act.wait_ge(s["oT_ps"], g * BLK + (t + 1))
                            a.copy(oT0, bank[7][:, 0:D].rearrange("p (k t) -> p k t", k=KC)).then_inc(s["oT_ready"], 1)
            def expert_choice(s, n, c):
                act.wait_ge(s["xT_ps"], (n + c) + 1)
                a.copy(xTe, bank[0][:, 0:D].rearrange("p (k t) -> p k t", k=KC)).then_inc(s["xT_ready"], 1)
                act.wait_ge(s["qnT_ps"], (n + c) + 1)
                a.copy(qnT, bank[0][:, 0:D].rearrange("p (k t) -> p k t", k=KC)).then_inc(s["qnT_ready"], 1)
                flat = scores.rearrange("p r n -> p (r n)")
                for j in range(4):
                    act.wait_ge(s["s_ps"], (n + c) * 4 + (j + 1))
                    a.copy(flat[:, j * BW:(j + 1) * BW], bank[2 + j]).then_inc(s["s_ready"], 1)
                act.wait_ge(s["shift_ready"], (n + c) + 1)
                a.activation(wexp, wexp, ACT.Exp).then_inc(s["w_ready"], 1)

            def expert_mix(s, n, c):
                for g in range(NG):
                    act.wait_ge(s["hid_ready"], (n + c) * NG + (g + 1))
                    a.activation(gel[:, g % 2, :], hid[:, g % 2, :], ACT.Gelu).then_inc(s["gel_ready"], 1)
                act.wait_ge(s["oT_ps"], (n + c) + 1)
                a.copy(oTe, bank[6][:, 0:D].rearrange("p (k t) -> p k t", k=KC)).then_inc(s["oT_ready"], 1)

            def experts(s, c):
                expert_choice(s, 0, c)
                with act.Fori(0, NT - 1) as n:
                    expert_choice(s, n + 1, c)
                    expert_mix(s, n, c)
                expert_mix(s, NT - 1, c)

            def attention(s):
                with act.Fori(0, SEQS) as q:
                    with act.Fori(0, SB) as b:
                        g = b + q * SB
                        cols = bass.ds(b * BW, BW)
                        act.wait_ge(s["xT_ps"], g + 1)
                        for k in range(KC):
                            a.copy(sT1[:, k, cols], bank[k]).then_inc(s["xT_ready"], 1)
                        act.wait_ge(s["c_ps"], g + 1)
                        a.copy(cb, bank[2]).then_inc(s["c_ready"], 1)
                        a.copy(cT[:, cols], bank[2]).then_inc(s["c_ready"], 1)
                        act.wait_ge(s["r_ready"], g * 2 + 2)
                        for to in (KA, QA):
                            a.copy(to[64:64 + DR, cols], to[0:DR, cols]).then_inc(s["rope_copied"], 1)
                    with act.Fori(0, PAIRS) as p:
                        pq = p + q * PAIRS
                        for e in range(2):
                            for qt in range(ST):
                                u, w = e * ST + qt, (qt + 1) * P
                                act.wait_ge(s["m_ready"], pq * (2 * ST) + (u + 1))
                                S = psum[:, 0:4, :].rearrange("p a b -> p (a b)")
                                a.activation(probs[:, 0:w], S[:, 0:w], ACT.Exp, bias=nmax[:, u % 2, :],
                                             scale=SCALE).then_inc(s["p_ready"], 1)
                                for g in range((qt + BLK) // BLK):
                                    gw = min(BLK, qt + 1 - g * BLK) * P
                                    act.wait_ge(s["pt_ps"], pq * (2 * PTN) + (PT_AT[u] + g + 1))
                                    a.copy(PT[:, g * BW:g * BW + gw],
                                           bank[4 + (PT_AT[u] + g) % 2][:, 0:gw]).then_inc(s["pt_ready"], 1)
                    with act.Fori(0, ST) as t:
                        act.wait_ge(s["ot_ps"], q * ST + (t + 1))
                        a.copy(oT1, bank[6][:, 0:D].rearrange("p (k t) -> p k t", k=KC)).then_inc(s["ot_ready"], 1)

            begin(act, 0)
            act.wait_ge(const_ready, 2)
            ffn(sf, 0)
            if STAGES > 1:
                begin(act, 1)
                linear_attention(sk)
            if STAGES > 2:
                begin(act, 2)
                ffn(sf, 1)
            if STAGES > 3:
                begin(act, 3)
                experts(se, 0 * NT)
            if STAGES > 4:
                begin(act, 4)
                attention(sa)
            if STAGES > 5:
                begin(act, 5)
                experts(se, 1 * NT)

        @block.tensor
        def _(pe):
            t_ = nc.tensor
            def transpose_block(s, b):
                pe.wait_ge(s["xn_ready"], b * BLK + BLK)
                for k in range(KC):
                    for t in range(BLK):
                        mm = t_.transpose(bank[k][:, t * P:(t + 1) * P], xn[:, t, k * P:(k + 1) * P], ident[:])
                mm.then_inc(s["xT_ps"], 1)

            def project(dst, lhs, rhs):
                for k in range(KC):
                    mm = t_.matmul(dst, lhs(k), rhs(k), start=(k == 0), stop=(k == KC - 1))
                return mm

            def project_bias(dst, lhs, rhs, row):
                for k in range(KC):
                    t_.matmul(dst, lhs(k), rhs(k), start=(k == 0), stop=False)
                return t_.matmul(dst, ones[0:1, :], row, start=False, stop=True)

            def turn(dst, src):
                for k in range(KC):
                    mm = t_.transpose(dst[:, k * P:(k + 1) * P], src[:, k * P:(k + 1) * P], ident[:])
                return mm

            def ffn(s, r):
                with pe.Fori(0, NB) as b:
                    g = b + r * NB
                    transpose_block(s, g)
                    pe.wait_ge(s["xT_ready"], g * KC + KC)
                    for m in range(FC):
                        if m >= 4:
                            pe.wait_ge(s["h_ready"], g * FC + (m - 3))
                        project(bank[2 + m % 4], lambda k: w1t[:, k, m * P:(m + 1) * P],
                                lambda k: xT[:, k, :]).then_inc(s["h_ps"], 1)
                    pe.wait_ge(s["h_ready"], g * FC + FC)
                    for t in range(BLK):
                        ps = bank[6 + t // 2][:, (t % 2) * D:(t % 2 + 1) * D]
                        for m in range(FC):
                            t_.matmul(ps, h[:, m, t * P:(t + 1) * P], w2t[:, m, :], start=(m == 0), stop=False)
                        t_.matmul(ps, ones[0:1, :], b2r, start=False, stop=True).then_inc(s["out_ps"], 1)

            def linear_attention(s):
                with pe.Fori(0, SEQS) as q:
                    with pe.Fori(0, SB) as b:
                        g = b + q * SB
                        transpose_block(s, g)
                        pe.wait_ge(s["xT_ready"], g * (2 * KC) + 2 * KC)
                        for m in range(KC):
                            project(bank[2 + m], lambda k: wk0[:, k, m * P:(m + 1) * P],
                                    lambda k: xT[:, k, :]).then_inc(s["kT_ps"], 1)
                        pe.wait_ge(s["kT_ready"], g * KC + KC)
                        for t in range(BLK + 1):
                            if t:
                                pe.wait_ge(s["kf_ready"], g * (3 * BLK) + 3 * t)
                            if t < BLK:
                                for m in range(KC):
                                    t_.matmul(bank[4 + m], kT[:, m, t * P:(t + 1) * P], rm, start=True, stop=True)
                                project_bias(bank[6][:, 0:D], lambda k: xT[:, k, t * P:(t + 1) * P],
                                             lambda k: wv0[:, k, :], bv0).then_inc(s["kf_ps"], 1)
                            if t:
                                u = t - 1
                                for p in range(PAIRS):
                                    mm = t_.matmul(bank[7][:, p * 2 * VC:(p + 1) * 2 * VC],
                                                   kf[:, u % 2, p * P:(p + 1) * P],
                                                   vext[:, u % 2, 2 * p:2 * p + 2, :].rearrange("p h c -> p (h c)"),
                                                   start=(u == 0 and p == 0), stop=(u == BLK - 1),
                                                   skip_group_check=True)
                                mm.then_inc(s["kv_ps"], 1)
                    with pe.Fori(0, SB) as b:
                        g = b + q * SB
                        pe.wait_ge(s["kv_done"], q + 1)
                        for m in range(KC):
                            project(bank[m], lambda k: wq0[:, k, m * P:(m + 1) * P],
                                    lambda k: sT[:, k, bass.ds(b * BW, BW)]).then_inc(s["q_ps"], 1)
                        pe.wait_ge(s["qT_ready"], g * KC + KC)
                        for p in range(PAIRS):
                            if p >= 4:
                                pe.wait_ge(s["qf_ready"], g * PAIRS + (p - 3))
                            t_.matmul(bank[2 + p % 4], rm[:, (p % 4) * P:(p % 4 + 1) * P], kT[:, p // 4, :],
                                      start=True, stop=True).then_inc(s["qf_ps"], 1)
                        pe.wait_ge(s["qf_ready"], g * PAIRS + PAIRS)
                        for t in range(BLK + 1):
                            if t:
                                pe.wait_ge(s["o_ready"], g * BLK + t)
                            if t < BLK:
                                for p in range(PAIRS):
                                    mm = t_.matmul(bank[6][:, p * 2 * VC:(p + 1) * 2 * VC], qf[:, p, t * P:(t + 1) * P],
                                                   kv[:, p, :], start=True, stop=True)
                                mm.then_inc(s["o_ps"], 1)
                            if t:
                                u = t - 1
                                if u:
                                    pe.wait_ge(s["y_added"], g * BLK + u)
                                turn(bank[7], o0).then_inc(s["oT_ps"], 1)
                                pe.wait_ge(s["oT_ready"], g * BLK + t)
                                project_bias(bank[7][:, D:2 * D], lambda k: oT0[:, k, :], lambda k: wo0[:, k, :],
                                             bo0).then_inc(s["y_ps"], 1)
                    pe.wait_ge(s["y_added"], q * ST + ST)
            def expert_choice(s, n, c, buf):
                pe.wait_ge(s["xn_ready"], (n + c) + 1)
                turn(bank[0], xne[buf][:, 0, :]).then_inc(s["xT_ps"], 1)
                pe.wait_ge(s["xT_ready"], (n + c) + 1)
                project(bank[1][:, 0:D], lambda k: xTe[:, k, :], lambda k: wqe[:, k, :]).then_inc(s["q_ps"], 1)
                pe.wait_ge(s["qn_ready"], (n + c) + 1)
                turn(bank[0], qc.rearrange("p h d -> p (h d)")).then_inc(s["qnT_ps"], 1)
                pe.wait_ge(s["qnT_ready"], (n + c) + 1)
                for j in range(4):
                    t_.matmul(bank[2 + j], qnT[:, j // 2, :], keys[:, (j % 2) * BW:(j % 2 + 1) * BW],
                              start=True, stop=True).then_inc(s["s_ps"], 1)

            def expert_mix(s, n, c):
                pe.wait_ge(s["oe_ready"], (n + c) + 1)
                turn(bank[6], oe.rearrange("p h d -> p (h d)")).then_inc(s["oT_ps"], 1)
                pe.wait_ge(s["oT_ready"], (n + c) + 1)
                project(bank[7][:, 0:D], lambda k: oTe[:, k, :], lambda k: woute[:, k, :]).then_inc(s["y_ps"], 1)

            def experts(s, c):
                expert_choice(s, 0, c, 0)
                with pe.Fori(0, NT - 2, 2) as n:
                    for e in range(2):
                        expert_choice(s, n + (e + 1), c, 1 - e)
                        expert_mix(s, n + e, c)
                expert_choice(s, NT - 1, c, 1)
                expert_mix(s, NT - 2, c)
                expert_mix(s, NT - 1, c)

            def attention(s):
                with pe.Fori(0, SEQS) as q:
                    with pe.Fori(0, SB) as b:
                        g = b + q * SB
                        cols = bass.ds(b * BW, BW)
                        transpose_block(s, g)
                        pe.wait_ge(s["xT_ready"], g * KC + KC)
                        project(bank[2], lambda k: wkvd[:, k, :], lambda k: sT1[:, k, cols]).then_inc(s["c_ps"], 1)
                        pe.wait_ge(s["c_ready"], g * 2 + 2)
                        t_.matmul(bank[3][0:DR, :], wkr, cb, start=True, stop=True)
                        t_.matmul(bank[4][0:DR, :], wkrs, cb, start=True, stop=True).then_inc(s["r_ps"], 1)
                        project(bank[5][0:DR, :], lambda k: wqr[:, k, :], lambda k: sT1[:, k, cols])
                        project(bank[6][0:DR, :], lambda k: wqrs[:, k, :],
                                lambda k: sT1[:, k, cols]).then_inc(s["r_ps"], 1)
                        for t in range(BLK):
                            mm = t_.matmul(bank[t // 2][:, (t % 2) * D:(t % 2 + 1) * D],
                                           cb[:, t * P:(t + 1) * P], wvup, start=True, stop=True)
                            if t % 2:
                                mm.then_inc(s["v_ps"], 1)
                        pe.wait_ge(s["v_ready"], g * BLK + BLK)
                    with pe.Fori(0, PAIRS) as p:
                        pq = p + q * PAIRS
                        pe.wait_ge(s["rope_copied"], q * (2 * SB) + 2 * SB)
                        pe.wait_ge(s["wpair_ready"], pq * (1 + KC) + (1 + KC))
                        for i in range(8):
                            j = i % 4
                            if i < 4:
                                mm = t_.matmul(bank[i], wpair[:, 0, :], cT[:, j * BW:(j + 1) * BW], start=True, stop=True)
                            else:
                                mm = project(bank[i], lambda k: wpair[:, 1 + k, :],
                                             lambda k: sT1[:, k, j * BW:(j + 1) * BW])
                            mm.then_inc(s["kq_ps"], 1)
                        pe.wait_ge(s["kq_ready"], pq * 16 + 16)
                        for u in range(2 * ST + 1):
                            if u < 2 * ST:
                                e, qt = u // ST, u % ST
                                if u:
                                    pe.wait_ge(s["p_ready"], pq * (2 * ST) + u)
                                rows = slice(64 * e, 64 * e + DR + HD)
                                for j in range((qt + BLK) // BLK):
                                    w = min(BLK, qt + 1 - j * BLK) * P
                                    mm = t_.matmul(bank[j][:, 0:w], QA[rows, qt * P:(qt + 1) * P],
                                                   KA[rows, j * BW:j * BW + w], start=True, stop=True)
                                mm.then_inc(s["s_ps"], 1)
                            if u:
                                values(s, p, pq, u - 1)
                        pe.wait_ge(s["o_read"], pq * (2 * ST) + 2 * ST)
                    with pe.Fori(0, ST) as t:
                        pe.wait_ge(s["pair_done"], q + 1)
                        pe.wait_ge(s["otile_ready"], q * ST + (t + 1))
                        turn(bank[6], otile).then_inc(s["ot_ps"], 1)
                        pe.wait_ge(s["ot_ready"], q * ST + (t + 1))
                        project(bank[7][:, 0:D], lambda k: oT1[:, k, :], lambda k: wo1[:, k, :]).then_inc(s["y_ps"], 1)
                        pe.wait_ge(s["y_added"], q * ST + (t + 1))
            def values(s, p, pq, u):
                e, qt = u // ST, u % ST
                pe.wait_ge(s["p_ready"], pq * (2 * ST) + (u + 1))
                for g in range((qt + BLK) // BLK):
                    n = min(BLK, qt + 1 - g * BLK)
                    if PT_AT[u] + g >= 2:
                        pe.wait_ge(s["pt_ready"], pq * (2 * PTN) + (PT_AT[u] + g - 1))
                    for i in range(n):
                        kt = g * BLK + i
                        mm = t_.transpose(bank[4 + (PT_AT[u] + g) % 2][:, i * P:(i + 1) * P],
                                          probs[:, kt * P:(kt + 1) * P], ident[:])
                    mm.then_inc(s["pt_ps"], 1)
                if u >= 2:
                    pe.wait_ge(s["o_read"], pq * (2 * ST) + (u - 1))
                for g in range((qt + BLK) // BLK):
                    pe.wait_ge(s["pt_ready"], pq * (2 * PTN) + (PT_AT[u] + g + 1))
                    for i in range(min(BLK, qt + 1 - g * BLK)):
                        kt = g * BLK + i
                        vh = vall[:, kt, :, :].rearrange("p h c -> p (h c)")[:, bass.ds(p * (2 * VC) + e * VC, VC)]
                        mm = t_.matmul(bank[6 + u % 2][:, 0:VC], PT[:, kt * P:(kt + 1) * P], vh,
                                       start=(kt == 0), stop=(kt == qt))
                mm.then_inc(s["o_ps"], 1)

            pe.wait_ge(const_ready, 1)
            for c in range(2):
                pe.wait_ge(gsum_ready, c + 1)
                t_.matmul(bank[0][:, c:c + 1], ones[:], gsum[:, c:c + 1],
                          start=True, stop=True).then_inc(gamma_ready, 1)
            begin(pe, 0)
            pe.wait_ge(const_ready, 2)
            ffn(sf, 0)
            if STAGES > 1:
                begin(pe, 1)
                linear_attention(sk)
            if STAGES > 2:
                begin(pe, 2)
                ffn(sf, 1)
            if STAGES > 3:
                begin(pe, 3)
                experts(se, 0 * NT)
            if STAGES > 4:
                begin(pe, 4)
                attention(sa)
            if STAGES > 5:
                begin(pe, 5)
                experts(se, 1 * NT)

        @block.gpsimd
        def _(pool):
            def gather(s, n, c, buf, first):
                pool.wait_ge(s["idx_ready"], (n + c) + 1)
                pool.sem_inc(passed_pool, 1)
                for g in range(NG):
                    if not first:
                        pool.wait_ge(s["slot_free"], (n + c) * NG + (g + 1 - NG))
                        pool.sem_inc(passed_pool, 1)
                    for j in range(GH * TOP):
                        col = g * GH * TOP + j
                        nc.gpsimd.indirect_dma_start(
                            G[:, g, j, :], None, ins["experts"],
                            bass.IndirectOffsetOnAxis(ap=gidx[buf][:, col:col + 1], axis=0)).then_inc(gathered[c // NT][g], 16)

            def experts(s, c):
                gather(s, 0, c, 0, True)
                gather(s, 1, c, 1, False)
                with pool.Fori(2, NT, 2) as n:
                    gather(s, n, c, 0, False)
                    gather(s, n + 1, c, 1, False)

            if STAGES > 3:
                begin(pool, 3)
                experts(se, 0 * NT)
            if STAGES > 5:
                begin(pool, 5)
                experts(se, 1 * NT)


def _pad_pairs(w):
    out = np.zeros((w.shape[0], PAIRS, P), w.dtype)
    w = w.reshape(w.shape[0], PAIRS, 2, HD)
    out[:, :, DR:DR + HD] = w[:, :, 0]
    out[:, :, 64 + DR:64 + DR + HD] = w[:, :, 1]
    return out


def _block_diagonal(w, copies):
    out = np.zeros((copies * w.shape[0], copies * w.shape[1]), w.dtype)
    for i in range(copies):
        out[i * w.shape[0]:(i + 1) * w.shape[0], i * w.shape[1]:(i + 1) * w.shape[1]] = w
    return out


def kernel(**inputs):
    import concourse.bacc as bacc
    from concourse.bass_utils import run_bass_kernel_spmd as run

    nc = bacc.Bacc("TRN2", target_bir_lowering=False, num_devices=1)
    i = {k: np.asarray(a) for k, a in inputs.items()}
    f = np.float32
    half = DR // 2
    inv_freq = (f(1.0) / np.power(f(10000.0), np.arange(0, DR, 2, dtype=f) / f(DR))).astype(f)
    freqs = np.outer(np.arange(SL, dtype=f), inv_freq).astype(f)
    cos, sin = np.cos(freqs).T, np.sin(freqs).T
    swap = np.r_[half:DR, 0:half]
    both = np.zeros((HD, 2 * NK), f)
    both[:HD // 2, :NK] = i["L1_ffn_c_keys"].T
    both[HD // 2:, NK:] = i["L1_ffn_c_prime_keys"].T
    laid = {
        "x": i["L0_attn_x"].reshape(T, D), "ident": np.eye(P, dtype=f),
        "w1t": i["L0_ffn_W1"].T, "b1": i["L0_ffn_b1"].reshape(FC, P).T,
        "w2t": i["L0_ffn_W2"].T, "b2": i["L0_ffn_b2"].reshape(1, D),
        "wq0": i["L0_attn_Wq"], "wk0": i["L0_attn_Wk"], "wv0": i["L0_attn_Wv"], "wo0": i["L0_attn_Wo"],
        "bq0": i["L0_attn_bq"].reshape(KC, P).T, "bk0": i["L0_attn_bk"].reshape(KC, P).T,
        "bv0": i["L0_attn_bv"].reshape(1, D), "bo0": i["L0_attn_bo"].reshape(1, D),
        "rm": _block_diagonal(i["L0_attn_random_matrix"], HK),
        "wqe": i["L1_ffn_Wq"], "woute": i["L1_ffn_Wout"], "keys": _block_diagonal(both, HK),
        "lng": i["L1_ffn_ln_g"], "lnb": i["L1_ffn_ln_b"], "iota": np.arange(NJ, dtype=f),
        "experts": np.concatenate([i["L1_ffn_w_down"], i["L1_ffn_w_up"]], axis=1),
        "wkvd": i["L1_attn_W_kv_down"], "wkup": _pad_pairs(i["L1_attn_W_k_up"]), "wqp": _pad_pairs(i["L1_attn_W_q"]),
        "wvup": i["L1_attn_W_v_up"], "wqr": i["L1_attn_W_q_rope"], "wqrs": i["L1_attn_W_q_rope"][:, swap],
        "wkr": i["L1_attn_W_k_rope"], "wkrs": i["L1_attn_W_k_rope"][:, swap], "wo1": i["L1_attn_W_o"],
        "cos": np.concatenate([cos, cos]), "sin": np.concatenate([-sin, sin]),
        "causal": np.where(np.arange(P)[None, :] > np.arange(P)[:, None], f(LOWEST), f(0)).astype(f),
    }
    arrays, ins = {}, {}
    for name, a in laid.items():
        a = np.ascontiguousarray(a)
        arrays[f"in_{name}"] = a
        ins[name] = nc.dram_tensor(f"in_{name}", a.shape, mybir.dt.from_np(a.dtype), kind="ExternalInput").ap()
    out = nc.dram_tensor("out_x", (T, D), F32, kind="ExternalOutput").ap()
    macaron(nc, ins, out)
    r = run(nc, [arrays], core_ids=[0])
    return r.results[0]["out_x"].reshape(SEQS, SL, D)
```

```python
import numpy as np
import concourse.bass as bass
from concourse import mybir
from concourse.alu_op_type import AluOpType as ALU
from contextlib import ExitStack

F32 = mybir.dt.float32
I32 = mybir.dt.int32
BF16 = mybir.dt.bfloat16
ACT = mybir.ActivationFunctionType
AX = mybir.AxisListType

P = 128
SEQS = 2
T = 4096
NT = T // P
ST = NT // SEQS
SL = T // SEQS
BLK = 4
BW = BLK * P
NB = NT // BLK
SB = ST // BLK
D = 256
KC = D // P
FF = 1024
FC = FF // P
EPS = 1e-5
H = 16
HD = D // H
PAIRS = H // 2
HK = P // HD
M0 = 64
VC = HD + 1
DR = 32
DC = 128
SCALE = float(1.0 / np.sqrt(HD + DR))
NK = 64
TOP = 16
TOP1 = 24
SEGS = [(0, 1, 17, 0), (1, 1, 8, 17), (2, 1, 5, 25), (3, 1, 4, 30), (4, 1, 3, 34), (5, 3, 2, 37), (8, 9, 1, 43)]
NJ = 52
NE = NK * NK
CH = NE // P
CR = P // NK
YG = P // (CR * HD)
NG = CH // YG
NW = NE + P + NG * P
W_PARTS = [0, 1, 2, 0, 1, 0]
NS = len(W_PARTS)
FT = HD + 3
NF = FT + HD
RING = 4
AHEAD = 4
LISTS_AT = 26
CHOSEN_AT = LISTS_AT + 77
LARGEST_AT = [0, 1, 3, 4, 6]
SPLIT_AT = CHOSEN_AT % CH + 5
EARLY = 5
F_BANK = [5, 6, 7, 5, 6, 7, 5, 6, 7]
UNITS = NB * H
LOWEST = -3.0e38
GROUPS = [(u % ST + BLK) // BLK for u in range(2 * ST)]
PT_AT = [sum(GROUPS[:u]) for u in range(2 * ST)]
PTN = sum(GROUPS) // 2
STAGES = 6


class Chain:

    def __init__(self, eng, sem):
        self.eng, self.sem, self.n = eng, sem, 0

    def mark(self, ins):
        ins.then_inc(self.sem, 1)
        self.n += 1

    def sync(self):
        self.eng.wait_ge(self.sem, self.n)

    def link(self, ins):
        self.mark(ins)
        self.sync()

    def restart(self):
        self.sync()
        self.eng.sem_clear(self.sem)
        self.n = 0


class Arena:

    def __init__(self, tensor, words):
        self.tensor, self.words, self.at = tensor, words, 0

    def reset(self):
        self.at = 0

    def take(self, *shape, parts=P, dt=F32):
        n = int(np.prod(shape))
        assert self.at + n <= self.words, (self.at, n, self.words)
        v = self.tensor[0:parts, self.at:self.at + n]
        self.at += n
        if dt is not F32:
            v = v.bitcast(dt)
        if len(shape) == 2:
            v = v.rearrange("p (a b) -> p a b", a=shape[0])
        elif len(shape) == 3:
            v = v.rearrange("p (a b c) -> p a b c", a=shape[0], b=shape[1])
        return v


def macaron(nc, ins, out):
    ctx = ExitStack()
    with ctx:
        def sb(name, shape, dt=F32):
            return ctx.enter_context(nc.sbuf_tensor(name, shape, dt))

        def sem(name):
            return ctx.enter_context(nc.semaphore(name))

        def sems(prefix, names):
            return {n: sem(f"{prefix}_{n}") for n in names.split()}

        psum = ctx.enter_context(nc.psum_tensor("psum", [P, 8, 512], F32))
        bank = [psum[:, i, :] for i in range(8)]

        X = sb("X", [P, NT, D])
        ident = sb("ident", [P, P])
        ones = sb("ones", [P, P])
        stats = sb("stats", [P, BLK, 6])
        mv = sb("mv", [P, BLK, 2])
        var = sb("var", [P, BLK])
        rstd = sb("rstd", [P, BLK])
        newton = sb("newton", [P, BLK])
        xn = sb("xn", [P, BLK, D])
        xT = sb("xT", [P, KC, BW])
        WORDS = 42000
        arena = Arena(sb("arena", [P, WORDS]), WORDS)

        w1t = arena.take(KC, FF)
        w2t = arena.take(FC, D)
        b1c = arena.take(FC)
        b2r = arena.take(D, parts=1)
        gsum = arena.take(2)
        thr = arena.take(4)
        wq0, wk0, wv0, wo0 = [arena.take(KC, D) for _ in range(4)]
        bq0, bk0 = arena.take(KC), arena.take(KC)
        bv0, bo0 = arena.take(D, parts=1), arena.take(D, parts=1)
        rm = arena.take(HK * M0)
        kv = arena.take(PAIRS, 2 * VC)
        vext = arena.take(2, H, VC)
        h = arena.take(FC, BW)
        wtmp = h.rearrange("p a b -> p (a b)")
        sT = arena.take(KC, SL)
        kT = arena.take(KC, BW)
        emin = arena.take(2, BW)
        efeat = arena.take(2, BW)
        kf = arena.take(2, PAIRS * P)
        o0 = arena.take(D)
        oT0 = arena.take(KC, P)
        nrm = arena.take(H)
        rnrm = arena.take(H)
        qf = h

        arena.reset()
        wqe = arena.take(KC, D)
        woute = arena.take(BLK, D, parts=4 * HD)
        keys = arena.take(HK * 2 * NK)
        lng = arena.take(HD)
        lnb = arena.take(HD)
        upw = arena.take(CH, CR * HD)
        fold = arena.take(4, 4 * HD)
        identb = arena.take(P // 2, dt=BF16)
        partl = arena.take(3, parts=NS * HD)
        partd = arena.take(3, parts=NS * FT)
        down = arena.take(NE // 2, parts=NS * HD, dt=BF16)
        pairk = arena.take(NW // 2, parts=NS * FT, dt=BF16)
        xne = arena.take(1, D)
        xTe = arena.take(KC, P)
        qc = arena.take(H, HD)
        qsq = arena.take(H, HD)
        hmean = arena.take(H)
        hvar = arena.take(H)
        hrstd = arena.take(H)
        hnewton = arena.take(H)
        qnT = arena.take(KC, P)
        scores = arena.take(2 * H, NK)
        scoresB = arena.take(2 * H, NK)
        V = arena.take(2 * H, TOP1)
        J = arena.take(H, NJ)
        best = arena.take(H, TOP1)
        edge = arena.take(H)
        wexp = arena.take(H, TOP)
        wsum = arena.take(H)
        split = arena.take(BLK, NF)
        part1 = arena.take(BLK * NF // 2, dt=BF16).rearrange("p (t f) -> p t f", t=BLK)
        part2 = arena.take(BLK * NF // 2, dt=BF16).rearrange("p (t f) -> p t f", t=BLK)
        slotd = arena.take(BLK * NS * FT // 2, dt=BF16).rearrange("p (t s f) -> p t s f", t=BLK, s=NS)
        slotl = arena.take(BLK * NS * HD // 2, dt=BF16).rearrange("p (t s f) -> p t s f", t=BLK, s=NS)
        dT = [arena.take(BW // 2, parts=NS * FT, dt=BF16) for _ in range(2)]
        lT = [arena.take(BW // 2, parts=NS * HD, dt=BF16) for _ in range(2)]
        E2 = [arena.take(BW) for _ in range(2)]
        acc = arena.take(4, BW)
        ytmp = xT
        oTe = arena.take(BLK, BW, parts=4 * HD)
        tables_at = arena.at
        E1 = arena.take(2, NG, BW)
        F = arena.take(BLK, 2 * H, NF)
        downf = arena.tensor[0:NS * HD, tables_at:tables_at + NE]
        pairf = arena.tensor[0:NS * FT, tables_at + NE:tables_at + NE + NW]
        parts_at = arena.at
        GE = arena.take(RING, BW)
        GM = arena.take(RING, BW)
        HH = arena.take(RING, BW)
        tpart = [arena.tensor[:, parts_at + i * NW // 2:parts_at + (i + 1) * NW // 2].bitcast(BF16) for i in range(2)]

        arena.reset()
        wkvd = arena.take(KC, DC)
        wkup = arena.take(PAIRS, P)
        wqp = arena.take(KC, PAIRS, P)
        wvup = arena.take(D)
        wqr, wqrs = arena.take(KC, DR), arena.take(KC, DR)
        wkr, wkrs = arena.take(DR), arena.take(DR)
        wo1 = arena.take(KC, D)
        cosT = arena.take(SL, parts=DR)
        sinT = arena.take(SL, parts=DR)
        causal = arena.take(P)
        rt = arena.take(4, BW, parts=DR)
        QA = arena.take(SL)
        KA = arena.take(SL)
        cb = arena.take(BW)
        cT = arena.take(SL)
        wpair = arena.take(1 + KC, P)
        otile = arena.take(D)
        vall = arena.take(ST, H, VC)
        probs = arena.take(SL)
        PT = arena.take(SL)
        oall = arena.take(ST, D)
        sT1 = arena.take(KC, SL)
        rmax = arena.take(2, 1)
        nmax = arena.take(2, 1)
        rden = arena.take(2, 1)
        oT1 = arena.take(KC, P)

        loaded = [sem(f"loaded{i}") for i in range(5)]
        const_ready = sem("const_ready")
        dve_chain = sem("dve_chain")
        gsum_ready = sem("gsum_ready")
        gamma_ready = sem("gamma_ready")
        phase_done = sem("phase_done")
        stored = sem("stored")
        passed_dve = sem("passed_dve")
        sf = sems("ffn", "xn_ready xT_ps xT_ready h_ps h_ready out_ps")
        sk = sems("lin", "xn_ready xT_ps xT_ready kT_ps kT_ready kf_ps emin_ready e_ready kf_ready kv_ps "
                              "q_ps qT_ready qf_ps qmin_ready qe_ready qf_ready o_ps o_ready oT_ps oT_ready y_ps "
                              "y_added kv_done")
        se = sems("exp", "xn_ready xT_ps xT_ready q_ps qn_ready qnT_ps qnT_ready s_ps s_ready sum_ready log_ready "
                         "shift_ready w_ready f_ready split_ready slots_ps slots_ready e_ps e_ready l_ps ge_ready "
                         "d_ps gm_ready h_made up_ps y_weighed acc_ready fold_ps oT_ready y_ps y_added tables_ready")
        pool_chain = sem("pool_chain")
        sa = sems("att", "xn_ready xT_ps xT_ready c_ps c_ready r_ps r_ready rope_copied v_ps v_ready "
                              "wpair_ready otile_ready kq_ps kq_ready pair_done s_ps m_ready p_ready pt_ps pt_ready o_ps o_read ot_ps "
                              "ot_ready y_ps y_added")

        block = ctx.enter_context(nc.Block())

        L0_LOADS = [
            (X[:], ins["x"].rearrange("(t p) d -> p t d", p=P)), (ident[:], ins["ident"]),
            (w1t, ins["w1t"].rearrange("(k p) f -> p k f", p=P)),
            (w2t, ins["w2t"].rearrange("(k p) f -> p k f", p=P)),
            (b1c, ins["b1"]), (b2r, ins["b2"]),
            (wq0, ins["wq0"].rearrange("(k p) n -> p k n", p=P)), (wk0, ins["wk0"].rearrange("(k p) n -> p k n", p=P)),
            (wv0, ins["wv0"].rearrange("(k p) n -> p k n", p=P)), (wo0, ins["wo0"].rearrange("(k p) n -> p k n", p=P)),
            (bq0, ins["bq0"]), (bk0, ins["bk0"]), (bv0, ins["bv0"]), (bo0, ins["bo0"]), (rm, ins["rm"])]
        EXP_LOADS = [
            (wqe, ins["wqe"].rearrange("(k p) n -> p k n", p=P)),
            (woute, ins["woute"].rearrange("(j p) n -> p j n", p=4 * HD)), (fold, ins["fold"]),
            (keys, ins["keys"]), (lng, ins["lng"].partition_broadcast(P)), (lnb, ins["lnb"].partition_broadcast(P)),
            (upw, ins["upw"]), (partl, ins["partl"]), (partd, ins["partd"]),
            (downf, ins["down"]), (pairf, ins["pairk"])]
        ATT_LOADS = [
            (wkvd, ins["wkvd"].rearrange("(k p) n -> p k n", p=P)), (wkup, ins["wkup"]),
            (wqp, ins["wqp"].rearrange("(k p) a n -> p k a n", p=P)), (wvup, ins["wvup"]),
            (wqr, ins["wqr"].rearrange("(k p) n -> p k n", p=P)), (wqrs, ins["wqrs"].rearrange("(k p) n -> p k n", p=P)),
            (wkr, ins["wkr"]), (wkrs, ins["wkrs"]), (wo1, ins["wo1"].rearrange("(k p) n -> p k n", p=P)),
            (cosT, ins["cos"]), (sinT, ins["sin"]), (causal, ins["causal"])]
        PHASE_LOADS = [L0_LOADS, [], [], EXP_LOADS, ATT_LOADS, EXP_LOADS]

        @block.sync
        def _(sp):
            for ph, loads in enumerate(PHASE_LOADS[:STAGES]):
                if ph and loads:
                    sp.wait_ge(phase_done, ph)
                for dst, src in loads:
                    sp.dma_start(dst, src).then_inc(loaded[[0, 0, 0, 1, 2, 3][ph]], 16)
            sp.wait_ge(phase_done, STAGES)
            sp.dma_start(out.rearrange("(t p) d -> p t d", p=P), X[:]).then_inc(stored, 16)
            sp.wait_ge(stored, 16)

        def begin(eng, ph):
            if ph:
                eng.wait_ge(phase_done, ph)
            if PHASE_LOADS[ph]:
                eng.wait_ge(loaded[[0, 0, 0, 1, 2, 3][ph]], 16 * len(PHASE_LOADS[ph]))

        @block.vector
        def _(dve):
            ch = Chain(dve, dve_chain)
            v = nc.vector

            def end_phase():
                ch.sync()
                dve.sem_inc(phase_done, 1)

            def rsqrt_guess(y, x, c):
                ch.link(v.tensor_scalar(c.bitcast(I32), x.bitcast(I32), 1, None, ALU.logical_shift_right))
                ch.link(v.tensor_scalar(y.bitcast(I32), c.bitcast(I32), -1.0, float(0x5f3759df), ALU.mult, ALU.add))

            def rsqrt_step(y, x, c):
                ch.link(v.scalar_tensor_tensor(out=c, in0=y, scalar=-0.5, in1=x, op0=ALU.mult, op1=ALU.mult))
                ch.link(v.tensor_tensor(c, c, y, ALU.mult))
                ch.link(v.scalar_tensor_tensor(out=y, in0=c, scalar=1.5, in1=y, op0=ALU.add, op1=ALU.mult))

            def rsqrt(y, x, c):
                rsqrt_guess(y, x, c)
                for _ in range(3):
                    rsqrt_step(y, x, c)

            def layernorm(srcs, dst, ready):
                n = len(srcs)
                for t, src in enumerate(srcs):
                    ch.mark(v.bn_stats(stats[:, t, :], src))
                ch.sync()
                for t in range(n):
                    ch.mark(v.bn_aggr(mv[:, t, :], stats[:, t, :]))
                ch.sync()
                ch.link(v.tensor_scalar(var[:, 0:n], mv[:, 0:n, 1], EPS, None, ALU.add))
                rsqrt(rstd[:, 0:n], var[:, 0:n], newton[:, 0:n])
                for t, src in enumerate(srcs):
                    v.tensor_scalar(dst[:, t, :], src, mv[:, t, 0:1], rstd[:, t:t + 1],
                                    ALU.subtract, ALU.mult).then_inc(ready, 1)

            def ternary(w, col, count):
                ch.link(v.scalar_tensor_tensor(out=wtmp[:, 0:count // P], in0=w, scalar=-1.0, in1=w,
                                               op0=ALU.mult, op1=ALU.max))
                v.reduce_sum(gsum[:, col:col + 1], wtmp[:, 0:count // P], AX.X).then_inc(gsum_ready, 1)
                dve.wait_ge(gamma_ready, col + 1)
                tot = bank[0][:, col:col + 1]
                ch.mark(v.tensor_scalar(thr[:, 0:1], tot, 0.5 / count, 0.5 * EPS, ALU.mult, ALU.add))
                ch.mark(v.tensor_scalar(thr[:, 1:2], tot, -0.5 / count, -0.5 * EPS, ALU.mult, ALU.add))
                ch.sync()
                ch.link(v.tensor_scalar(wtmp[:, 0:count // P], w, thr[:, 1:2], None, ALU.is_lt))
                ch.link(v.scalar_tensor_tensor(out=w, in0=w, scalar=thr[:, 0:1], in1=wtmp[:, 0:count // P],
                                               op0=ALU.is_gt, op1=ALU.subtract))

            def ffn(s, r):
                ch.restart()
                with dve.Fori(0, NB) as b:
                    g = b + r * NB
                    layernorm([X[:, b * BLK + t, :] for t in range(BLK)], xn, s["xn_ready"])
                    for t in range(BLK):
                        dve.wait_ge(s["out_ps"], g * BLK + (t // 2 * 2 + 2))
                        xt = X[:, b * BLK + t, :]
                        ps = bank[6 + t // 2][:, (t % 2) * D:(t % 2 + 1) * D]
                        ch.mark(v.scalar_tensor_tensor(out=xt, in0=ps, scalar=0.5, in1=xt, op0=ALU.mult, op1=ALU.add))
                    ch.restart()

            def linear_attention(s):
                ch.restart()
                with dve.Fori(0, SEQS) as q:
                    ch.mark(v.memset(kv, 0.0))
                    ch.mark(v.memset(vext[:, :, :, HD:VC], 1.0))
                    ch.restart()
                    with dve.Fori(0, SB) as b:
                        g = b + q * SB
                        layernorm([X[:, g * BLK + t, :] for t in range(BLK)], xn, s["xn_ready"])
                        for t in range(BLK):
                            dve.wait_ge(s["kf_ps"], g * BLK + (t + 1))
                            for m in range(KC):
                                v.tensor_scalar(emin[:, m, :], bank[4 + m], 0.0, None,
                                                ALU.min).then_inc(s["emin_ready"], 1)
                            dve.wait_ge(s["e_ready"], g * BLK + (t + 1))
                            if t >= 2:
                                dve.wait_ge(s["kv_ps"], g * BLK + (t - 1))
                            for m in range(KC):
                                v.scalar_tensor_tensor(out=kf[:, t % 2, m * BW:(m + 1) * BW], in0=bank[4 + m],
                                                       scalar=0.0, in1=efeat[:, m, :], op0=ALU.max,
                                                       op1=ALU.add).then_inc(s["kf_ready"], 1)
                            v.tensor_copy(vext[:, t % 2, :, 0:HD],
                                          bank[6][:, 0:D].rearrange("p (h d) -> p h d", h=H)).then_inc(s["kf_ready"], 1)
                        dve.wait_ge(s["kv_ps"], g * BLK + BLK)
                        ps = bank[7][:, 0:PAIRS * 2 * VC].rearrange("p (a c) -> p a c", a=PAIRS)
                        for e in range(2):
                            rows, cols = slice(64 * e, 64 * e + 64), slice(VC * e, VC * e + VC)
                            ch.mark(v.scalar_tensor_tensor(out=kv[rows, :, cols], in0=ps[rows, :, cols],
                                                           scalar=1.0 / 256, in1=kv[rows, :, cols],
                                                           op0=ALU.mult, op1=ALU.add))
                        ch.restart()
                    dve.sem_inc(s["kv_done"], 1)
                    with dve.Fori(0, SB) as b:
                        g = b + q * SB
                        for p in range(PAIRS + 1):
                            if p < PAIRS:
                                dve.wait_ge(s["qf_ps"], g * PAIRS + (p + 1))
                                v.tensor_scalar(emin[:, p % 2, :], bank[2 + p % 4], 0.0, None,
                                                ALU.min).then_inc(s["qmin_ready"], 1)
                            if p:
                                dve.wait_ge(s["qe_ready"], g * PAIRS + p)
                                v.scalar_tensor_tensor(out=qf[:, p - 1, :], in0=bank[2 + (p - 1) % 4], scalar=0.0,
                                                       in1=efeat[:, (p - 1) % 2, :], op0=ALU.max,
                                                       op1=ALU.add).then_inc(s["qf_ready"], 1)
                        for t in range(BLK):
                            dve.wait_ge(s["o_ps"], g * BLK + (t + 1))
                            ps = bank[6][:, 0:H * VC].rearrange("p (h c) -> p h c", h=H)
                            ch.link(v.tensor_scalar(nrm, ps[:, :, HD], 1e-6, None, ALU.max))
                            ch.link(v.reciprocal(rnrm, nrm))
                            v.tensor_tensor(o0.rearrange("p (h d) -> p h d", h=H), ps[:, :, 0:HD],
                                            rnrm[:, :, None].to_broadcast([P, H, HD]), ALU.mult).then_inc(s["o_ready"], 1)
                            dve.wait_ge(s["y_ps"], g * BLK + (t + 1))
                            xt = X[:, g * BLK + t, :]
                            ch.link(v.tensor_tensor(xt, bank[7][:, D:2 * D], xt, ALU.add))
                            dve.sem_inc(s["y_added"], 1)
                        ch.restart()

            def build_table(table, src, part, width):
                p1, p2 = [x[0:part.shape[0], 0:width] for x in tpart]
                ch.link(v.tensor_copy(p1, src))
                ch.link(v.tensor_tensor(src, src, p1, ALU.subtract))
                ch.link(v.tensor_copy(p2, src))
                ch.link(v.tensor_tensor(src, src, p2, ALU.subtract))
                ch.link(v.tensor_scalar(table, p1, part[:, 0:1], None, ALU.mult))
                ch.link(v.scalar_tensor_tensor(out=table, in0=p2, scalar=part[:, 1:2], in1=table,
                                               op0=ALU.mult, op1=ALU.add))
                ch.link(v.scalar_tensor_tensor(out=table, in0=src, scalar=part[:, 2:3], in1=table,
                                               op0=ALU.mult, op1=ALU.add))

            def largest(dst, src, rest, rows, step):
                ch.sync()
                for r in rows:
                    at = dst[:, r, step // 2 * 8:step // 2 * 8 + 8]
                    if step % 2 == 0:
                        ch.mark(v.max(at, (rest if step else src)[:, r, :]))
                    else:
                        ch.mark(v.match_replace(rest[:, r, :], at, (src if step == 1 else rest)[:, r, :], LOWEST))

            def sums(half, segs):
                hs = slice(half * H // 2, (half + 1) * H // 2)
                v4 = V.rearrange("p (h two) k -> p h two k", two=2)[:, hs]
                for i0, ni, nj, off in segs:
                    x = v4[:, :, 0, i0:i0 + ni][:, :, :, None].to_broadcast([P, H // 2, ni, nj])
                    y = v4[:, :, 1, 0:nj][:, :, None, :].to_broadcast([P, H // 2, ni, nj])
                    o = J[:, hs, off:off + ni * nj].rearrange("p h (i j) -> p h i j", i=ni)
                    if ni == 1:
                        x, y, o = x[:, :, 0, :], y[:, :, 0, :], o[:, :, 0, :]
                    elif nj == 1:
                        x, y, o = x[:, :, :, 0], y[:, :, :, 0], o[:, :, :, 0]
                    ch.mark(v.tensor_tensor(o, x, y, ALU.add))

            def expert_choice(s, g, j, c, k, i):
                n = g * BLK + j
                cnt = n + c * NT
                rows = bass.ds((g % 2) * H, H)
                at = k * CH + i
                if at == 0:
                    ch.link(v.bn_stats(stats[:, 0, :], X[:, n, :]))
                    ch.link(v.bn_aggr(mv[:, 0, :], stats[:, 0, :]))
                    ch.link(v.tensor_scalar(var[:, 0:1], mv[:, 0:1, 1], EPS, None, ALU.add))
                if at == 1:
                    rsqrt_guess(rstd[:, 0:1], var[:, 0:1], newton[:, 0:1])
                if at in (1, 2, 3):
                    rsqrt_step(rstd[:, 0:1], var[:, 0:1], newton[:, 0:1])
                if at == 4:
                    v.tensor_scalar(xne[:, 0, :], X[:, n, :], mv[:, 0, 0:1], rstd[:, 0:1],
                                    ALU.subtract, ALU.mult).then_inc(s["xn_ready"], 1)
                if at == 5:
                    dve.wait_ge(s["xn_ready"], cnt + 1)
                    ch.mark(v.tensor_copy(F[:, j, rows, FT:NF], xne[:, 0, :].rearrange("p (h d) -> p h d", h=H)))
                if at == 11:
                    dve.wait_ge(s["q_ps"], cnt + 1)
                    q = bank[7][:, 0:D].rearrange("p (h d) -> p h d", h=H)
                    ch.link(v.reduce_sum(hmean, q, AX.X))
                    ch.link(v.tensor_scalar(hmean, hmean, 1.0 / HD, None, ALU.mult))
                    ch.link(v.tensor_tensor(qc, q, hmean[:, :, None].to_broadcast([P, H, HD]), ALU.subtract))
                if at == 12:
                    ch.link(v.tensor_tensor(qsq, qc, qc, ALU.mult))
                    ch.link(v.reduce_sum(hvar, qsq, AX.X))
                if at == 13:
                    ch.link(v.tensor_scalar(hvar, hvar, 1.0 / HD, EPS, ALU.mult, ALU.add))
                    rsqrt_guess(hrstd, hvar, hnewton)
                if at in (14, 15, 16):
                    rsqrt_step(hrstd, hvar, hnewton)
                if at == 17:
                    ch.link(v.tensor_tensor(qc, qc, hrstd[:, :, None].to_broadcast([P, H, HD]), ALU.mult))
                    ch.link(v.tensor_tensor(qc, qc, lng[:, None, :].to_broadcast([P, H, HD]), ALU.mult))
                if at == 18:
                    v.tensor_tensor(qc, qc, lnb[:, None, :].to_broadcast([P, H, HD]), ALU.add).then_inc(s["qn_ready"], 1)
                if at == 20:
                    dve.wait_ge(s["qn_ready"], cnt + 1)
                    ch.mark(v.tensor_copy(F[:, j, rows, 0:HD], qc))
                if at in (LISTS_AT, LISTS_AT + 32):
                    dve.wait_ge(s["s_ready"], cnt * 4 + (2 if at == LISTS_AT else 4))
                    dve.sem_inc(passed_dve, 1)
                if LISTS_AT <= at < LISTS_AT + 4 * H:
                    two, step = divmod(at - LISTS_AT, 8)
                    if step in LARGEST_AT:
                        largest(V, scores, scoresB, range(4 * two, 4 * two + 4), LARGEST_AT.index(step))
                for half in range(2):
                    to = at - (LISTS_AT + 4 * H // 2 * (half + 1))
                    if 0 <= to < 3:
                        ch.sync()
                        sums(half, SEGS[3 * to:3 * to + 3])
                if LISTS_AT + 35 <= at < LISTS_AT + 65 and (at - LISTS_AT - 35) % 3 == 0:
                    four, step = divmod((at - LISTS_AT - 35) // 3, 5)
                    largest(best, J, J, range(4 * four, 4 * four + 4), step)
                if LISTS_AT + 67 <= at < CHOSEN_AT:
                    four, step = divmod(at - LISTS_AT - 67, 5)
                    largest(best, J, J, range(4 * four + 8, 4 * four + 12), step)
                if at == CHOSEN_AT:
                    ch.sync()
                    v.tensor_tensor(wexp, best[:, :, 0:TOP], best[:, :, 0:1].to_broadcast([P, H, TOP]),
                                    ALU.subtract).then_inc(s["shift_ready"], 1)
                    ch.link(v.tensor_tensor(edge, best[:, :, TOP - 1], best[:, :, TOP], ALU.add))
                    ch.link(v.tensor_scalar(F[:, j, rows, HD], edge, 0.5, None, ALU.mult))
                    v4 = V.rearrange("p (h two) k -> p h two k", two=2)
                    ch.mark(v.tensor_copy(F[:, j, rows, HD + 1:HD + 2], v4[:, :, 1, 0:1]))
                if at == CHOSEN_AT + 1:
                    dve.wait_ge(s["w_ready"], cnt + 1)
                    v.reduce_sum(wsum, wexp, AX.X).then_inc(s["sum_ready"], 1)
                if at == CHOSEN_AT + 3:
                    dve.wait_ge(s["log_ready"], cnt + 1)
                    v4 = V.rearrange("p (h two) k -> p h two k", two=2)
                    ch.link(v.tensor_tensor(F[:, j, rows, HD + 2], v4[:, :, 0, 0], wsum, ALU.add))
                    dve.sem_inc(s["f_ready"], 1)

            def weigh(s, U, k, g):
                dve.wait_ge(s["up_ps"], RING + U * CH + YG * (g + 1))
                dve.wait_ge(s["e_ready"], U * (1 + NG) + (2 + g))
                ch.sync()
                dst = ytmp[:, g % 2, :] if g else acc[:, k, :]
                v.tensor_tensor(dst, bank[4], E1[:, k % 2, g, :], ALU.mult).then_inc(s["y_weighed"], 1)
                if g >= 2:
                    dve.wait_ge(s["y_weighed"], U * NG + (g + 1))
                    ch.mark(v.tensor_tensor(acc[:, k, :], acc[:, k, :], ytmp[:, (g - 1) % 2, :], ALU.add))
                if g == NG - 1:
                    dve.wait_ge(s["y_weighed"], U * NG + (g + 2))
                    ch.sync()
                    ch.mark(v.tensor_tensor(acc[:, k, :], acc[:, k, :], ytmp[:, g % 2, :], ALU.add))

            def expert_group(s, b, j, c, choose, first):
                G = (b * BLK + j) + c * NT
                for k in range(4):
                    U = G * 4 + k
                    dve.wait_ge(s["e_ready"], U * (1 + NG) + 1)
                    for i in range(CH):
                        dve.wait_ge(s["d_ps"], U * CH + (i + 1))
                        dve.wait_ge(s["h_made"], U * CH + (i + 1))
                        v.scalar_tensor_tensor(out=GM[:, i % RING, :], in0=bank[2 + i % 2], scalar=0.0, in1=E2[k % 2],
                                               op0=ALU.is_ge, op1=ALU.mult).then_inc(s["gm_ready"], 1)
                        if i == 3 and (k or not first):
                            weigh(s, U - 1, (k - 1) % 4, NG - 1)
                            if k == 0:
                                ch.sync()
                                dve.sem_inc(s["acc_ready"], 1)
                        if k == 0 and i == 6 and not first:
                            dve.wait_ge(s["fold_ps"], G + 1)
                        if i % 4 == 3 and i > 3:
                            weigh(s, U, k, i // 4 - 1)
                        if choose:
                            expert_choice(s, b + 1, j, c, k, i)

            def expert_block(s, b, c, choose):
                expert_group(s, b, 0, c, choose, True)
                ch.restart()
                with dve.Fori(1, BLK) as j:
                    expert_group(s, b, j, c, choose, False)
                    ch.restart()
                weigh(s, b * H + (c * UNITS + H - 1), 3, NG - 1)
                ch.sync()
                dve.sem_inc(s["acc_ready"], 1)
                for t in range(BLK):
                    n = b * BLK + t
                    dve.wait_ge(s["y_ps"], n + (c * NT + 1))
                    ch.link(v.scalar_tensor_tensor(out=X[:, n, :], in0=bank[7][:, (t % 2) * D:(t % 2 + 1) * D], scalar=0.5,
                                                   in1=X[:, n, :], op0=ALU.mult, op1=ALU.add))
                    dve.sem_inc(s["y_added"], 1)
                ch.restart()

            def experts(s, c):
                ch.mark(v.tensor_copy(identb, ident[:]))
                build_table(down, downf, partl, NE)
                build_table(pairk, pairf, partd, NW)
                dve.sem_inc(s["tables_ready"], 1)
                if c == 0:
                    dve.sem_inc(s["h_made"], RING)
                ch.restart()
                with dve.Fori(0, BLK) as j:
                    for k in range(4):
                        for i in range(CH):
                            expert_choice(s, 0, j, c, k, i)
                    ch.restart()
                with dve.Fori(0, NB - 1) as b:
                    expert_block(s, b, c, True)
                expert_block(s, NB - 1, c, False)

            def attention(s):
                ch.restart()
                with dve.Fori(0, SEQS) as q:
                    ch.mark(v.memset(vall[:, :, :, HD:VC], 1.0))
                    ch.restart()
                    with dve.Fori(0, SB) as b:
                        g = b + q * SB
                        layernorm([X[:, g * BLK + t, :] for t in range(BLK)], xn, s["xn_ready"])
                        cols = bass.ds(b * BW, BW)
                        for i, to in enumerate((KA, QA)):
                            dve.wait_ge(s["r_ps"], g * 2 + (i + 1))
                            ch.mark(v.tensor_tensor(rt[:, 2 * i, :], bank[3 + 2 * i][0:DR, :], cosT[:, cols], ALU.mult))
                            ch.mark(v.tensor_tensor(rt[:, 2 * i + 1, :], bank[4 + 2 * i][0:DR, :], sinT[:, cols], ALU.mult))
                            ch.sync()
                            v.tensor_tensor(to[0:DR, cols], rt[:, 2 * i, :], rt[:, 2 * i + 1, :],
                                            ALU.add).then_inc(s["r_ready"], 1)
                        for t in range(BLK):
                            dve.wait_ge(s["v_ps"], g * 2 + (t // 2 + 1))
                            ps = bank[t // 2][:, (t % 2) * D:(t % 2 + 1) * D].rearrange("p (h d) -> p h d", h=H)
                            v.tensor_copy(vall[:, b * BLK + t, :, 0:HD], ps).then_inc(s["v_ready"], 1)
                        ch.restart()
                    with dve.Fori(0, PAIRS) as p:
                        pq = p + q * PAIRS
                        v.tensor_copy(wpair[:, 0, :], wkup[:, p, :]).then_inc(s["wpair_ready"], 1)
                        for k in range(KC):
                            v.tensor_copy(wpair[:, 1 + k, :], wqp[:, k, p, :]).then_inc(s["wpair_ready"], 1)
                        for i in range(8):
                            dve.wait_ge(s["kq_ps"], pq * 8 + (i + 1))
                            to, j = (KA, i) if i < 4 else (QA, i - 4)
                            for e in range(2):
                                r0 = 64 * e + DR
                                v.tensor_copy(to[r0:r0 + HD, j * BW:(j + 1) * BW],
                                              bank[i][r0:r0 + HD, :]).then_inc(s["kq_ready"], 1)
                        for e in range(2):
                            for qt in range(ST):
                                u, w = e * ST + qt, (qt + 1) * P
                                dve.wait_ge(s["s_ps"], pq * (2 * ST) + (u + 1))
                                S = psum[:, 0:4, :].rearrange("p a b -> p (a b)")
                                ch.link(v.tensor_tensor(S[:, qt * P:w], S[:, qt * P:w], causal, ALU.add))
                                ch.link(v.reduce_max(rmax[:, u % 2, :], S[:, 0:w], AX.X))
                                v.tensor_scalar(nmax[:, u % 2, :], rmax[:, u % 2, :], -SCALE, None,
                                                ALU.mult).then_inc(s["m_ready"], 1)
                                if u:
                                    finish(s, p, pq, u - 1)
                        finish(s, p, pq, 2 * ST - 1)
                        ch.restart()
                    dve.sem_inc(s["pair_done"], 1)
                    with dve.Fori(0, ST) as t:
                        v.tensor_copy(otile, oall[:, t, :]).then_inc(s["otile_ready"], 1)
                        dve.wait_ge(s["y_ps"], q * ST + (t + 1))
                        xt = X[:, q * ST + t, :]
                        ch.link(v.tensor_tensor(xt, bank[7][:, 0:D], xt, ALU.add))
                        dve.sem_inc(s["y_added"], 1)
                        ch.restart()

            def finish(s, p, pq, u):
                e, qt = u // ST, u % ST
                dve.wait_ge(s["o_ps"], pq * (2 * ST) + (u + 1))
                ps = bank[6 + u % 2]
                ch.link(v.reciprocal(rden[:, u % 2, :], ps[:, HD:VC]))
                v.tensor_scalar(oall[:, qt, bass.ds(p * (2 * HD) + e * HD, HD)], ps[:, 0:HD], rden[:, u % 2, :], None,
                                ALU.mult).then_inc(s["o_read"], 1)

            v.memset(ones[:], 1.0).then_inc(const_ready, 1)
            begin(dve, 0)
            ternary(w1t.rearrange("p k f -> p (k f)"), 0, D * FF)
            ternary(w2t.rearrange("p k f -> p (k f)"), 1, D * FF)
            dve.sem_inc(const_ready, 1)
            ffn(sf, 0)
            end_phase()
            if STAGES > 1:
                linear_attention(sk)
                end_phase()
            if STAGES > 2:
                ffn(sf, 1)
                end_phase()
            if STAGES > 3:
                begin(dve, 3)
                experts(se, 0)
                end_phase()
            if STAGES > 4:
                begin(dve, 4)
                attention(sa)
                end_phase()
            if STAGES > 5:
                begin(dve, 5)
                experts(se, 1)
                end_phase()

        @block.scalar
        def _(act):
            a = nc.scalar

            def ffn(s, r):
                with act.Fori(0, NB) as b:
                    g = b + r * NB
                    act.wait_ge(s["xT_ps"], g + 1)
                    for k in range(KC):
                        a.copy(xT[:, k, :], bank[k]).then_inc(s["xT_ready"], 1)
                    for m in range(FC):
                        act.wait_ge(s["h_ps"], g * FC + (m + 1))
                        a.activation(h[:, m, :], bank[2 + m % 4], ACT.Relu,
                                     bias=b1c[:, m:m + 1]).then_inc(s["h_ready"], 1)

            def linear_attention(s):
                with act.Fori(0, SEQS) as q:
                    with act.Fori(0, SB) as b:
                        g = b + q * SB
                        act.wait_ge(s["xT_ps"], g + 1)
                        for k in range(KC):
                            a.copy(xT[:, k, :], bank[k]).then_inc(s["xT_ready"], 1)
                            a.copy(sT[:, k, bass.ds(b * BW, BW)], bank[k]).then_inc(s["xT_ready"], 1)
                        for m in range(KC):
                            act.wait_ge(s["kT_ps"], g * KC + (m + 1))
                            a.activation(kT[:, m, :], bank[2 + m], ACT.Identity,
                                         bias=bk0[:, m:m + 1]).then_inc(s["kT_ready"], 1)
                        for t in range(BLK):
                            act.wait_ge(s["emin_ready"], g * (2 * BLK) + 2 * (t + 1))
                            a.activation(efeat, emin, ACT.Exp).then_inc(s["e_ready"], 1)
                    with act.Fori(0, SB) as b:
                        g = b + q * SB
                        for m in range(KC):
                            act.wait_ge(s["q_ps"], g * KC + (m + 1))
                            a.activation(kT[:, m, :], bank[m], ACT.Identity,
                                         bias=bq0[:, m:m + 1]).then_inc(s["qT_ready"], 1)
                        for p in range(PAIRS):
                            act.wait_ge(s["qmin_ready"], g * PAIRS + (p + 1))
                            a.activation(efeat[:, p % 2, :], emin[:, p % 2, :], ACT.Exp).then_inc(s["qe_ready"], 1)
                        for t in range(BLK):
                            act.wait_ge(s["oT_ps"], g * BLK + (t + 1))
                            a.copy(oT0, bank[7][:, 0:D].rearrange("p (k t) -> p k t", k=KC)).then_inc(s["oT_ready"], 1)

            def expert_choice(s, g, j, c, k, i):
                n = g * BLK + j
                cnt = n + c * NT
                at = k * CH + i
                if at == 7:
                    act.wait_ge(s["xT_ps"], cnt + 1)
                    a.copy(xTe, bank[6][:, 0:D].rearrange("p (k t) -> p k t", k=KC)).then_inc(s["xT_ready"], 1)
                if at == 21:
                    act.wait_ge(s["qnT_ps"], cnt + 1)
                    a.copy(qnT, bank[6][:, 0:D].rearrange("p (k t) -> p k t", k=KC)).then_inc(s["qnT_ready"], 1)
                if at in (24, 25, CH + 3, CH + 4):
                    m = (24, 25, CH + 3, CH + 4).index(at)
                    act.wait_ge(s["s_ps"], cnt * 4 + (m + 1))
                    a.copy(scores[:, 8 * m:8 * m + 8, :], bank[6 + m % 2].rearrange("p (r n) -> p r n", r=8)).then_inc(
                        s["s_ready"], 1)
                if at == CHOSEN_AT + 1:
                    act.wait_ge(s["shift_ready"], cnt + 1)
                    a.activation(wexp, wexp, ACT.Exp).then_inc(s["w_ready"], 1)
                    act.wait_ge(s["sum_ready"], cnt + 1)
                    a.activation(wsum, wsum, ACT.Ln).then_inc(s["log_ready"], 1)

            def slots_copy(s, U, par):
                act.wait_ge(s["slots_ps"], U + 1)
                b16 = bank[5].bitcast(BF16)
                a.copy(dT[par], b16[0:NS * FT, 0:BW]).then_inc(s["slots_ready"], 1)
                a.copy(lT[par], b16[0:NS * HD, BW:2 * BW]).then_inc(s["slots_ready"], 1)

            def factors(s, U, par, ms):
                for m in ms:
                    act.wait_ge(s["e_ps"], U * (1 + NG) + (m + 1))
                    dst = E1[:, par, m - 1, :] if m else E2[par]
                    a.activation(dst, bank[F_BANK[m]], ACT.Exp).then_inc(s["e_ready"], 1)

            def outputs_copy(s, j, G):
                act.wait_ge(s["fold_ps"], G + 2)
                a.copy(oTe[:, j, :], bank[7][0:4 * HD, :]).then_inc(s["oT_ready"], 1)

            def expert_group(s, b, j, c, choose, first, last):
                G = (b * BLK + j) + c * NT
                for k in range(4):
                    U = G * 4 + k
                    for i in range(CH):
                        act.wait_ge(s["l_ps"], U * CH + (i + 1))
                        act.wait_ge(s["h_made"], U * CH + (i + 1))
                        a.activation(GE[:, i % RING, :], bank[i % 2], ACT.Gelu).then_inc(s["ge_ready"], 1)
                        if k == 0 and i == 5 and not first:
                            outputs_copy(s, j - 1, G - 1)
                        if choose:
                            expert_choice(s, b + 1, j, c, k, i)
                        if i == 15:
                            factors(s, U, k % 2, range(EARLY, 1 + NG))
                        if not (last and k == 3):
                            if i == 25:
                                slots_copy(s, U + 1, (k + 1) % 2)
                            if i == CH - 1:
                                factors(s, U + 1, (k + 1) % 2, range(EARLY))

            def experts(s, c):
                with act.Fori(0, BLK) as j:
                    for k in range(4):
                        for i in range(CH):
                            expert_choice(s, 0, j, c, k, i)
                slots_copy(s, c * UNITS, 0)
                factors(s, c * UNITS, 0, range(EARLY))
                with act.Fori(0, NB - 1) as b:
                    expert_group(s, b, 0, c, True, True, False)
                    with act.Fori(1, BLK) as j:
                        expert_group(s, b, j, c, True, False, False)
                    outputs_copy(s, BLK - 1, b * BLK + (c * NT + BLK - 1))
                expert_group(s, NB - 1, 0, c, False, True, False)
                with act.Fori(1, BLK - 1) as j:
                    expert_group(s, NB - 1, j, c, False, False, False)
                expert_group(s, NB - 1, BLK - 1, c, False, False, True)
                outputs_copy(s, BLK - 1, c * NT + NT - 1)

            def attention(s):
                with act.Fori(0, SEQS) as q:
                    with act.Fori(0, SB) as b:
                        g = b + q * SB
                        cols = bass.ds(b * BW, BW)
                        act.wait_ge(s["xT_ps"], g + 1)
                        for k in range(KC):
                            a.copy(sT1[:, k, cols], bank[k]).then_inc(s["xT_ready"], 1)
                        act.wait_ge(s["c_ps"], g + 1)
                        a.copy(cb, bank[2]).then_inc(s["c_ready"], 1)
                        a.copy(cT[:, cols], bank[2]).then_inc(s["c_ready"], 1)
                        act.wait_ge(s["r_ready"], g * 2 + 2)
                        for to in (KA, QA):
                            a.copy(to[64:64 + DR, cols], to[0:DR, cols]).then_inc(s["rope_copied"], 1)
                    with act.Fori(0, PAIRS) as p:
                        pq = p + q * PAIRS
                        for e in range(2):
                            for qt in range(ST):
                                u, w = e * ST + qt, (qt + 1) * P
                                act.wait_ge(s["m_ready"], pq * (2 * ST) + (u + 1))
                                S = psum[:, 0:4, :].rearrange("p a b -> p (a b)")
                                a.activation(probs[:, 0:w], S[:, 0:w], ACT.Exp, bias=nmax[:, u % 2, :],
                                             scale=SCALE).then_inc(s["p_ready"], 1)
                                for g in range((qt + BLK) // BLK):
                                    gw = min(BLK, qt + 1 - g * BLK) * P
                                    act.wait_ge(s["pt_ps"], pq * (2 * PTN) + (PT_AT[u] + g + 1))
                                    a.copy(PT[:, g * BW:g * BW + gw],
                                           bank[4 + (PT_AT[u] + g) % 2][:, 0:gw]).then_inc(s["pt_ready"], 1)
                    with act.Fori(0, ST) as t:
                        act.wait_ge(s["ot_ps"], q * ST + (t + 1))
                        a.copy(oT1, bank[6][:, 0:D].rearrange("p (k t) -> p k t", k=KC)).then_inc(s["ot_ready"], 1)

            begin(act, 0)
            act.wait_ge(const_ready, 2)
            ffn(sf, 0)
            if STAGES > 1:
                begin(act, 1)
                linear_attention(sk)
            if STAGES > 2:
                begin(act, 2)
                ffn(sf, 1)
            if STAGES > 3:
                begin(act, 3)
                experts(se, 0)
            if STAGES > 4:
                begin(act, 4)
                attention(sa)
            if STAGES > 5:
                begin(act, 5)
                experts(se, 1)

        @block.tensor
        def _(pe):
            t_ = nc.tensor
            def transpose_block(s, b):
                pe.wait_ge(s["xn_ready"], b * BLK + BLK)
                for k in range(KC):
                    for t in range(BLK):
                        mm = t_.transpose(bank[k][:, t * P:(t + 1) * P], xn[:, t, k * P:(k + 1) * P], ident[:])
                mm.then_inc(s["xT_ps"], 1)

            def project(dst, lhs, rhs):
                for k in range(KC):
                    mm = t_.matmul(dst, lhs(k), rhs(k), start=(k == 0), stop=(k == KC - 1))
                return mm

            def project_bias(dst, lhs, rhs, row):
                for k in range(KC):
                    t_.matmul(dst, lhs(k), rhs(k), start=(k == 0), stop=False)
                return t_.matmul(dst, ones[0:1, :], row, start=False, stop=True)

            def turn(dst, src):
                for k in range(KC):
                    mm = t_.transpose(dst[:, k * P:(k + 1) * P], src[:, k * P:(k + 1) * P], ident[:])
                return mm

            def ffn(s, r):
                with pe.Fori(0, NB) as b:
                    g = b + r * NB
                    transpose_block(s, g)
                    pe.wait_ge(s["xT_ready"], g * KC + KC)
                    for m in range(FC):
                        if m >= 4:
                            pe.wait_ge(s["h_ready"], g * FC + (m - 3))
                        project(bank[2 + m % 4], lambda k: w1t[:, k, m * P:(m + 1) * P],
                                lambda k: xT[:, k, :]).then_inc(s["h_ps"], 1)
                    pe.wait_ge(s["h_ready"], g * FC + FC)
                    for t in range(BLK):
                        ps = bank[6 + t // 2][:, (t % 2) * D:(t % 2 + 1) * D]
                        for m in range(FC):
                            t_.matmul(ps, h[:, m, t * P:(t + 1) * P], w2t[:, m, :], start=(m == 0), stop=False)
                        t_.matmul(ps, ones[0:1, :], b2r, start=False, stop=True).then_inc(s["out_ps"], 1)

            def linear_attention(s):
                with pe.Fori(0, SEQS) as q:
                    with pe.Fori(0, SB) as b:
                        g = b + q * SB
                        transpose_block(s, g)
                        pe.wait_ge(s["xT_ready"], g * (2 * KC) + 2 * KC)
                        for m in range(KC):
                            project(bank[2 + m], lambda k: wk0[:, k, m * P:(m + 1) * P],
                                    lambda k: xT[:, k, :]).then_inc(s["kT_ps"], 1)
                        pe.wait_ge(s["kT_ready"], g * KC + KC)
                        for t in range(BLK + 1):
                            if t:
                                pe.wait_ge(s["kf_ready"], g * (3 * BLK) + 3 * t)
                            if t < BLK:
                                for m in range(KC):
                                    t_.matmul(bank[4 + m], kT[:, m, t * P:(t + 1) * P], rm, start=True, stop=True)
                                project_bias(bank[6][:, 0:D], lambda k: xT[:, k, t * P:(t + 1) * P],
                                             lambda k: wv0[:, k, :], bv0).then_inc(s["kf_ps"], 1)
                            if t:
                                u = t - 1
                                for p in range(PAIRS):
                                    mm = t_.matmul(bank[7][:, p * 2 * VC:(p + 1) * 2 * VC],
                                                   kf[:, u % 2, p * P:(p + 1) * P],
                                                   vext[:, u % 2, 2 * p:2 * p + 2, :].rearrange("p h c -> p (h c)"),
                                                   start=(u == 0 and p == 0), stop=(u == BLK - 1),
                                                   skip_group_check=True)
                                mm.then_inc(s["kv_ps"], 1)
                    with pe.Fori(0, SB) as b:
                        g = b + q * SB
                        pe.wait_ge(s["kv_done"], q + 1)
                        for m in range(KC):
                            project(bank[m], lambda k: wq0[:, k, m * P:(m + 1) * P],
                                    lambda k: sT[:, k, bass.ds(b * BW, BW)]).then_inc(s["q_ps"], 1)
                        pe.wait_ge(s["qT_ready"], g * KC + KC)
                        for p in range(PAIRS):
                            if p >= 4:
                                pe.wait_ge(s["qf_ready"], g * PAIRS + (p - 3))
                            t_.matmul(bank[2 + p % 4], rm[:, (p % 4) * P:(p % 4 + 1) * P], kT[:, p // 4, :],
                                      start=True, stop=True).then_inc(s["qf_ps"], 1)
                        pe.wait_ge(s["qf_ready"], g * PAIRS + PAIRS)
                        for t in range(BLK + 1):
                            if t:
                                pe.wait_ge(s["o_ready"], g * BLK + t)
                            if t < BLK:
                                for p in range(PAIRS):
                                    mm = t_.matmul(bank[6][:, p * 2 * VC:(p + 1) * 2 * VC], qf[:, p, t * P:(t + 1) * P],
                                                   kv[:, p, :], start=True, stop=True)
                                mm.then_inc(s["o_ps"], 1)
                            if t:
                                u = t - 1
                                if u:
                                    pe.wait_ge(s["y_added"], g * BLK + u)
                                turn(bank[7], o0).then_inc(s["oT_ps"], 1)
                                pe.wait_ge(s["oT_ready"], g * BLK + t)
                                project_bias(bank[7][:, D:2 * D], lambda k: oT0[:, k, :], lambda k: wo0[:, k, :],
                                             bo0).then_inc(s["y_ps"], 1)
                    pe.wait_ge(s["y_added"], q * ST + ST)

            def expert_choice(s, g, j, c, k, i):
                cnt = (g * BLK + j) + c * NT
                at = k * CH + i
                if at == 5:
                    pe.wait_ge(s["xn_ready"], cnt + 1)
                    turn(bank[6], xne[:, 0, :]).then_inc(s["xT_ps"], 1)
                if at == 8:
                    pe.wait_ge(s["xT_ready"], cnt + 1)
                    pe.wait_ge(s["oT_ready"], cnt + 1)
                    project(bank[7][:, 0:D], lambda k: xTe[:, k, :], lambda k: wqe[:, k, :]).then_inc(s["q_ps"], 1)
                if at == 19:
                    pe.wait_ge(s["qn_ready"], cnt + 1)
                    turn(bank[6], qc.rearrange("p h d -> p (h d)")).then_inc(s["qnT_ps"], 1)
                if at in (22, 23, CH + 1, CH + 2):
                    m = (22, 23, CH + 1, CH + 2).index(at)
                    if m == 0:
                        pe.wait_ge(s["qnT_ready"], cnt + 1)
                    if m == 2:
                        pe.wait_ge(s["s_ready"], cnt * 4 + 2)
                    t_.matmul(bank[6 + m % 2], qnT[:, m // 2, :], keys[:, (m % 2) * BW:(m % 2 + 1) * BW],
                              start=True, stop=True).then_inc(s["s_ps"], 1)
                if at in (25, CH + 5):
                    pe.wait_ge(s["s_ready"], cnt * 4 + (2 if at == 25 else 4))

            def slots_turn(s, U, first):
                pe.wait_ge(s["split_ready"], U + 1)
                if not first:
                    pe.wait_ge(s["e_ready"], U * (1 + NG))
                b16 = bank[5].bitcast(BF16)
                for t in range(BLK):
                    t_.transpose(b16[0:NS * FT, t * P:(t + 1) * P], slotd[:, t, :, :].rearrange("p s f -> p (s f)"),
                                 identb)
                for t in range(BLK):
                    mm = t_.transpose(b16[0:NS * HD, BW + t * P:BW + (t + 1) * P],
                                      slotl[:, t, :, :].rearrange("p s f -> p (s f)"), identb)
                mm.then_inc(s["slots_ps"], 1)

            def shifted_scores(s, U, par, m):
                if m == 0:
                    pe.wait_ge(s["slots_ready"], 2 * U + 2)
                if F_BANK[m] in F_BANK[:m]:
                    before = max(x for x in range(m) if F_BANK[x] == F_BANK[m])
                    pe.wait_ge(s["e_ready"], U * (1 + NG) + (before + 1))
                t_.matmul(bank[F_BANK[m]], pairk[:, NE + m * P:NE + (m + 1) * P], dT[par],
                          start=True, stop=True).then_inc(s["e_ps"], 1)

            def chunk_down(s, U, par, i):
                if i == 0:
                    pe.wait_ge(s["slots_ready"], 2 * U + 2)
                pe.wait_ge(s["ge_ready"], U * CH + (i + 1))
                t_.matmul(bank[i % 2], down[:, i * P:(i + 1) * P], lT[par], start=True, stop=True).then_inc(s["l_ps"], 1)
                pe.wait_ge(s["gm_ready"], U * CH + (i + 1))
                t_.matmul(bank[2 + i % 2], pairk[:, i * P:(i + 1) * P], dT[par],
                          start=True, stop=True).then_inc(s["d_ps"], 1)

            def chunk_up(s, U, i):
                pe.wait_ge(s["h_made"], U * CH + (RING + i + 1))
                if i % YG == 0:
                    pe.wait_ge(s["y_weighed"], U * NG + (i // YG + 1))
                q = i % YG * CR * HD
                t_.matmul(bank[4][q:q + CR * HD, :], upw[:, i, :], HH[:, i % RING, :],
                          start=True, stop=True).then_inc(s["up_ps"], 1)

            def fold_group(s, G):
                pe.wait_ge(s["acc_ready"], G + 1)
                for k in range(4):
                    mm = t_.matmul(bank[7][0:4 * HD, :], fold[:, k, :], acc[:, k, :], start=(k == 0), stop=(k == 3))
                mm.then_inc(s["fold_ps"], 1)

            def expert_group(s, b, j, c, choose, first, ends, last):
                G = (b * BLK + j) + c * NT
                for k in range(4):
                    U = G * 4 + k
                    more = not (last and k == 3)
                    pe.wait_ge(s["e_ready"], U * (1 + NG) + EARLY)
                    for i in range(CH):
                        if k == 0 and i == 4 and not first:
                            fold_group(s, G - 1)
                        if i + AHEAD < CH:
                            chunk_down(s, U, k % 2, i + AHEAD)
                        elif more and not (ends and k == 3 and i + AHEAD - CH >= 2):
                            chunk_down(s, U + 1, (k + 1) % 2, i + AHEAD - CH)
                        chunk_up(s, U, i)
                        if choose:
                            expert_choice(s, b + 1, j, c, k, i)
                        if i in (10, 13):
                            for m in (5, 6, 7) if i == 10 else (8,):
                                shifted_scores(s, U, k % 2, m)
                        if i == 18:
                            pe.wait_ge(s["e_ready"], (U + 1) * (1 + NG))
                        if more and i == 23:
                            slots_turn(s, U + 1, False)
                        if more and i == 26:
                            for m in range(3):
                                shifted_scores(s, U + 1, (k + 1) % 2, m)
                        if more and i == 29:
                            for m in range(3, EARLY):
                                shifted_scores(s, U + 1, (k + 1) % 2, m)
                if ends:
                    if not last:
                        pe.wait_ge(s["e_ready"], (U + 1) * (1 + NG) + EARLY)
                    fold_group(s, G)

            def second_pair(s, U):
                for i in range(2, AHEAD):
                    chunk_down(s, U, 0, i)

            def expert_out(s, b, c):
                pe.wait_ge(s["oT_ready"], b * BLK + (c * NT + 2 * BLK + 1))
                for t in range(BLK):
                    n = (b * BLK + t) + c * NT
                    if t:
                        pe.wait_ge(s["y_added"], n)
                    for j in range(BLK):
                        mm = t_.matmul(bank[7][:, (t % 2) * D:(t % 2 + 1) * D], oTe[:, j, t * P:(t + 1) * P],
                                       woute[:, j, :], start=(j == 0), stop=(j == BLK - 1))
                    mm.then_inc(s["y_ps"], 1)
                pe.wait_ge(s["y_added"], b * BLK + (c * NT + BLK))

            def experts(s, c):
                if c == 0:
                    pe.sem_inc(s["ge_ready"], 2)
                    pe.sem_inc(s["gm_ready"], 2)
                    pe.sem_inc(s["y_weighed"], 1)
                    pe.sem_inc(s["oT_ready"], BLK + 1)
                    pe.sem_inc(s["fold_ps"], 1)
                with pe.Fori(0, BLK) as j:
                    for k in range(4):
                        for i in range(CH):
                            expert_choice(s, 0, j, c, k, i)
                pe.wait_ge(s["tables_ready"], c + 1)
                slots_turn(s, c * UNITS, c == 0)
                for m in range(EARLY):
                    shifted_scores(s, c * UNITS, 0, m)
                for i in range(AHEAD):
                    chunk_down(s, c * UNITS, 0, i)
                with pe.Fori(0, NB - 1) as b:
                    expert_group(s, b, 0, c, True, True, False, False)
                    with pe.Fori(1, BLK - 1) as j:
                        expert_group(s, b, j, c, True, False, False, False)
                    expert_group(s, b, BLK - 1, c, True, False, True, False)
                    expert_out(s, b, c)
                    second_pair(s, b * H + (c * UNITS + H))
                expert_group(s, NB - 1, 0, c, False, True, False, False)
                with pe.Fori(1, BLK - 1) as j:
                    expert_group(s, NB - 1, j, c, False, False, False, False)
                expert_group(s, NB - 1, BLK - 1, c, False, False, True, True)
                expert_out(s, NB - 1, c)

            def attention(s):
                with pe.Fori(0, SEQS) as q:
                    with pe.Fori(0, SB) as b:
                        g = b + q * SB
                        cols = bass.ds(b * BW, BW)
                        transpose_block(s, g)
                        pe.wait_ge(s["xT_ready"], g * KC + KC)
                        project(bank[2], lambda k: wkvd[:, k, :], lambda k: sT1[:, k, cols]).then_inc(s["c_ps"], 1)
                        pe.wait_ge(s["c_ready"], g * 2 + 2)
                        t_.matmul(bank[3][0:DR, :], wkr, cb, start=True, stop=True)
                        t_.matmul(bank[4][0:DR, :], wkrs, cb, start=True, stop=True).then_inc(s["r_ps"], 1)
                        project(bank[5][0:DR, :], lambda k: wqr[:, k, :], lambda k: sT1[:, k, cols])
                        project(bank[6][0:DR, :], lambda k: wqrs[:, k, :],
                                lambda k: sT1[:, k, cols]).then_inc(s["r_ps"], 1)
                        for t in range(BLK):
                            mm = t_.matmul(bank[t // 2][:, (t % 2) * D:(t % 2 + 1) * D],
                                           cb[:, t * P:(t + 1) * P], wvup, start=True, stop=True)
                            if t % 2:
                                mm.then_inc(s["v_ps"], 1)
                        pe.wait_ge(s["v_ready"], g * BLK + BLK)
                    with pe.Fori(0, PAIRS) as p:
                        pq = p + q * PAIRS
                        pe.wait_ge(s["rope_copied"], q * (2 * SB) + 2 * SB)
                        pe.wait_ge(s["wpair_ready"], pq * (1 + KC) + (1 + KC))
                        for i in range(8):
                            j = i % 4
                            if i < 4:
                                mm = t_.matmul(bank[i], wpair[:, 0, :], cT[:, j * BW:(j + 1) * BW], start=True, stop=True)
                            else:
                                mm = project(bank[i], lambda k: wpair[:, 1 + k, :],
                                             lambda k: sT1[:, k, j * BW:(j + 1) * BW])
                            mm.then_inc(s["kq_ps"], 1)
                        pe.wait_ge(s["kq_ready"], pq * 16 + 16)
                        for u in range(2 * ST + 1):
                            if u < 2 * ST:
                                e, qt = u // ST, u % ST
                                if u:
                                    pe.wait_ge(s["p_ready"], pq * (2 * ST) + u)
                                rows = slice(64 * e, 64 * e + DR + HD)
                                for j in range((qt + BLK) // BLK):
                                    w = min(BLK, qt + 1 - j * BLK) * P
                                    mm = t_.matmul(bank[j][:, 0:w], QA[rows, qt * P:(qt + 1) * P],
                                                   KA[rows, j * BW:j * BW + w], start=True, stop=True)
                                mm.then_inc(s["s_ps"], 1)
                            if u:
                                values(s, p, pq, u - 1)
                        pe.wait_ge(s["o_read"], pq * (2 * ST) + 2 * ST)
                    with pe.Fori(0, ST) as t:
                        pe.wait_ge(s["pair_done"], q + 1)
                        pe.wait_ge(s["otile_ready"], q * ST + (t + 1))
                        turn(bank[6], otile).then_inc(s["ot_ps"], 1)
                        pe.wait_ge(s["ot_ready"], q * ST + (t + 1))
                        project(bank[7][:, 0:D], lambda k: oT1[:, k, :], lambda k: wo1[:, k, :]).then_inc(s["y_ps"], 1)
                        pe.wait_ge(s["y_added"], q * ST + (t + 1))
            def values(s, p, pq, u):
                e, qt = u // ST, u % ST
                pe.wait_ge(s["p_ready"], pq * (2 * ST) + (u + 1))
                for g in range((qt + BLK) // BLK):
                    n = min(BLK, qt + 1 - g * BLK)
                    if PT_AT[u] + g >= 2:
                        pe.wait_ge(s["pt_ready"], pq * (2 * PTN) + (PT_AT[u] + g - 1))
                    for i in range(n):
                        kt = g * BLK + i
                        mm = t_.transpose(bank[4 + (PT_AT[u] + g) % 2][:, i * P:(i + 1) * P],
                                          probs[:, kt * P:(kt + 1) * P], ident[:])
                    mm.then_inc(s["pt_ps"], 1)
                if u >= 2:
                    pe.wait_ge(s["o_read"], pq * (2 * ST) + (u - 1))
                for g in range((qt + BLK) // BLK):
                    pe.wait_ge(s["pt_ready"], pq * (2 * PTN) + (PT_AT[u] + g + 1))
                    for i in range(min(BLK, qt + 1 - g * BLK)):
                        kt = g * BLK + i
                        vh = vall[:, kt, :, :].rearrange("p h c -> p (h c)")[:, bass.ds(p * (2 * VC) + e * VC, VC)]
                        mm = t_.matmul(bank[6 + u % 2][:, 0:VC], PT[:, kt * P:(kt + 1) * P], vh,
                                       start=(kt == 0), stop=(kt == qt))
                mm.then_inc(s["o_ps"], 1)

            pe.wait_ge(const_ready, 1)
            for c in range(2):
                pe.wait_ge(gsum_ready, c + 1)
                t_.matmul(bank[0][:, c:c + 1], ones[:], gsum[:, c:c + 1],
                          start=True, stop=True).then_inc(gamma_ready, 1)
            begin(pe, 0)
            pe.wait_ge(const_ready, 2)
            ffn(sf, 0)
            if STAGES > 1:
                begin(pe, 1)
                linear_attention(sk)
            if STAGES > 2:
                begin(pe, 2)
                ffn(sf, 1)
            if STAGES > 3:
                begin(pe, 3)
                experts(se, 0)
            if STAGES > 4:
                begin(pe, 4)
                attention(sa)
            if STAGES > 5:
                begin(pe, 5)
                experts(se, 1)

        @block.gpsimd
        def _(pool):
            ch = Chain(pool, pool_chain)
            g_ = nc.gpsimd

            def split_step(s, U, step, first):
                f = F[:, :, U % (2 * H), :]
                if step == 0:
                    if not first:
                        pool.wait_ge(s["slots_ps"], U)
                    ch.mark(g_.tensor_copy(part1, f))
                if step == 1:
                    ch.sync()
                    ch.mark(g_.tensor_tensor(split, f, part1, ALU.subtract))
                if step == 2:
                    ch.mark(g_.tensor_copy(slotd[:, :, 0:3, :],
                                           part1[:, :, None, 0:FT].to_broadcast([P, BLK, 3, FT])))
                if step == 3:
                    ch.mark(g_.tensor_copy(slotl[:, :, 0:3, :],
                                           part1[:, :, None, FT:NF].to_broadcast([P, BLK, 3, HD])))
                    ch.sync()
                if step == 4:
                    ch.mark(g_.tensor_copy(part2, split))
                if step == 5:
                    ch.sync()
                    ch.mark(g_.tensor_copy(slotd[:, :, 3:5, :],
                                           part2[:, :, None, 0:FT].to_broadcast([P, BLK, 2, FT])))
                if step == 6:
                    ch.mark(g_.tensor_copy(slotl[:, :, 3:5, :],
                                           part2[:, :, None, FT:NF].to_broadcast([P, BLK, 2, HD])))
                if step == 7:
                    ch.mark(g_.tensor_tensor(slotd[:, :, 5, :], split[:, :, 0:FT], part2[:, :, 0:FT], ALU.subtract))
                if step == 8:
                    ch.mark(g_.tensor_tensor(slotl[:, :, 5, :], split[:, :, FT:NF], part2[:, :, FT:NF], ALU.subtract))
                    ch.sync()
                    pool.sem_inc(s["split_ready"], 1)

            def expert_group(s, b, j, c, choose, last):
                for k in range(4):
                    U = (b * H + j * 4) + (c * UNITS + k)
                    for i in range(CH):
                        pool.wait_ge(s["ge_ready"], U * CH + (2 + i + 1))
                        pool.wait_ge(s["gm_ready"], U * CH + (2 + i + 1))
                        pool.wait_ge(s["up_ps"], U * CH + (i + 1))
                        g_.tensor_tensor(HH[:, i % RING, :], GE[:, i % RING, :], GM[:, i % RING, :],
                                         ALU.mult).then_inc(s["h_made"], 1)
                        if SPLIT_AT <= i < SPLIT_AT + 9 and not (last and k == 3):
                            if choose and k == 3 and i == SPLIT_AT:
                                pool.wait_ge(s["f_ready"], (b * BLK + j) + (c * NT + BLK + 1))
                            split_step(s, U + 1, i - SPLIT_AT, False)
                ch.restart()

            def experts(s, c):
                if c == 0:
                    pool.sem_inc(s["up_ps"], RING)
                pool.wait_ge(s["f_ready"], c * NT + BLK)
                for step in range(9):
                    split_step(s, c * UNITS, step, c == 0)
                ch.restart()
                with pool.Fori(0, NB - 1) as b:
                    with pool.Fori(0, BLK) as j:
                        expert_group(s, b, j, c, True, False)
                with pool.Fori(0, BLK - 1) as j:
                    expert_group(s, NB - 1, j, c, False, False)
                expert_group(s, NB - 1, BLK - 1, c, False, True)

            if STAGES > 3:
                begin(pool, 3)
                experts(se, 0)
            if STAGES > 5:
                begin(pool, 5)
                experts(se, 1)


def _pad_pairs(w):
    out = np.zeros((w.shape[0], PAIRS, P), w.dtype)
    w = w.reshape(w.shape[0], PAIRS, 2, HD)
    out[:, :, DR:DR + HD] = w[:, :, 0]
    out[:, :, 64 + DR:64 + DR + HD] = w[:, :, 1]
    return out


def _block_diagonal(w, copies):
    out = np.zeros((copies * w.shape[0], copies * w.shape[1]), w.dtype)
    for i in range(copies):
        out[i * w.shape[0]:(i + 1) * w.shape[0], i * w.shape[1]:(i + 1) * w.shape[1]] = w
    return out


def kernel(**inputs):
    import concourse.bacc as bacc
    from concourse.bass_utils import run_bass_kernel_spmd as run

    nc = bacc.Bacc("TRN2", target_bir_lowering=False, num_devices=1)
    i = {k: np.asarray(a) for k, a in inputs.items()}
    f = np.float32
    half = DR // 2
    inv_freq = (f(1.0) / np.power(f(10000.0), np.arange(0, DR, 2, dtype=f) / f(DR))).astype(f)
    freqs = np.outer(np.arange(SL, dtype=f), inv_freq).astype(f)
    cos, sin = np.cos(freqs).T, np.sin(freqs).T
    swap = np.r_[half:DR, 0:half]
    both = np.zeros((HD, 2 * NK), f)
    both[:HD // 2, :NK] = i["L1_ffn_c_keys"].T
    both[HD // 2:, NK:] = i["L1_ffn_c_prime_keys"].T
    down = np.tile(i["L1_ffn_w_down"][:NE].T, (NS, 1))
    c1, c2 = i["L1_ffn_c_keys"].T, i["L1_ffn_c_prime_keys"].T
    pairk = np.zeros((FT, NW), f)
    pairk[0:HD // 2, :NE] = np.repeat(c1, NK, axis=1)
    pairk[HD // 2:HD, :NE + P] = np.tile(c2, (1, NK + CR))
    pairk[0:HD // 2, NE + P:] = np.repeat(c1, HD, axis=1)
    pairk[HD, :NE] = -1
    pairk[HD + 1, NE:NE + P] = -1
    pairk[HD + 2, NE + P:] = -1
    fold = np.zeros((P // HD, HD, 4, 4, HD), f)
    for k in range(4):
        fold[:, :, k, k] = np.eye(HD, dtype=f)
    upw = np.zeros((P, CH, CR, HD), f)
    for r in range(CR):
        upw[r * NK:(r + 1) * NK, :, r] = i["L1_ffn_w_up"][:NE].reshape(CH, CR, NK, HD)[:, r].transpose(1, 0, 2)
    part = np.array(W_PARTS)[:, None] == np.arange(3)[None, :]
    laid = {
        "x": i["L0_attn_x"].reshape(T, D), "ident": np.eye(P, dtype=f),
        "w1t": i["L0_ffn_W1"].T, "b1": i["L0_ffn_b1"].reshape(FC, P).T,
        "w2t": i["L0_ffn_W2"].T, "b2": i["L0_ffn_b2"].reshape(1, D),
        "wq0": i["L0_attn_Wq"], "wk0": i["L0_attn_Wk"], "wv0": i["L0_attn_Wv"], "wo0": i["L0_attn_Wo"],
        "bq0": i["L0_attn_bq"].reshape(KC, P).T, "bk0": i["L0_attn_bk"].reshape(KC, P).T,
        "bv0": i["L0_attn_bv"].reshape(1, D), "bo0": i["L0_attn_bo"].reshape(1, D),
        "rm": _block_diagonal(i["L0_attn_random_matrix"], HK),
        "wqe": i["L1_ffn_Wq"], "woute": i["L1_ffn_Wout"], "keys": _block_diagonal(both, HK),
        "lng": i["L1_ffn_ln_g"], "lnb": i["L1_ffn_ln_b"], "down": down, "pairk": np.tile(pairk, (NS, 1)),
        "upw": upw.reshape(P, CH, CR * HD), "fold": fold.reshape(P, 4, 4 * HD),
        "partl": np.repeat(part, HD, axis=0).astype(f), "partd": np.repeat(part, FT, axis=0).astype(f),
        "wkvd": i["L1_attn_W_kv_down"], "wkup": _pad_pairs(i["L1_attn_W_k_up"]), "wqp": _pad_pairs(i["L1_attn_W_q"]),
        "wvup": i["L1_attn_W_v_up"], "wqr": i["L1_attn_W_q_rope"], "wqrs": i["L1_attn_W_q_rope"][:, swap],
        "wkr": i["L1_attn_W_k_rope"], "wkrs": i["L1_attn_W_k_rope"][:, swap], "wo1": i["L1_attn_W_o"],
        "cos": np.concatenate([cos, cos]), "sin": np.concatenate([-sin, sin]),
        "causal": np.where(np.arange(P)[None, :] > np.arange(P)[:, None], f(LOWEST), f(0)).astype(f),
    }
    arrays, ins = {}, {}
    for name, a in laid.items():
        a = np.ascontiguousarray(a)
        arrays[f"in_{name}"] = a
        ins[name] = nc.dram_tensor(f"in_{name}", a.shape, mybir.dt.from_np(a.dtype), kind="ExternalInput").ap()
    out = nc.dram_tensor("out_x", (T, D), F32, kind="ExternalOutput").ap()
    macaron(nc, ins, out)
    r = run(nc, [arrays], core_ids=[0])
    return r.results[0]["out_x"].reshape(SEQS, SL, D)
```

```python
import numpy as np
import concourse.bass as bass
from concourse import mybir
from concourse.alu_op_type import AluOpType as ALU
from contextlib import ExitStack

F32 = mybir.dt.float32
I32 = mybir.dt.int32
BF16 = mybir.dt.bfloat16
ACT = mybir.ActivationFunctionType
AX = mybir.AxisListType

P = 128
SEQS = 2
T = 4096
NT = T // P
ST = NT // SEQS
SL = T // SEQS
BLK = 4
BW = BLK * P
NB = NT // BLK
SB = ST // BLK
D = 256
KC = D // P
FF = 1024
FC = FF // P
EPS = 1e-5
H = 16
HD = D // H
PAIRS = H // 2
HK = P // HD
M0 = 64
VC = HD + 1
DR = 32
DC = 128
SCALE = float(1.0 / np.sqrt(HD + DR))
NK = 64
TOP = 16
TOP1 = 24
SEGS = [(0, 1, 17, 0), (1, 1, 8, 17), (2, 1, 5, 25), (3, 1, 4, 30), (4, 1, 3, 34), (5, 3, 2, 37), (8, 9, 1, 43)]
NJ = 52
NE = NK * NK
CH = NE // P
CR = P // NK
YG = P // (CR * HD)
NG = CH // YG
NW = NE + P + NG * P
W_PARTS = [0, 1, 2, 0, 1, 0]
NS = len(W_PARTS)
FT = HD + 3
NF = FT + HD
SLOTS = 8
RING = 4
AHEAD = 5
LISTS_AT = 27
CHOSEN_AT = LISTS_AT + 77
LARGEST_AT = [0, 1, 3, 4, 6]
SPLIT_AT = CHOSEN_AT % CH + 5
EARLY = 5
F_BANK = [5, 6, 7, 5, 6, 7, 5, 6, 7]
UNITS = NB * H
LOWEST = -3.0e38
HALF = 8
CHUNKS = [(e, qt, k0, min(HALF, qt + 1 - k0)) for e in range(2) for qt in range(ST) for k0 in range(0, qt + 1, HALF)]
CN = len(CHUNKS)
GROUPS = [(nt + BLK - 1) // BLK for _, _, _, nt in CHUNKS]
PT_AT = [sum(GROUPS[:x]) for x in range(CN)]
PTN = sum(GROUPS)
MERGED = [x for x in range(CN) if CHUNKS[x][2]]
MN = len(MERGED)
STAGES = 6


class Chain:

    def __init__(self, eng, sem):
        self.eng, self.sem, self.n = eng, sem, 0

    def mark(self, ins):
        ins.then_inc(self.sem, 1)
        self.n += 1

    def sync(self):
        self.eng.wait_ge(self.sem, self.n)

    def link(self, ins):
        self.mark(ins)
        self.sync()

    def restart(self):
        self.sync()
        self.eng.sem_clear(self.sem)
        self.n = 0


class Arena:

    def __init__(self, tensor, words):
        self.tensor, self.words, self.at = tensor, words, 0

    def reset(self):
        self.at = 0

    def take(self, *shape, parts=P, dt=F32):
        n = int(np.prod(shape))
        assert self.at + n <= self.words, (self.at, n, self.words)
        v = self.tensor[0:parts, self.at:self.at + n]
        self.at += n
        if dt is not F32:
            v = v.bitcast(dt)
        if len(shape) == 2:
            v = v.rearrange("p (a b) -> p a b", a=shape[0])
        elif len(shape) == 3:
            v = v.rearrange("p (a b c) -> p a b c", a=shape[0], b=shape[1])
        return v


def macaron(nc, ins, out):
    ctx = ExitStack()
    with ctx:
        def sb(name, shape, dt=F32):
            return ctx.enter_context(nc.sbuf_tensor(name, shape, dt))

        def sem(name):
            return ctx.enter_context(nc.semaphore(name))

        def sems(prefix, names):
            return {n: sem(f"{prefix}_{n}") for n in names.split()}

        psum = ctx.enter_context(nc.psum_tensor("psum", [P, 8, 512], F32))
        bank = [psum[:, i, :] for i in range(8)]

        X = sb("X", [P, NT, D])
        ident = sb("ident", [P, P])
        ones = sb("ones", [P, P])
        stats = sb("stats", [P, BLK, 6])
        mv = sb("mv", [P, BLK, 2])
        var = sb("var", [P, BLK])
        rstd = sb("rstd", [P, BLK])
        newton = sb("newton", [P, BLK])
        xn = sb("xn", [P, BLK, D])
        xT = sb("xT", [P, KC, BW])
        WORDS = 42000
        arena = Arena(sb("arena", [P, WORDS]), WORDS)

        w1t = arena.take(KC, FF)
        w2t = arena.take(FC, D)
        b1c = arena.take(FC)
        b2r = arena.take(D, parts=1)
        gsum = arena.take(2)
        thr = arena.take(4)
        wq0, wk0, wv0, wo0 = [arena.take(KC, D) for _ in range(4)]
        bq0, bk0 = arena.take(KC), arena.take(KC)
        bv0, bo0 = arena.take(D, parts=1), arena.take(D, parts=1)
        rm = arena.take(HK * M0)
        kv = arena.take(PAIRS, 2 * VC)
        vext = arena.take(2, H, VC)
        h = arena.take(FC, BW)
        wtmp = h.rearrange("p a b -> p (a b)")
        sT = arena.take(KC, SL)
        kT = arena.take(KC, BW)
        emin = arena.take(2, BW)
        efeat = arena.take(2, BW)
        kf = arena.take(2, PAIRS * P)
        o0 = arena.take(D)
        oT0 = arena.take(KC, P)
        nrm = arena.take(H)
        rnrm = arena.take(H)
        qf = h

        arena.reset()
        wqe = arena.take(KC, D)
        woute = arena.take(BLK, D, parts=4 * HD)
        keys = arena.take(HK * 2 * NK)
        lng = arena.take(HD)
        lnb = arena.take(HD)
        upw = arena.take(CH, CR * HD)
        fold = arena.take(4, 4 * HD)
        identb = arena.take(P // 2, dt=BF16)
        partl = arena.take(3, parts=NS * HD)
        partd = arena.take(3, parts=NS * FT)
        down = arena.take(NE // 2, parts=NS * HD, dt=BF16)
        pairk = arena.take(NW // 2, parts=NS * FT, dt=BF16)
        xne = arena.take(1, D)
        xTe = arena.take(KC, P)
        qc = arena.take(H, HD)
        qsq = arena.take(H, HD)
        hmean = arena.take(H)
        hvar = arena.take(H)
        hrstd = arena.take(H)
        hnewton = arena.take(H)
        qnT = arena.take(KC, P)
        scores = arena.take(2 * H, NK)
        scoresB = arena.take(2 * H, NK)
        V = arena.take(2 * H, TOP1)
        J = arena.take(H, NJ)
        best = arena.take(H, TOP1)
        edge = arena.take(H)
        wexp = arena.take(H, TOP)
        wsum = arena.take(H)
        split = arena.take(BLK, NF)
        part1 = arena.take(BLK * NF // 2, dt=BF16).rearrange("p (t f) -> p t f", t=BLK)
        part2 = arena.take(BLK * NF // 2, dt=BF16).rearrange("p (t f) -> p t f", t=BLK)
        slotd = arena.take(BLK * NS * FT // 2, dt=BF16).rearrange("p (t s f) -> p t s f", t=BLK, s=NS)
        slotl = arena.take(BLK * NS * HD // 2, dt=BF16).rearrange("p (t s f) -> p t s f", t=BLK, s=NS)
        dT = [arena.take(BW // 2, parts=NS * FT, dt=BF16) for _ in range(2)]
        lT = [arena.take(BW // 2, parts=NS * HD, dt=BF16) for _ in range(2)]
        E2 = [arena.take(BW) for _ in range(2)]
        acc_at = arena.at
        acc = arena.take(4, BW)
        ytmp = xT
        oTe = arena.take(BLK, BW, parts=4 * HD)
        tables_at = arena.at
        E1 = arena.take(NG, BW)
        F = arena.take(BLK, 2 * H, NF)
        parts_at = arena.at
        GE = arena.take(SLOTS, BW)
        GM = arena.take(SLOTS, BW)
        HH = arena.take(RING, BW)
        assert NE <= NG * BW and NW // 2 <= 8 * BW and NW + NW // 2 <= (2 * SLOTS + RING) * BW
        downf = arena.tensor[0:NS * HD, tables_at:tables_at + NE]
        pairf = arena.tensor[0:NS * FT, parts_at:parts_at + NW]
        tpart = [arena.tensor[:, at:at + NW // 2].bitcast(BF16) for at in (parts_at + NW, acc_at)]

        arena.reset()
        wkvd = arena.take(KC, DC)
        wkup = arena.take(PAIRS, P)
        wqp = arena.take(KC, PAIRS, P)
        wvup = arena.take(D)
        wqr, wqrs = arena.take(KC, DR), arena.take(KC, DR)
        wkr, wkrs = arena.take(DR), arena.take(DR)
        wo1 = arena.take(KC, D)
        cosT = arena.take(SL, parts=DR)
        sinT = arena.take(SL, parts=DR)
        causal = arena.take(P)
        rt = arena.take(4, BW, parts=DR)
        QA = arena.take(SL)
        KA = arena.take(SL)
        cb = arena.take(BW)
        cT = arena.take(SL)
        wpair = arena.take(1 + KC, P)
        otile = arena.take(D)
        vall = arena.take(ST, H, VC)
        probs = arena.take(2, HALF * P)
        PT = arena.take(2, HALF * P)
        oall = arena.take(ST, D)
        sT1 = arena.take(KC, SL)
        rmax = arena.take(8, 1)
        nmax = arena.take(8, 1)
        rden = arena.take(2, 1)
        both_max = arena.take(1)
        behind = arena.take(4, 2)
        shrink = arena.take(4, 2)
        osum = arena.take(2, VC)
        ofirst = arena.take(VC)
        ocols = arena.take(2, P, parts=VC)
        vpair = arena.take(ST, 2 * VC)
        oT1 = arena.take(KC, P)

        loaded = [sem(f"loaded{i}") for i in range(5)]
        const_ready = sem("const_ready")
        dve_chain = sem("dve_chain")
        gsum_ready = sem("gsum_ready")
        gamma_ready = sem("gamma_ready")
        phase_done = sem("phase_done")
        stored = sem("stored")
        passed_dve = sem("passed_dve")
        passed_pe = sem("passed_pe")
        sf = sems("ffn", "xn_ready xT_ps xT_ready h_ps h_ready out_ps")
        sk = sems("lin", "xn_ready xT_ps xT_ready kT_ps kT_ready kf_ps emin_ready e_ready kf_ready kv_ps "
                              "q_ps qT_ready qf_ps qmin_ready qe_ready qf_ready o_ps o_ready oT_ps oT_ready y_ps "
                              "y_added kv_done")
        se = sems("exp", "xn_ready xT_ps xT_ready q_ps qn_ready qnT_ps qnT_ready s_ps s_ready sum_ready log_ready "
                         "shift_ready w_ready f_ready split_ready slots_ps laid_out rest_ready slots_ready e_ps e_ready l_ps ge_ready "
                         "d_ps gm_ready h_made up_ps y_weighed acc_ready fold_ps oT_ready y_ps y_added tables_ready")
        pool_chain = sem("pool_chain")
        sa = sems("att", "xn_ready xT_ps xT_ready c_ps c_ready r_ps r_ready rope_copied v_ps v_ready "
                              "wpair_ready otile_ready kq_ps kq_ready pair_done s_ps m_ready p_ready pt_ps pt_ready o_ps ocols_ready oturn_ps o_read behind_ready shrink_ready ot_ps "
                              "ot_ready y_ps y_added")

        block = ctx.enter_context(nc.Block())

        L0_LOADS = [
            (X[:], ins["x"].rearrange("(t p) d -> p t d", p=P)), (ident[:], ins["ident"]),
            (w1t, ins["w1t"].rearrange("(k p) f -> p k f", p=P)),
            (w2t, ins["w2t"].rearrange("(k p) f -> p k f", p=P)),
            (b1c, ins["b1"]), (b2r, ins["b2"]),
            (wq0, ins["wq0"].rearrange("(k p) n -> p k n", p=P)), (wk0, ins["wk0"].rearrange("(k p) n -> p k n", p=P)),
            (wv0, ins["wv0"].rearrange("(k p) n -> p k n", p=P)), (wo0, ins["wo0"].rearrange("(k p) n -> p k n", p=P)),
            (bq0, ins["bq0"]), (bk0, ins["bk0"]), (bv0, ins["bv0"]), (bo0, ins["bo0"]), (rm, ins["rm"])]
        EXP_LOADS = [
            (wqe, ins["wqe"].rearrange("(k p) n -> p k n", p=P)),
            (woute, ins["woute"].rearrange("(j p) n -> p j n", p=4 * HD)), (fold, ins["fold"]),
            (keys, ins["keys"]), (lng, ins["lng"].partition_broadcast(P)), (lnb, ins["lnb"].partition_broadcast(P)),
            (upw, ins["upw"]), (partl, ins["partl"]), (partd, ins["partd"]),
            (downf, ins["down"]), (pairf, ins["pairk"])]
        ATT_LOADS = [
            (wkvd, ins["wkvd"].rearrange("(k p) n -> p k n", p=P)), (wkup, ins["wkup"]),
            (wqp, ins["wqp"].rearrange("(k p) a n -> p k a n", p=P)), (wvup, ins["wvup"]),
            (wqr, ins["wqr"].rearrange("(k p) n -> p k n", p=P)), (wqrs, ins["wqrs"].rearrange("(k p) n -> p k n", p=P)),
            (wkr, ins["wkr"]), (wkrs, ins["wkrs"]), (wo1, ins["wo1"].rearrange("(k p) n -> p k n", p=P)),
            (cosT, ins["cos"]), (sinT, ins["sin"]), (causal, ins["causal"])]
        PHASE_LOADS = [L0_LOADS, [], [], EXP_LOADS, ATT_LOADS, EXP_LOADS]

        @block.sync
        def _(sp):
            for ph, loads in enumerate(PHASE_LOADS[:STAGES]):
                if ph and loads:
                    sp.wait_ge(phase_done, ph)
                for dst, src in loads:
                    sp.dma_start(dst, src).then_inc(loaded[[0, 0, 0, 1, 2, 3][ph]], 16)
            sp.wait_ge(phase_done, STAGES)
            sp.dma_start(out.rearrange("(t p) d -> p t d", p=P), X[:]).then_inc(stored, 16)
            sp.wait_ge(stored, 16)

        def begin(eng, ph):
            if ph:
                eng.wait_ge(phase_done, ph)
            if PHASE_LOADS[ph]:
                eng.wait_ge(loaded[[0, 0, 0, 1, 2, 3][ph]], 16 * len(PHASE_LOADS[ph]))

        @block.vector
        def _(dve):
            ch = Chain(dve, dve_chain)
            v = nc.vector

            def end_phase():
                ch.sync()
                dve.sem_inc(phase_done, 1)

            def rsqrt_guess(y, x, c):
                ch.link(v.tensor_scalar(c.bitcast(I32), x.bitcast(I32), 1, None, ALU.logical_shift_right))
                ch.link(v.tensor_scalar(y.bitcast(I32), c.bitcast(I32), -1.0, float(0x5f3759df), ALU.mult, ALU.add))

            def rsqrt_step(y, x, c):
                ch.link(v.scalar_tensor_tensor(out=c, in0=y, scalar=-0.5, in1=x, op0=ALU.mult, op1=ALU.mult))
                ch.link(v.tensor_tensor(c, c, y, ALU.mult))
                ch.link(v.scalar_tensor_tensor(out=y, in0=c, scalar=1.5, in1=y, op0=ALU.add, op1=ALU.mult))

            def rsqrt(y, x, c):
                rsqrt_guess(y, x, c)
                for _ in range(3):
                    rsqrt_step(y, x, c)

            def layernorm(srcs, dst, ready):
                n = len(srcs)
                for t, src in enumerate(srcs):
                    ch.mark(v.bn_stats(stats[:, t, :], src))
                ch.sync()
                for t in range(n):
                    ch.mark(v.bn_aggr(mv[:, t, :], stats[:, t, :]))
                ch.sync()
                ch.link(v.tensor_scalar(var[:, 0:n], mv[:, 0:n, 1], EPS, None, ALU.add))
                rsqrt(rstd[:, 0:n], var[:, 0:n], newton[:, 0:n])
                for t, src in enumerate(srcs):
                    v.tensor_scalar(dst[:, t, :], src, mv[:, t, 0:1], rstd[:, t:t + 1],
                                    ALU.subtract, ALU.mult).then_inc(ready, 1)

            def ternary(w, col, count):
                ch.link(v.scalar_tensor_tensor(out=wtmp[:, 0:count // P], in0=w, scalar=-1.0, in1=w,
                                               op0=ALU.mult, op1=ALU.max))
                v.reduce_sum(gsum[:, col:col + 1], wtmp[:, 0:count // P], AX.X).then_inc(gsum_ready, 1)
                dve.wait_ge(gamma_ready, col + 1)
                tot = bank[0][:, col:col + 1]
                ch.mark(v.tensor_scalar(thr[:, 0:1], tot, 0.5 / count, 0.5 * EPS, ALU.mult, ALU.add))
                ch.mark(v.tensor_scalar(thr[:, 1:2], tot, -0.5 / count, -0.5 * EPS, ALU.mult, ALU.add))
                ch.sync()
                ch.link(v.tensor_scalar(wtmp[:, 0:count // P], w, thr[:, 1:2], None, ALU.is_lt))
                ch.link(v.scalar_tensor_tensor(out=w, in0=w, scalar=thr[:, 0:1], in1=wtmp[:, 0:count // P],
                                               op0=ALU.is_gt, op1=ALU.subtract))

            def ffn(s, r):
                ch.restart()
                with dve.Fori(0, NB) as b:
                    g = b + r * NB
                    layernorm([X[:, b * BLK + t, :] for t in range(BLK)], xn, s["xn_ready"])
                    for t in range(BLK):
                        dve.wait_ge(s["out_ps"], g * BLK + (t // 2 * 2 + 2))
                        xt = X[:, b * BLK + t, :]
                        ps = bank[6 + t // 2][:, (t % 2) * D:(t % 2 + 1) * D]
                        ch.mark(v.scalar_tensor_tensor(out=xt, in0=ps, scalar=0.5, in1=xt, op0=ALU.mult, op1=ALU.add))
                    ch.restart()

            def linear_attention(s):
                ch.restart()
                with dve.Fori(0, SEQS) as q:
                    ch.mark(v.memset(kv, 0.0))
                    ch.mark(v.memset(vext[:, :, :, HD:VC], 1.0))
                    ch.restart()
                    with dve.Fori(0, SB) as b:
                        g = b + q * SB
                        layernorm([X[:, g * BLK + t, :] for t in range(BLK)], xn, s["xn_ready"])
                        for t in range(BLK):
                            dve.wait_ge(s["kf_ps"], g * BLK + (t + 1))
                            for m in range(KC):
                                v.tensor_scalar(emin[:, m, :], bank[4 + m], 0.0, None,
                                                ALU.min).then_inc(s["emin_ready"], 1)
                            dve.wait_ge(s["e_ready"], g * BLK + (t + 1))
                            if t >= 2:
                                dve.wait_ge(s["kv_ps"], g * BLK + (t - 1))
                            for m in range(KC):
                                v.scalar_tensor_tensor(out=kf[:, t % 2, m * BW:(m + 1) * BW], in0=bank[4 + m],
                                                       scalar=0.0, in1=efeat[:, m, :], op0=ALU.max,
                                                       op1=ALU.add).then_inc(s["kf_ready"], 1)
                            v.tensor_copy(vext[:, t % 2, :, 0:HD],
                                          bank[6][:, 0:D].rearrange("p (h d) -> p h d", h=H)).then_inc(s["kf_ready"], 1)
                        dve.wait_ge(s["kv_ps"], g * BLK + BLK)
                        ps = bank[7][:, 0:PAIRS * 2 * VC].rearrange("p (a c) -> p a c", a=PAIRS)
                        for e in range(2):
                            rows, cols = slice(64 * e, 64 * e + 64), slice(VC * e, VC * e + VC)
                            ch.mark(v.scalar_tensor_tensor(out=kv[rows, :, cols], in0=ps[rows, :, cols],
                                                           scalar=1.0 / 256, in1=kv[rows, :, cols],
                                                           op0=ALU.mult, op1=ALU.add))
                        ch.restart()
                    dve.sem_inc(s["kv_done"], 1)
                    with dve.Fori(0, SB) as b:
                        g = b + q * SB
                        for p in range(PAIRS + 1):
                            if p < PAIRS:
                                dve.wait_ge(s["qf_ps"], g * PAIRS + (p + 1))
                                v.tensor_scalar(emin[:, p % 2, :], bank[2 + p % 4], 0.0, None,
                                                ALU.min).then_inc(s["qmin_ready"], 1)
                            if p:
                                dve.wait_ge(s["qe_ready"], g * PAIRS + p)
                                v.scalar_tensor_tensor(out=qf[:, p - 1, :], in0=bank[2 + (p - 1) % 4], scalar=0.0,
                                                       in1=efeat[:, (p - 1) % 2, :], op0=ALU.max,
                                                       op1=ALU.add).then_inc(s["qf_ready"], 1)
                        for t in range(BLK):
                            dve.wait_ge(s["o_ps"], g * BLK + (t + 1))
                            ps = bank[6][:, 0:H * VC].rearrange("p (h c) -> p h c", h=H)
                            ch.link(v.tensor_scalar(nrm, ps[:, :, HD], 1e-6, None, ALU.max))
                            ch.link(v.reciprocal(rnrm, nrm))
                            v.tensor_tensor(o0.rearrange("p (h d) -> p h d", h=H), ps[:, :, 0:HD],
                                            rnrm[:, :, None].to_broadcast([P, H, HD]), ALU.mult).then_inc(s["o_ready"], 1)
                            dve.wait_ge(s["y_ps"], g * BLK + (t + 1))
                            xt = X[:, g * BLK + t, :]
                            ch.link(v.tensor_tensor(xt, bank[7][:, D:2 * D], xt, ALU.add))
                            dve.sem_inc(s["y_added"], 1)
                        ch.restart()

            def largest(dst, src, rest, rows, step):
                ch.sync()
                for r in rows:
                    at = dst[:, r, step // 2 * 8:step // 2 * 8 + 8]
                    if step % 2 == 0:
                        ch.mark(v.max(at, (rest if step else src)[:, r, :]))
                    else:
                        ch.mark(v.match_replace(rest[:, r, :], at, (src if step == 1 else rest)[:, r, :], LOWEST))

            def sums(half, segs):
                hs = slice(half * H // 2, (half + 1) * H // 2)
                v4 = V.rearrange("p (h two) k -> p h two k", two=2)[:, hs]
                for i0, ni, nj, off in segs:
                    x = v4[:, :, 0, i0:i0 + ni][:, :, :, None].to_broadcast([P, H // 2, ni, nj])
                    y = v4[:, :, 1, 0:nj][:, :, None, :].to_broadcast([P, H // 2, ni, nj])
                    o = J[:, hs, off:off + ni * nj].rearrange("p h (i j) -> p h i j", i=ni)
                    if ni == 1:
                        x, y, o = x[:, :, 0, :], y[:, :, 0, :], o[:, :, 0, :]
                    elif nj == 1:
                        x, y, o = x[:, :, :, 0], y[:, :, :, 0], o[:, :, :, 0]
                    ch.mark(v.tensor_tensor(o, x, y, ALU.add))

            def expert_choice(s, g, j, c, k, i):
                n = g * BLK + j
                cnt = n + c * NT
                rows = bass.ds((g % 2) * H, H)
                at = k * CH + i
                if at == 0:
                    ch.link(v.bn_stats(stats[:, 0, :], X[:, n, :]))
                    ch.link(v.bn_aggr(mv[:, 0, :], stats[:, 0, :]))
                    ch.link(v.tensor_scalar(var[:, 0:1], mv[:, 0:1, 1], EPS, None, ALU.add))
                if at == 1:
                    rsqrt_guess(rstd[:, 0:1], var[:, 0:1], newton[:, 0:1])
                if at in (1, 2, 3):
                    rsqrt_step(rstd[:, 0:1], var[:, 0:1], newton[:, 0:1])
                if at == 4:
                    v.tensor_scalar(xne[:, 0, :], X[:, n, :], mv[:, 0, 0:1], rstd[:, 0:1],
                                    ALU.subtract, ALU.mult).then_inc(s["xn_ready"], 1)
                if at == 5:
                    dve.wait_ge(s["xn_ready"], cnt + 1)
                    ch.mark(v.tensor_copy(F[:, j, rows, FT:NF], xne[:, 0, :].rearrange("p (h d) -> p h d", h=H)))
                if at == 12:
                    dve.wait_ge(s["q_ps"], cnt + 1)
                    q = bank[7][:, 0:D].rearrange("p (h d) -> p h d", h=H)
                    ch.link(v.reduce_sum(hmean, q, AX.X))
                    ch.link(v.tensor_scalar(hmean, hmean, 1.0 / HD, None, ALU.mult))
                    ch.link(v.tensor_tensor(qc, q, hmean[:, :, None].to_broadcast([P, H, HD]), ALU.subtract))
                if at == 13:
                    ch.link(v.tensor_tensor(qsq, qc, qc, ALU.mult))
                    ch.link(v.reduce_sum(hvar, qsq, AX.X))
                if at == 14:
                    ch.link(v.tensor_scalar(hvar, hvar, 1.0 / HD, EPS, ALU.mult, ALU.add))
                    rsqrt_guess(hrstd, hvar, hnewton)
                if at in (15, 16, 17):
                    rsqrt_step(hrstd, hvar, hnewton)
                if at == 18:
                    ch.link(v.tensor_tensor(qc, qc, hrstd[:, :, None].to_broadcast([P, H, HD]), ALU.mult))
                    ch.link(v.tensor_tensor(qc, qc, lng[:, None, :].to_broadcast([P, H, HD]), ALU.mult))
                if at == 19:
                    v.tensor_tensor(qc, qc, lnb[:, None, :].to_broadcast([P, H, HD]), ALU.add).then_inc(s["qn_ready"], 1)
                if at == 21:
                    dve.wait_ge(s["qn_ready"], cnt + 1)
                    ch.mark(v.tensor_copy(F[:, j, rows, 0:HD], qc))
                if at in (LISTS_AT, LISTS_AT + 32):
                    dve.wait_ge(s["s_ready"], cnt * 4 + (2 if at == LISTS_AT else 4))
                    dve.sem_inc(passed_dve, 1)
                if LISTS_AT <= at < LISTS_AT + 4 * H:
                    two, step = divmod(at - LISTS_AT, 8)
                    if step in LARGEST_AT:
                        largest(V, scores, scoresB, range(4 * two, 4 * two + 4), LARGEST_AT.index(step))
                for half in range(2):
                    to = at - (LISTS_AT + 4 * H // 2 * (half + 1))
                    if 0 <= to < 3:
                        ch.sync()
                        sums(half, SEGS[3 * to:3 * to + 3])
                if LISTS_AT + 35 <= at < LISTS_AT + 65 and (at - LISTS_AT - 35) % 3 == 0:
                    four, step = divmod((at - LISTS_AT - 35) // 3, 5)
                    largest(best, J, J, range(4 * four, 4 * four + 4), step)
                if LISTS_AT + 67 <= at < CHOSEN_AT:
                    four, step = divmod(at - LISTS_AT - 67, 5)
                    largest(best, J, J, range(4 * four + 8, 4 * four + 12), step)
                if at == CHOSEN_AT:
                    ch.sync()
                    v.tensor_tensor(wexp, best[:, :, 0:TOP], best[:, :, 0:1].to_broadcast([P, H, TOP]),
                                    ALU.subtract).then_inc(s["shift_ready"], 1)
                    ch.link(v.tensor_tensor(edge, best[:, :, TOP - 1], best[:, :, TOP], ALU.add))
                    ch.link(v.tensor_scalar(F[:, j, rows, HD], edge, 0.5, None, ALU.mult))
                    v4 = V.rearrange("p (h two) k -> p h two k", two=2)
                    ch.mark(v.tensor_copy(F[:, j, rows, HD + 1:HD + 2], v4[:, :, 1, 0:1]))
                if at == CHOSEN_AT + 1:
                    dve.wait_ge(s["w_ready"], cnt + 1)
                    v.reduce_sum(wsum, wexp, AX.X).then_inc(s["sum_ready"], 1)
                if at == CHOSEN_AT + 3:
                    dve.wait_ge(s["log_ready"], cnt + 1)
                    v4 = V.rearrange("p (h two) k -> p h two k", two=2)
                    ch.link(v.tensor_tensor(F[:, j, rows, HD + 2], v4[:, :, 0, 0], wsum, ALU.add))
                    dve.sem_inc(s["f_ready"], 1)

            def weigh(s, U, k, g):
                dve.wait_ge(s["up_ps"], RING + U * CH + YG * (g + 1))
                dve.wait_ge(s["e_ready"], U * (1 + NG) + (2 + g))
                ch.sync()
                dst = ytmp[:, g % 2, :] if g else acc[:, k, :]
                v.tensor_tensor(dst, bank[4], E1[:, g, :], ALU.mult).then_inc(s["y_weighed"], 1)
                if g >= 2:
                    dve.wait_ge(s["y_weighed"], U * NG + (g + 1))
                    ch.mark(v.tensor_tensor(acc[:, k, :], acc[:, k, :], ytmp[:, (g - 1) % 2, :], ALU.add))
                if g == NG - 1:
                    dve.wait_ge(s["y_weighed"], U * NG + (g + 2))
                    ch.sync()
                    ch.mark(v.tensor_tensor(acc[:, k, :], acc[:, k, :], ytmp[:, g % 2, :], ALU.add))

            def expert_group(s, b, j, c, choose, first):
                G = (b * BLK + j) + c * NT
                for k in range(4):
                    U = G * 4 + k
                    dve.wait_ge(s["e_ready"], U * (1 + NG) + 1)
                    for i in range(CH):
                        dve.wait_ge(s["d_ps"], U * CH + (i + 1))
                        dve.wait_ge(s["h_made"], U * CH + (i + 1))
                        v.scalar_tensor_tensor(out=GM[:, i % SLOTS, :], in0=bank[2 + i % 2], scalar=0.0, in1=E2[k % 2],
                                               op0=ALU.is_ge, op1=ALU.mult).then_inc(s["gm_ready"], 1)
                        if i == 3 and (k or not first):
                            weigh(s, U - 1, (k - 1) % 4, NG - 1)
                            if k == 0:
                                ch.sync()
                                dve.sem_inc(s["acc_ready"], 1)
                        if k == 0 and i == 7 and not first:
                            dve.wait_ge(s["fold_ps"], G + 1)
                        if i % 4 == 3 and i > 3:
                            weigh(s, U, k, i // 4 - 1)
                        if choose:
                            expert_choice(s, b + 1, j, c, k, i)

            def expert_block(s, b, c, choose):
                expert_group(s, b, 0, c, choose, True)
                ch.restart()
                with dve.Fori(1, BLK) as j:
                    expert_group(s, b, j, c, choose, False)
                    ch.restart()
                weigh(s, b * H + (c * UNITS + H - 1), 3, NG - 1)
                ch.sync()
                dve.sem_inc(s["acc_ready"], 1)
                for t in range(BLK):
                    n = b * BLK + t
                    dve.wait_ge(s["y_ps"], n + (c * NT + 1))
                    ch.link(v.scalar_tensor_tensor(out=X[:, n, :], in0=bank[7][:, (t % 2) * D:(t % 2 + 1) * D], scalar=0.5,
                                                   in1=X[:, n, :], op0=ALU.mult, op1=ALU.add))
                    dve.sem_inc(s["y_added"], 1)
                ch.restart()

            def experts(s, c):
                if c == 0:
                    dve.sem_inc(s["h_made"], SLOTS)
                ch.restart()
                with dve.Fori(0, BLK) as j:
                    for k in range(4):
                        for i in range(CH):
                            expert_choice(s, 0, j, c, k, i)
                    ch.restart()
                with dve.Fori(0, NB - 1) as b:
                    expert_block(s, b, c, True)
                expert_block(s, NB - 1, c, False)

            def attention(s):
                ch.restart()
                with dve.Fori(0, SEQS) as q:
                    ch.mark(v.memset(vall[:, :, :, HD:VC], 1.0))
                    ch.restart()
                    with dve.Fori(0, SB) as b:
                        g = b + q * SB
                        layernorm([X[:, g * BLK + t, :] for t in range(BLK)], xn, s["xn_ready"])
                        cols = bass.ds(b * BW, BW)
                        for i, to in enumerate((KA, QA)):
                            dve.wait_ge(s["r_ps"], g * 2 + (i + 1))
                            ch.mark(v.tensor_tensor(rt[:, 2 * i, :], bank[3 + 2 * i][0:DR, :], cosT[:, cols], ALU.mult))
                            ch.mark(v.tensor_tensor(rt[:, 2 * i + 1, :], bank[4 + 2 * i][0:DR, :], sinT[:, cols], ALU.mult))
                            ch.sync()
                            v.tensor_tensor(to[0:DR, cols], rt[:, 2 * i, :], rt[:, 2 * i + 1, :],
                                            ALU.add).then_inc(s["r_ready"], 1)
                        for t in range(BLK):
                            dve.wait_ge(s["v_ps"], g * 2 + (t // 2 + 1))
                            ps = bank[t // 2][:, (t % 2) * D:(t % 2 + 1) * D].rearrange("p (h d) -> p h d", h=H)
                            v.tensor_copy(vall[:, b * BLK + t, :, 0:HD], ps).then_inc(s["v_ready"], 1)
                        ch.restart()
                    with dve.Fori(0, PAIRS) as p:
                        pq = p + q * PAIRS
                        v.tensor_copy(wpair[:, 0, :], wkup[:, p, :]).then_inc(s["wpair_ready"], 1)
                        for k in range(KC):
                            v.tensor_copy(wpair[:, 1 + k, :], wqp[:, k, p, :]).then_inc(s["wpair_ready"], 1)
                        dve.wait_ge(s["v_ready"], q * ST + ST)
                        v.tensor_copy(vpair, vall.rearrange("p t h c -> p t (h c)")[:, :, bass.ds(p * (2 * VC), 2 * VC)]
                                      ).then_inc(s["wpair_ready"], 1)
                        for i in range(8):
                            dve.wait_ge(s["kq_ps"], pq * 8 + (i + 1))
                            to, j = (KA, i) if i < 4 else (QA, i - 4)
                            for e in range(2):
                                r0 = 64 * e + DR
                                v.tensor_copy(to[r0:r0 + HD, j * BW:(j + 1) * BW],
                                              bank[i][r0:r0 + HD, :]).then_inc(s["kq_ready"], 1)
                        for x in range(CN + 5):
                            if x >= 5:
                                finish(s, p, pq, x - 5)
                            if 4 <= x < CN + 4:
                                dve.wait_ge(s["o_ps"], pq * CN + (x - 3))
                                v.tensor_copy(ocols[:, x % 2, :], bank[6 + x % 2][0:VC, 0:P]).then_inc(s["ocols_ready"], 1)
                            if x < CN:
                                maximum(s, pq, x)
                        ch.restart()
                    dve.sem_inc(s["pair_done"], 1)
                    with dve.Fori(0, ST) as t:
                        v.tensor_copy(otile, oall[:, t, :]).then_inc(s["otile_ready"], 1)
                        dve.wait_ge(s["y_ps"], q * ST + (t + 1))
                        xt = X[:, q * ST + t, :]
                        ch.link(v.tensor_tensor(xt, bank[7][:, 0:D], xt, ALU.add))
                        dve.sem_inc(s["y_added"], 1)
                        ch.restart()

            def maximum(s, pq, x):
                e, qt, k0, nt = CHUNKS[x]
                dve.wait_ge(s["s_ps"], pq * CN + (x + 1))
                S = psum[:, 2 * (x % 2):2 * (x % 2) + 2, :].rearrange("p a b -> p (a b)")
                if k0 + nt == qt + 1:
                    ch.link(v.tensor_tensor(S[:, (nt - 1) * P:nt * P], S[:, (nt - 1) * P:nt * P], causal, ALU.add))
                ch.link(v.reduce_max(rmax[:, x % 8, :], S[:, 0:nt * P], AX.X))
                v.tensor_scalar(nmax[:, x % 8, :], rmax[:, x % 8, :], -SCALE, None, ALU.mult).then_inc(s["m_ready"], 1)
                if k0:
                    m = MERGED.index(x)
                    ch.link(v.tensor_tensor(both_max, rmax[:, (x - 1) % 8, :], rmax[:, x % 8, :], ALU.max))
                    ch.mark(v.tensor_tensor(behind[:, m % 4, 0:1], rmax[:, (x - 1) % 8, :], both_max, ALU.subtract))
                    ch.link(v.tensor_tensor(behind[:, m % 4, 1:2], rmax[:, x % 8, :], both_max, ALU.subtract))
                    dve.sem_inc(s["behind_ready"], 1)

            def finish(s, p, pq, x):
                e, qt, k0, nt = CHUNKS[x]
                dve.wait_ge(s["oturn_ps"], pq * CN + (x + 1))
                ps = bank[6 + x % 2][:, P:P + VC]
                if k0 + nt < qt + 1:
                    ch.sync()
                    ch.link(v.tensor_copy(ofirst, ps))
                    dve.sem_inc(s["o_read"], 1)
                    return
                if k0:
                    m = MERGED.index(x)
                    dve.wait_ge(s["shrink_ready"], pq * MN + (m + 1))
                    ch.link(v.tensor_scalar(osum[:, 0, :], ofirst, shrink[:, m % 4, 0:1], None, ALU.mult))
                    ch.link(v.scalar_tensor_tensor(out=osum[:, 1, :], in0=ps, scalar=shrink[:, m % 4, 1:2],
                                                   in1=osum[:, 0, :], op0=ALU.mult, op1=ALU.add))
                    ps = osum[:, 1, :]
                ch.link(v.reciprocal(rden[:, x % 2, :], ps[:, HD:VC]))
                ch.link(v.tensor_scalar(oall[:, qt, bass.ds(p * (2 * HD) + e * HD, HD)], ps[:, 0:HD],
                                        rden[:, x % 2, :], None, ALU.mult))
                dve.sem_inc(s["o_read"], 1)

            v.memset(ones[:], 1.0).then_inc(const_ready, 1)
            begin(dve, 0)
            ternary(w1t.rearrange("p k f -> p (k f)"), 0, D * FF)
            ternary(w2t.rearrange("p k f -> p (k f)"), 1, D * FF)
            dve.sem_inc(const_ready, 1)
            ffn(sf, 0)
            end_phase()
            if STAGES > 1:
                linear_attention(sk)
                end_phase()
            if STAGES > 2:
                ffn(sf, 1)
                end_phase()
            if STAGES > 3:
                begin(dve, 3)
                experts(se, 0)
                end_phase()
            if STAGES > 4:
                begin(dve, 4)
                attention(sa)
                end_phase()
            if STAGES > 5:
                begin(dve, 5)
                experts(se, 1)
                end_phase()

        @block.scalar
        def _(act):
            a = nc.scalar

            def ffn(s, r):
                with act.Fori(0, NB) as b:
                    g = b + r * NB
                    act.wait_ge(s["xT_ps"], g + 1)
                    for k in range(KC):
                        a.copy(xT[:, k, :], bank[k]).then_inc(s["xT_ready"], 1)
                    for m in range(FC):
                        act.wait_ge(s["h_ps"], g * FC + (m + 1))
                        a.activation(h[:, m, :], bank[2 + m % 4], ACT.Relu,
                                     bias=b1c[:, m:m + 1]).then_inc(s["h_ready"], 1)

            def linear_attention(s):
                with act.Fori(0, SEQS) as q:
                    with act.Fori(0, SB) as b:
                        g = b + q * SB
                        act.wait_ge(s["xT_ps"], g + 1)
                        for k in range(KC):
                            a.copy(xT[:, k, :], bank[k]).then_inc(s["xT_ready"], 1)
                            a.copy(sT[:, k, bass.ds(b * BW, BW)], bank[k]).then_inc(s["xT_ready"], 1)
                        for m in range(KC):
                            act.wait_ge(s["kT_ps"], g * KC + (m + 1))
                            a.activation(kT[:, m, :], bank[2 + m], ACT.Identity,
                                         bias=bk0[:, m:m + 1]).then_inc(s["kT_ready"], 1)
                        for t in range(BLK):
                            act.wait_ge(s["emin_ready"], g * (2 * BLK) + 2 * (t + 1))
                            a.activation(efeat, emin, ACT.Exp).then_inc(s["e_ready"], 1)
                    with act.Fori(0, SB) as b:
                        g = b + q * SB
                        for m in range(KC):
                            act.wait_ge(s["q_ps"], g * KC + (m + 1))
                            a.activation(kT[:, m, :], bank[m], ACT.Identity,
                                         bias=bq0[:, m:m + 1]).then_inc(s["qT_ready"], 1)
                        for p in range(PAIRS):
                            act.wait_ge(s["qmin_ready"], g * PAIRS + (p + 1))
                            a.activation(efeat[:, p % 2, :], emin[:, p % 2, :], ACT.Exp).then_inc(s["qe_ready"], 1)
                        for t in range(BLK):
                            act.wait_ge(s["oT_ps"], g * BLK + (t + 1))
                            a.copy(oT0, bank[7][:, 0:D].rearrange("p (k t) -> p k t", k=KC)).then_inc(s["oT_ready"], 1)

            def expert_choice(s, g, j, c, k, i):
                n = g * BLK + j
                cnt = n + c * NT
                at = k * CH + i
                if at == 9:
                    act.wait_ge(s["xT_ps"], cnt + 1)
                    a.copy(xTe, bank[6][:, 0:D].rearrange("p (k t) -> p k t", k=KC)).then_inc(s["xT_ready"], 1)
                if at == 23:
                    act.wait_ge(s["qnT_ps"], cnt + 1)
                    a.copy(qnT, bank[6][:, 0:D].rearrange("p (k t) -> p k t", k=KC)).then_inc(s["qnT_ready"], 1)
                if at in (26, 27, CH + 5, CH + 6):
                    m = (26, 27, CH + 5, CH + 6).index(at)
                    act.wait_ge(s["s_ps"], cnt * 4 + (m + 1))
                    a.copy(scores[:, 8 * m:8 * m + 8, :], bank[6 + m % 2].rearrange("p (r n) -> p r n", r=8)).then_inc(
                        s["s_ready"], 1)
                if at == CHOSEN_AT + 1:
                    act.wait_ge(s["shift_ready"], cnt + 1)
                    a.activation(wexp, wexp, ACT.Exp).then_inc(s["w_ready"], 1)
                    act.wait_ge(s["sum_ready"], cnt + 1)
                    a.activation(wsum, wsum, ACT.Ln).then_inc(s["log_ready"], 1)

            def lay_out(s, U, first, step):
                f = F[:, :, U % (2 * H), :]
                if step == 0:
                    if not first:
                        act.wait_ge(s["slots_ps"], U)
                    a.copy(slotd[:, :, 0:3, :], f[:, :, None, 0:FT].to_broadcast([P, BLK, 3, FT])).then_inc(
                        s["laid_out"], 1)
                if step == 1:
                    a.copy(slotl[:, :, 0:3, :], f[:, :, None, FT:NF].to_broadcast([P, BLK, 3, HD])).then_inc(
                        s["laid_out"], 1)
                if step == 2:
                    act.wait_ge(s["rest_ready"], U + 1)
                    a.copy(slotd[:, :, 3:5, :], split[:, :, None, 0:FT].to_broadcast([P, BLK, 2, FT])).then_inc(
                        s["laid_out"], 1)
                if step == 3:
                    a.copy(slotl[:, :, 3:5, :], split[:, :, None, FT:NF].to_broadcast([P, BLK, 2, HD])).then_inc(
                        s["laid_out"], 1)

            def slots_copy(s, U, par):
                act.wait_ge(s["slots_ps"], U + 1)
                b16 = bank[5].bitcast(BF16)
                a.copy(dT[par], b16[0:NS * FT, 0:BW]).then_inc(s["slots_ready"], 1)
                a.copy(lT[par], b16[0:NS * HD, BW:2 * BW]).then_inc(s["slots_ready"], 1)

            def factors(s, U, par, ms):
                for m in ms:
                    act.wait_ge(s["e_ps"], U * (1 + NG) + (m + 1))
                    dst = E1[:, m - 1, :] if m else E2[par]
                    a.activation(dst, bank[F_BANK[m]], ACT.Exp).then_inc(s["e_ready"], 1)

            def outputs_copy(s, j, G):
                act.wait_ge(s["fold_ps"], G + 2)
                a.copy(oTe[:, j, :], bank[7][0:4 * HD, :]).then_inc(s["oT_ready"], 1)

            def expert_group(s, b, j, c, choose, first, last):
                G = (b * BLK + j) + c * NT
                for k in range(4):
                    U = G * 4 + k
                    for i in range(CH):
                        act.wait_ge(s["l_ps"], U * CH + (i + 1))
                        act.wait_ge(s["h_made"], U * CH + (i + 1))
                        a.activation(GE[:, i % SLOTS, :], bank[i % 2], ACT.Gelu).then_inc(s["ge_ready"], 1)
                        if k == 0 and i == 8 and not first:
                            outputs_copy(s, j - 1, G - 1)
                        if choose:
                            expert_choice(s, b + 1, j, c, k, i)
                        if i == 17:
                            factors(s, U, k % 2, range(EARLY, 1 + NG))
                        if not (last and k == 3):
                            if 19 <= i < 23:
                                if choose and k == 3 and i == 19:
                                    act.wait_ge(s["f_ready"], (b * BLK + j) + (c * NT + BLK + 1))
                                lay_out(s, U + 1, False, i - 19)
                            if i == 27:
                                slots_copy(s, U + 1, (k + 1) % 2)
                            if i == CH - 1:
                                factors(s, U + 1, (k + 1) % 2, range(EARLY))

            def experts(s, c):
                with act.Fori(0, BLK) as j:
                    for k in range(4):
                        for i in range(CH):
                            expert_choice(s, 0, j, c, k, i)
                act.wait_ge(s["f_ready"], c * NT + BLK)
                for step in range(4):
                    lay_out(s, c * UNITS, c == 0, step)
                slots_copy(s, c * UNITS, 0)
                factors(s, c * UNITS, 0, range(EARLY))
                with act.Fori(0, NB - 1) as b:
                    expert_group(s, b, 0, c, True, True, False)
                    with act.Fori(1, BLK) as j:
                        expert_group(s, b, j, c, True, False, False)
                    outputs_copy(s, BLK - 1, b * BLK + (c * NT + BLK - 1))
                expert_group(s, NB - 1, 0, c, False, True, False)
                with act.Fori(1, BLK - 1) as j:
                    expert_group(s, NB - 1, j, c, False, False, False)
                expert_group(s, NB - 1, BLK - 1, c, False, False, True)
                outputs_copy(s, BLK - 1, c * NT + NT - 1)

            def attention(s):
                with act.Fori(0, SEQS) as q:
                    with act.Fori(0, SB) as b:
                        g = b + q * SB
                        cols = bass.ds(b * BW, BW)
                        act.wait_ge(s["xT_ps"], g + 1)
                        for k in range(KC):
                            a.copy(sT1[:, k, cols], bank[k]).then_inc(s["xT_ready"], 1)
                        act.wait_ge(s["c_ps"], g + 1)
                        a.copy(cb, bank[2]).then_inc(s["c_ready"], 1)
                        a.copy(cT[:, cols], bank[2]).then_inc(s["c_ready"], 1)
                        act.wait_ge(s["r_ready"], g * 2 + 2)
                        for to in (KA, QA):
                            a.copy(to[64:64 + DR, cols], to[0:DR, cols]).then_inc(s["rope_copied"], 1)
                    with act.Fori(0, PAIRS) as p:
                        pq = p + q * PAIRS
                        for x in range(CN + 2):
                            if x >= 2:
                                for g in range(GROUPS[x - 2]):
                                    w = min(BLK, CHUNKS[x - 2][3] - g * BLK) * P
                                    act.wait_ge(s["pt_ps"], pq * PTN + (PT_AT[x - 2] + g + 1))
                                    a.copy(PT[:, x % 2, g * BW:g * BW + w],
                                           bank[4 + (PT_AT[x - 2] + g) % 2][:, 0:w]).then_inc(s["pt_ready"], 1)
                            if x < CN:
                                w = CHUNKS[x][3] * P
                                act.wait_ge(s["m_ready"], pq * CN + (x + 1))
                                S = psum[:, 2 * (x % 2):2 * (x % 2) + 2, :].rearrange("p a b -> p (a b)")
                                a.activation(probs[:, x % 2, 0:w], S[:, 0:w], ACT.Exp, bias=nmax[:, x % 8, :],
                                             scale=SCALE).then_inc(s["p_ready"], 1)
                                if x in MERGED:
                                    m = MERGED.index(x)
                                    act.wait_ge(s["behind_ready"], pq * MN + (m + 1))
                                    a.activation(shrink[:, m % 4, :], behind[:, m % 4, :], ACT.Exp,
                                                 scale=SCALE).then_inc(s["shrink_ready"], 1)
                    with act.Fori(0, ST) as t:
                        act.wait_ge(s["ot_ps"], q * ST + (t + 1))
                        a.copy(oT1, bank[6][:, 0:D].rearrange("p (k t) -> p k t", k=KC)).then_inc(s["ot_ready"], 1)

            begin(act, 0)
            act.wait_ge(const_ready, 2)
            ffn(sf, 0)
            if STAGES > 1:
                begin(act, 1)
                linear_attention(sk)
            if STAGES > 2:
                begin(act, 2)
                ffn(sf, 1)
            if STAGES > 3:
                begin(act, 3)
                experts(se, 0)
            if STAGES > 4:
                begin(act, 4)
                attention(sa)
            if STAGES > 5:
                begin(act, 5)
                experts(se, 1)

        @block.tensor
        def _(pe):
            t_ = nc.tensor

            def transpose_block(s, b):
                pe.wait_ge(s["xn_ready"], b * BLK + BLK)
                for k in range(KC):
                    for t in range(BLK):
                        mm = t_.transpose(bank[k][:, t * P:(t + 1) * P], xn[:, t, k * P:(k + 1) * P], ident[:])
                mm.then_inc(s["xT_ps"], 1)

            def project(dst, lhs, rhs):
                for k in range(KC):
                    mm = t_.matmul(dst, lhs(k), rhs(k), start=(k == 0), stop=(k == KC - 1))
                return mm

            def project_bias(dst, lhs, rhs, row):
                for k in range(KC):
                    t_.matmul(dst, lhs(k), rhs(k), start=(k == 0), stop=False)
                return t_.matmul(dst, ones[0:1, :], row, start=False, stop=True)

            def turn(dst, src):
                for k in range(KC):
                    mm = t_.transpose(dst[:, k * P:(k + 1) * P], src[:, k * P:(k + 1) * P], ident[:])
                return mm

            def ffn(s, r):
                with pe.Fori(0, NB) as b:
                    g = b + r * NB
                    transpose_block(s, g)
                    pe.wait_ge(s["xT_ready"], g * KC + KC)
                    for m in range(FC):
                        if m >= 4:
                            pe.wait_ge(s["h_ready"], g * FC + (m - 3))
                        project(bank[2 + m % 4], lambda k: w1t[:, k, m * P:(m + 1) * P],
                                lambda k: xT[:, k, :]).then_inc(s["h_ps"], 1)
                    pe.wait_ge(s["h_ready"], g * FC + FC)
                    for t in range(BLK):
                        ps = bank[6 + t // 2][:, (t % 2) * D:(t % 2 + 1) * D]
                        for m in range(FC):
                            t_.matmul(ps, h[:, m, t * P:(t + 1) * P], w2t[:, m, :], start=(m == 0), stop=False)
                        t_.matmul(ps, ones[0:1, :], b2r, start=False, stop=True).then_inc(s["out_ps"], 1)

            def linear_attention(s):
                with pe.Fori(0, SEQS) as q:
                    with pe.Fori(0, SB) as b:
                        g = b + q * SB
                        transpose_block(s, g)
                        pe.wait_ge(s["xT_ready"], g * (2 * KC) + 2 * KC)
                        for m in range(KC):
                            project(bank[2 + m], lambda k: wk0[:, k, m * P:(m + 1) * P],
                                    lambda k: xT[:, k, :]).then_inc(s["kT_ps"], 1)
                        pe.wait_ge(s["kT_ready"], g * KC + KC)
                        for t in range(BLK + 1):
                            if t:
                                pe.wait_ge(s["kf_ready"], g * (3 * BLK) + 3 * t)
                            if t < BLK:
                                for m in range(KC):
                                    t_.matmul(bank[4 + m], kT[:, m, t * P:(t + 1) * P], rm, start=True, stop=True)
                                project_bias(bank[6][:, 0:D], lambda k: xT[:, k, t * P:(t + 1) * P],
                                             lambda k: wv0[:, k, :], bv0).then_inc(s["kf_ps"], 1)
                            if t:
                                u = t - 1
                                for p in range(PAIRS):
                                    mm = t_.matmul(bank[7][:, p * 2 * VC:(p + 1) * 2 * VC],
                                                   kf[:, u % 2, p * P:(p + 1) * P],
                                                   vext[:, u % 2, 2 * p:2 * p + 2, :].rearrange("p h c -> p (h c)"),
                                                   start=(u == 0 and p == 0), stop=(u == BLK - 1),
                                                   skip_group_check=True)
                                mm.then_inc(s["kv_ps"], 1)
                    with pe.Fori(0, SB) as b:
                        g = b + q * SB
                        pe.wait_ge(s["kv_done"], q + 1)
                        for m in range(KC):
                            project(bank[m], lambda k: wq0[:, k, m * P:(m + 1) * P],
                                    lambda k: sT[:, k, bass.ds(b * BW, BW)]).then_inc(s["q_ps"], 1)
                        pe.wait_ge(s["qT_ready"], g * KC + KC)
                        for p in range(PAIRS):
                            if p >= 4:
                                pe.wait_ge(s["qf_ready"], g * PAIRS + (p - 3))
                            t_.matmul(bank[2 + p % 4], rm[:, (p % 4) * P:(p % 4 + 1) * P], kT[:, p // 4, :],
                                      start=True, stop=True).then_inc(s["qf_ps"], 1)
                        pe.wait_ge(s["qf_ready"], g * PAIRS + PAIRS)
                        for t in range(BLK + 1):
                            if t:
                                pe.wait_ge(s["o_ready"], g * BLK + t)
                            if t < BLK:
                                for p in range(PAIRS):
                                    mm = t_.matmul(bank[6][:, p * 2 * VC:(p + 1) * 2 * VC], qf[:, p, t * P:(t + 1) * P],
                                                   kv[:, p, :], start=True, stop=True)
                                mm.then_inc(s["o_ps"], 1)
                            if t:
                                u = t - 1
                                if u:
                                    pe.wait_ge(s["y_added"], g * BLK + u)
                                turn(bank[7], o0).then_inc(s["oT_ps"], 1)
                                pe.wait_ge(s["oT_ready"], g * BLK + t)
                                project_bias(bank[7][:, D:2 * D], lambda k: oT0[:, k, :], lambda k: wo0[:, k, :],
                                             bo0).then_inc(s["y_ps"], 1)
                    pe.wait_ge(s["y_added"], q * ST + ST)

            def expert_choice(s, g, j, c, k, i):
                cnt = (g * BLK + j) + c * NT
                at = k * CH + i
                if at == 5:
                    pe.wait_ge(s["xn_ready"], cnt + 1)
                    turn(bank[6], xne[:, 0, :]).then_inc(s["xT_ps"], 1)
                if at == 8:
                    pe.wait_ge(s["xT_ready"], cnt + 1)
                    pe.wait_ge(s["oT_ready"], cnt + 1)
                    project(bank[7][:, 0:D], lambda k: xTe[:, k, :], lambda k: wqe[:, k, :]).then_inc(s["q_ps"], 1)
                if at == 19:
                    pe.wait_ge(s["qn_ready"], cnt + 1)
                    turn(bank[6], qc.rearrange("p h d -> p (h d)")).then_inc(s["qnT_ps"], 1)
                if at in (22, 23, CH + 1, CH + 2):
                    m = (22, 23, CH + 1, CH + 2).index(at)
                    if m == 0:
                        pe.wait_ge(s["qnT_ready"], cnt + 1)
                    if m == 2:
                        pe.wait_ge(s["s_ready"], cnt * 4 + 2)
                    t_.matmul(bank[6 + m % 2], qnT[:, m // 2, :], keys[:, (m % 2) * BW:(m % 2 + 1) * BW],
                              start=True, stop=True).then_inc(s["s_ps"], 1)
                if at in (25, CH + 5):
                    pe.wait_ge(s["s_ready"], cnt * 4 + (2 if at == 25 else 4))

            def slots_turn(s, U, first):
                pe.wait_ge(s["split_ready"], U + 1)
                pe.wait_ge(s["laid_out"], 4 * U + 4)
                if not first:
                    pe.wait_ge(s["e_ready"], U * (1 + NG))
                b16 = bank[5].bitcast(BF16)
                for t in range(BLK):
                    t_.transpose(b16[0:NS * FT, t * P:(t + 1) * P], slotd[:, t, :, :].rearrange("p s f -> p (s f)"),
                                 identb)
                for t in range(BLK):
                    mm = t_.transpose(b16[0:NS * HD, BW + t * P:BW + (t + 1) * P],
                                      slotl[:, t, :, :].rearrange("p s f -> p (s f)"), identb)
                mm.then_inc(s["slots_ps"], 1)

            def shifted_scores(s, U, par, m):
                if m == 0:
                    pe.wait_ge(s["slots_ready"], 2 * U + 2)
                if F_BANK[m] in F_BANK[:m]:
                    before = max(x for x in range(m) if F_BANK[x] == F_BANK[m])
                    pe.wait_ge(s["e_ready"], U * (1 + NG) + (before + 1))
                t_.matmul(bank[F_BANK[m]], pairk[:, NE + m * P:NE + (m + 1) * P], dT[par],
                          start=True, stop=True).then_inc(s["e_ps"], 1)

            def chunk_down(s, U, par, i):
                if i == 0:
                    pe.wait_ge(s["slots_ready"], 2 * U + 2)
                pe.wait_ge(s["ge_ready"], U * CH + (i + 1))
                t_.matmul(bank[i % 2], down[:, i * P:(i + 1) * P], lT[par], start=True, stop=True).then_inc(s["l_ps"], 1)
                pe.wait_ge(s["gm_ready"], U * CH + (i + 1))
                t_.matmul(bank[2 + i % 2], pairk[:, i * P:(i + 1) * P], dT[par],
                          start=True, stop=True).then_inc(s["d_ps"], 1)

            def chunk_up(s, U, i):
                pe.wait_ge(s["h_made"], U * CH + (SLOTS + i + 1))
                if i % YG == 0:
                    pe.wait_ge(s["y_weighed"], U * NG + (i // YG + 1))
                q = i % YG * CR * HD
                t_.matmul(bank[4][q:q + CR * HD, :], upw[:, i, :], HH[:, i % RING, :],
                          start=True, stop=True).then_inc(s["up_ps"], 1)

            def fold_group(s, G):
                pe.wait_ge(s["acc_ready"], G + 1)
                for k in range(4):
                    mm = t_.matmul(bank[7][0:4 * HD, :], fold[:, k, :], acc[:, k, :], start=(k == 0), stop=(k == 3))
                mm.then_inc(s["fold_ps"], 1)

            def expert_group(s, b, j, c, choose, first, ends, last):
                G = (b * BLK + j) + c * NT
                for k in range(4):
                    U = G * 4 + k
                    more = not (last and k == 3)
                    pe.wait_ge(s["e_ready"], U * (1 + NG) + EARLY)
                    for i in range(CH):
                        if k == 0 and i == 4 and not first:
                            fold_group(s, G - 1)
                        if i + AHEAD < CH:
                            chunk_down(s, U, k % 2, i + AHEAD)
                        elif more and not (ends and k == 3 and i + AHEAD - CH >= 2):
                            chunk_down(s, U + 1, (k + 1) % 2, i + AHEAD - CH)
                        chunk_up(s, U, i)
                        if choose:
                            expert_choice(s, b + 1, j, c, k, i)
                        if i in (11, 13):
                            for m in (5, 6, 7) if i == 11 else (8,):
                                shifted_scores(s, U, k % 2, m)
                        if i == 18:
                            pe.wait_ge(s["e_ready"], (U + 1) * (1 + NG))
                        if more and i == 23:
                            slots_turn(s, U + 1, False)
                        if more and i == 26:
                            for m in range(3):
                                shifted_scores(s, U + 1, (k + 1) % 2, m)
                        if more and i == 27:
                            for m in range(3, EARLY):
                                shifted_scores(s, U + 1, (k + 1) % 2, m)
                if ends:
                    if not last:
                        pe.wait_ge(s["e_ready"], (U + 1) * (1 + NG) + EARLY)
                    fold_group(s, G)

            def second_pair(s, U):
                for i in range(2, AHEAD):
                    chunk_down(s, U, 0, i)

            def expert_out(s, b, c):
                pe.wait_ge(s["oT_ready"], b * BLK + (c * NT + 2 * BLK + 1))
                for t in range(BLK):
                    n = (b * BLK + t) + c * NT
                    if t:
                        pe.wait_ge(s["y_added"], n)
                    for j in range(BLK):
                        mm = t_.matmul(bank[7][:, (t % 2) * D:(t % 2 + 1) * D], oTe[:, j, t * P:(t + 1) * P],
                                       woute[:, j, :], start=(j == 0), stop=(j == BLK - 1))
                    mm.then_inc(s["y_ps"], 1)
                pe.wait_ge(s["y_added"], b * BLK + (c * NT + BLK))

            def experts(s, c):
                if c == 0:
                    pe.sem_inc(s["ge_ready"], 2)
                    pe.sem_inc(s["gm_ready"], 2)
                    pe.sem_inc(s["y_weighed"], 1)
                    pe.sem_inc(s["oT_ready"], BLK + 1)
                    pe.sem_inc(s["fold_ps"], 1)
                with pe.Fori(0, BLK) as j:
                    for k in range(4):
                        for i in range(CH):
                            expert_choice(s, 0, j, c, k, i)
                pe.wait_ge(s["tables_ready"], c + 1)
                slots_turn(s, c * UNITS, c == 0)
                for m in range(EARLY):
                    shifted_scores(s, c * UNITS, 0, m)
                for i in range(AHEAD):
                    chunk_down(s, c * UNITS, 0, i)
                with pe.Fori(0, NB - 1) as b:
                    expert_group(s, b, 0, c, True, True, False, False)
                    with pe.Fori(1, BLK - 1) as j:
                        expert_group(s, b, j, c, True, False, False, False)
                    expert_group(s, b, BLK - 1, c, True, False, True, False)
                    expert_out(s, b, c)
                    second_pair(s, b * H + (c * UNITS + H))
                expert_group(s, NB - 1, 0, c, False, True, False, False)
                with pe.Fori(1, BLK - 1) as j:
                    expert_group(s, NB - 1, j, c, False, False, False, False)
                expert_group(s, NB - 1, BLK - 1, c, False, False, True, True)
                expert_out(s, NB - 1, c)

            def attention(s):
                with pe.Fori(0, SEQS) as q:
                    with pe.Fori(0, SB) as b:
                        g = b + q * SB
                        cols = bass.ds(b * BW, BW)
                        transpose_block(s, g)
                        pe.wait_ge(s["xT_ready"], g * KC + KC)
                        project(bank[2], lambda k: wkvd[:, k, :], lambda k: sT1[:, k, cols]).then_inc(s["c_ps"], 1)
                        pe.wait_ge(s["c_ready"], g * 2 + 2)
                        t_.matmul(bank[3][0:DR, :], wkr, cb, start=True, stop=True)
                        t_.matmul(bank[4][0:DR, :], wkrs, cb, start=True, stop=True).then_inc(s["r_ps"], 1)
                        project(bank[5][0:DR, :], lambda k: wqr[:, k, :], lambda k: sT1[:, k, cols])
                        project(bank[6][0:DR, :], lambda k: wqrs[:, k, :],
                                lambda k: sT1[:, k, cols]).then_inc(s["r_ps"], 1)
                        for t in range(BLK):
                            mm = t_.matmul(bank[t // 2][:, (t % 2) * D:(t % 2 + 1) * D],
                                           cb[:, t * P:(t + 1) * P], wvup, start=True, stop=True)
                            if t % 2:
                                mm.then_inc(s["v_ps"], 1)
                        pe.wait_ge(s["v_ready"], g * BLK + BLK)
                    with pe.Fori(0, PAIRS) as p:
                        pq = p + q * PAIRS
                        pe.wait_ge(s["rope_copied"], q * (2 * SB) + 2 * SB)
                        pe.wait_ge(s["wpair_ready"], pq * (2 + KC) + (2 + KC))
                        for i in range(8):
                            j = i % 4
                            if i < 4:
                                mm = t_.matmul(bank[i], wpair[:, 0, :], cT[:, j * BW:(j + 1) * BW], start=True, stop=True)
                            else:
                                mm = project(bank[i], lambda k: wpair[:, 1 + k, :],
                                             lambda k: sT1[:, k, j * BW:(j + 1) * BW])
                            mm.then_inc(s["kq_ps"], 1)
                        pe.wait_ge(s["kq_ready"], pq * 16 + 16)
                        for x in range(CN + 4):
                            if x < CN:
                                e, qt, k0, nt = CHUNKS[x]
                                if x >= 2:
                                    pe.wait_ge(s["p_ready"], pq * CN + (x - 1))
                                rows = slice(64 * e, 64 * e + DR + HD)
                                for j in range((nt + BLK - 1) // BLK):
                                    w, at = min(BLK, nt - j * BLK) * P, (k0 + j * BLK) * P
                                    mm = t_.matmul(bank[2 * (x % 2) + j][:, 0:w], QA[rows, qt * P:(qt + 1) * P],
                                                   KA[rows, at:at + w], start=True, stop=True)
                                mm.then_inc(s["s_ps"], 1)
                            if 2 <= x < CN + 2:
                                weights_turn(s, pq, x - 2)
                            if 3 <= x < CN + 3:
                                values(s, pq, x - 3)
                            if x >= 4:
                                pe.wait_ge(s["ocols_ready"], pq * CN + (x - 3))
                                pe.sem_inc(passed_pe, 1)
                                t_.transpose(bank[6 + x % 2][:, P:P + VC], ocols[:, x % 2, :],
                                             ident[0:VC, 0:VC]).then_inc(s["oturn_ps"], 1)
                        pe.wait_ge(s["o_read"], pq * CN + CN)
                    with pe.Fori(0, ST) as t:
                        pe.wait_ge(s["pair_done"], q + 1)
                        pe.wait_ge(s["otile_ready"], q * ST + (t + 1))
                        turn(bank[6], otile).then_inc(s["ot_ps"], 1)
                        pe.wait_ge(s["ot_ready"], q * ST + (t + 1))
                        project(bank[7][:, 0:D], lambda k: oT1[:, k, :], lambda k: wo1[:, k, :]).then_inc(s["y_ps"], 1)
                        pe.wait_ge(s["y_added"], q * ST + (t + 1))

            def weights_turn(s, pq, x):
                pe.wait_ge(s["p_ready"], pq * CN + (x + 1))
                for g in range(GROUPS[x]):
                    if PT_AT[x] + g >= 2:
                        pe.wait_ge(s["pt_ready"], pq * PTN + (PT_AT[x] + g - 1))
                    for i in range(min(BLK, CHUNKS[x][3] - g * BLK)):
                        kt = g * BLK + i
                        mm = t_.transpose(bank[4 + (PT_AT[x] + g) % 2][:, i * P:(i + 1) * P],
                                          probs[:, x % 2, kt * P:(kt + 1) * P], ident[:])
                    mm.then_inc(s["pt_ps"], 1)

            def values(s, pq, x):
                e, qt, k0, nt = CHUNKS[x]
                if x >= 2:
                    pe.wait_ge(s["o_read"], pq * CN + (x - 1))
                pe.wait_ge(s["pt_ready"], pq * PTN + (PT_AT[x] + GROUPS[x]))
                for kt in range(nt):
                    mm = t_.matmul(bank[6 + x % 2][0:VC, 0:P], vpair[:, k0 + kt, e * VC:(e + 1) * VC],
                                   PT[:, x % 2, kt * P:(kt + 1) * P], start=(kt == 0), stop=(kt == nt - 1))
                mm.then_inc(s["o_ps"], 1)

            pe.wait_ge(const_ready, 1)
            for c in range(2):
                pe.wait_ge(gsum_ready, c + 1)
                t_.matmul(bank[0][:, c:c + 1], ones[:], gsum[:, c:c + 1],
                          start=True, stop=True).then_inc(gamma_ready, 1)
            begin(pe, 0)
            pe.wait_ge(const_ready, 2)
            ffn(sf, 0)
            if STAGES > 1:
                begin(pe, 1)
                linear_attention(sk)
            if STAGES > 2:
                begin(pe, 2)
                ffn(sf, 1)
            if STAGES > 3:
                begin(pe, 3)
                experts(se, 0)
            if STAGES > 4:
                begin(pe, 4)
                attention(sa)
            if STAGES > 5:
                begin(pe, 5)
                experts(se, 1)

        @block.gpsimd
        def _(pool):
            ch = Chain(pool, pool_chain)
            g_ = nc.gpsimd

            def build_table(table, src, part, width):
                p1, p2 = [x[0:part.shape[0], 0:width] for x in tpart]
                ch.link(g_.tensor_copy(p1, src))
                ch.link(g_.tensor_tensor(src, src, p1, ALU.subtract))
                ch.link(g_.tensor_copy(p2, src))
                ch.link(g_.tensor_tensor(src, src, p2, ALU.subtract))
                ch.link(g_.tensor_scalar(table, p1, part[:, 0:1], None, ALU.mult))
                for x, k in ((p2, 1), (src, 2)):
                    ch.link(g_.tensor_scalar(x, x, part[:, k:k + 1], None, ALU.mult))
                    ch.link(g_.tensor_tensor(table, table, x, ALU.add))

            def split_step(s, U, step, first):
                f = F[:, :, U % (2 * H), :]
                if step == 0:
                    if not first:
                        pool.wait_ge(s["slots_ps"], U)
                    ch.link(g_.tensor_copy(part1, f))
                if step == 1:
                    ch.link(g_.tensor_tensor(split, f, part1, ALU.subtract))
                    pool.sem_inc(s["rest_ready"], 1)
                if step == 2:
                    ch.mark(g_.tensor_copy(part2, split))
                if step == 3:
                    ch.sync()
                    ch.mark(g_.tensor_tensor(slotd[:, :, 5, :], split[:, :, 0:FT], part2[:, :, 0:FT], ALU.subtract))
                if step == 4:
                    ch.mark(g_.tensor_tensor(slotl[:, :, 5, :], split[:, :, FT:NF], part2[:, :, FT:NF], ALU.subtract))
                    ch.sync()
                    pool.sem_inc(s["split_ready"], 1)

            def expert_group(s, b, j, c, choose, last):
                for k in range(4):
                    U = (b * H + j * 4) + (c * UNITS + k)
                    for i in range(CH):
                        pool.wait_ge(s["ge_ready"], U * CH + (2 + i + 1))
                        pool.wait_ge(s["gm_ready"], U * CH + (2 + i + 1))
                        pool.wait_ge(s["up_ps"], U * CH + (i + 1))
                        g_.tensor_tensor(HH[:, i % RING, :], GE[:, i % SLOTS, :], GM[:, i % SLOTS, :],
                                         ALU.mult).then_inc(s["h_made"], 1)
                        if SPLIT_AT <= i < SPLIT_AT + 5 and not (last and k == 3):
                            if choose and k == 3 and i == SPLIT_AT:
                                pool.wait_ge(s["f_ready"], (b * BLK + j) + (c * NT + BLK + 1))
                            split_step(s, U + 1, i - SPLIT_AT, False)
                ch.restart()

            def experts(s, c):
                if c == 0:
                    pool.sem_inc(s["up_ps"], RING)
                ch.mark(g_.tensor_copy(identb, ident[:]))
                build_table(down, downf, partl, NE)
                build_table(pairk, pairf, partd, NW)
                pool.sem_inc(s["tables_ready"], 1)
                pool.wait_ge(s["f_ready"], c * NT + BLK)
                for step in range(5):
                    split_step(s, c * UNITS, step, c == 0)
                ch.restart()
                with pool.Fori(0, NB - 1) as b:
                    with pool.Fori(0, BLK) as j:
                        expert_group(s, b, j, c, True, False)
                with pool.Fori(0, BLK - 1) as j:
                    expert_group(s, NB - 1, j, c, False, False)
                expert_group(s, NB - 1, BLK - 1, c, False, True)

            if STAGES > 3:
                begin(pool, 3)
                experts(se, 0)
            if STAGES > 5:
                begin(pool, 5)
                experts(se, 1)


def _pad_pairs(w):
    out = np.zeros((w.shape[0], PAIRS, P), w.dtype)
    w = w.reshape(w.shape[0], PAIRS, 2, HD)
    out[:, :, DR:DR + HD] = w[:, :, 0]
    out[:, :, 64 + DR:64 + DR + HD] = w[:, :, 1]
    return out


def _block_diagonal(w, copies):
    out = np.zeros((copies * w.shape[0], copies * w.shape[1]), w.dtype)
    for i in range(copies):
        out[i * w.shape[0]:(i + 1) * w.shape[0], i * w.shape[1]:(i + 1) * w.shape[1]] = w
    return out


def kernel(**inputs):
    import concourse.bacc as bacc
    from concourse.bass_utils import run_bass_kernel_spmd as run

    nc = bacc.Bacc("TRN2", target_bir_lowering=False, num_devices=1)
    i = {k: np.asarray(a) for k, a in inputs.items()}
    f = np.float32
    half = DR // 2
    inv_freq = (f(1.0) / np.power(f(10000.0), np.arange(0, DR, 2, dtype=f) / f(DR))).astype(f)
    freqs = np.outer(np.arange(SL, dtype=f), inv_freq).astype(f)
    cos, sin = np.cos(freqs).T, np.sin(freqs).T
    swap = np.r_[half:DR, 0:half]
    both = np.zeros((HD, 2 * NK), f)
    both[:HD // 2, :NK] = i["L1_ffn_c_keys"].T
    both[HD // 2:, NK:] = i["L1_ffn_c_prime_keys"].T
    down = np.tile(i["L1_ffn_w_down"][:NE].T, (NS, 1))
    c1, c2 = i["L1_ffn_c_keys"].T, i["L1_ffn_c_prime_keys"].T
    pairk = np.zeros((FT, NW), f)
    pairk[0:HD // 2, :NE] = np.repeat(c1, NK, axis=1)
    pairk[HD // 2:HD, :NE + P] = np.tile(c2, (1, NK + CR))
    pairk[0:HD // 2, NE + P:] = np.repeat(c1, HD, axis=1)
    pairk[HD, :NE] = -1
    pairk[HD + 1, NE:NE + P] = -1
    pairk[HD + 2, NE + P:] = -1
    fold = np.zeros((P // HD, HD, 4, 4, HD), f)
    for k in range(4):
        fold[:, :, k, k] = np.eye(HD, dtype=f)
    upw = np.zeros((P, CH, CR, HD), f)
    for r in range(CR):
        upw[r * NK:(r + 1) * NK, :, r] = i["L1_ffn_w_up"][:NE].reshape(CH, CR, NK, HD)[:, r].transpose(1, 0, 2)
    part = np.array(W_PARTS)[:, None] == np.arange(3)[None, :]
    laid = {
        "x": i["L0_attn_x"].reshape(T, D), "ident": np.eye(P, dtype=f),
        "w1t": i["L0_ffn_W1"].T, "b1": i["L0_ffn_b1"].reshape(FC, P).T,
        "w2t": i["L0_ffn_W2"].T, "b2": i["L0_ffn_b2"].reshape(1, D),
        "wq0": i["L0_attn_Wq"], "wk0": i["L0_attn_Wk"], "wv0": i["L0_attn_Wv"], "wo0": i["L0_attn_Wo"],
        "bq0": i["L0_attn_bq"].reshape(KC, P).T, "bk0": i["L0_attn_bk"].reshape(KC, P).T,
        "bv0": i["L0_attn_bv"].reshape(1, D), "bo0": i["L0_attn_bo"].reshape(1, D),
        "rm": _block_diagonal(i["L0_attn_random_matrix"], HK),
        "wqe": i["L1_ffn_Wq"], "woute": i["L1_ffn_Wout"], "keys": _block_diagonal(both, HK),
        "lng": i["L1_ffn_ln_g"], "lnb": i["L1_ffn_ln_b"], "down": down, "pairk": np.tile(pairk, (NS, 1)),
        "upw": upw.reshape(P, CH, CR * HD), "fold": fold.reshape(P, 4, 4 * HD),
        "partl": np.repeat(part, HD, axis=0).astype(f), "partd": np.repeat(part, FT, axis=0).astype(f),
        "wkvd": i["L1_attn_W_kv_down"], "wkup": _pad_pairs(i["L1_attn_W_k_up"]), "wqp": _pad_pairs(i["L1_attn_W_q"]),
        "wvup": i["L1_attn_W_v_up"], "wqr": i["L1_attn_W_q_rope"], "wqrs": i["L1_attn_W_q_rope"][:, swap],
        "wkr": i["L1_attn_W_k_rope"], "wkrs": i["L1_attn_W_k_rope"][:, swap], "wo1": i["L1_attn_W_o"],
        "cos": np.concatenate([cos, cos]), "sin": np.concatenate([-sin, sin]),
        "causal": np.where(np.arange(P)[None, :] > np.arange(P)[:, None], f(LOWEST), f(0)).astype(f),
    }
    arrays, ins = {}, {}
    for name, a in laid.items():
        a = np.ascontiguousarray(a)
        arrays[f"in_{name}"] = a
        ins[name] = nc.dram_tensor(f"in_{name}", a.shape, mybir.dt.from_np(a.dtype), kind="ExternalInput").ap()
    out = nc.dram_tensor("out_x", (T, D), F32, kind="ExternalOutput").ap()
    macaron(nc, ins, out)
    r = run(nc, [arrays], core_ids=[0])
    return r.results[0]["out_x"].reshape(SEQS, SL, D)
```
